# Optimizing a Trainium2 kernel written in Bass

```python
import numpy as np
import jax
import jax.numpy as jnp

def _softmax(x, axis=-1):
    return jax.nn.softmax(x, axis=axis)

def _gelu(x):
    return jax.nn.gelu(x, approximate=True)

def _silu(x):
    return jax.nn.silu(x)

def _sigmoid(x):
    return jax.nn.sigmoid(x)

def _layernorm(x, axis=-1, eps=1e-05):
    m = jnp.mean(x, axis=axis, keepdims=True)
    v = jnp.var(x, axis=axis, keepdims=True)
    return (x - m) / jnp.sqrt(v + eps)

def _scatter_add(tgt, idx, src, axis=0):
    return tgt.at[idx].add(src)

def _segment_sum(src, seg, n):
    return jax.ops.segment_sum(src, seg, n)
kernel_name = 'mk_decoder_preln_d1_seqx_r4_62aa09'

def setup_inputs(seed: int=0):
    np.random.seed(seed)
    _w = jnp.asarray

    def _rec_inputs():
        import jax
        import jax.numpy as jnp
        _rk = jax.random.key(seed)
        x = 0.0003765 + 1 * jax.random.normal(jax.random.fold_in(_rk, 1), (16, 256, 512), jnp.float32)
        _lenS = 256 - jax.random.randint(jax.random.fold_in(_rk, 7), (16,), 0, max(1, 256 // 4) + 1, jnp.int32)
        _lenS2 = 256 - jax.random.randint(jax.random.fold_in(_rk, 8), (16,), 0, max(1, 256 // 4) + 1, jnp.int32)
        _ctx_2048P = jax.random.normal(jax.random.fold_in(_rk, 11), (16, 16, 512), jnp.float32)
        _ctx_2048c = jax.random.dirichlet(jax.random.fold_in(_rk, 511), 0.3 * jnp.ones((16,), jnp.float32), (16, 256))
        _ctx_2048t = jnp.einsum('bsk,bkd->bsd', _ctx_2048c, _ctx_2048P)
        _ctx_2048t = _ctx_2048t * jax.lax.rsqrt(jnp.mean(jnp.square(_ctx_2048t)) + 1e-12) * 0.953939
        ctx_2048 = -0.000292821 + 1.00034 * (_ctx_2048t + 0.3 * jax.random.normal(jax.random.fold_in(_rk, 611), (16, 256, 512), jnp.float32))
        return (x, ctx_2048)
    x, ctx_2048 = _rec_inputs()

    def _L0_attn_setup():
        import jax, jax.numpy as jnp
        import numpy as np
        D_MODEL = 512
        NUM_HEADS = 16
        D_Q = 384
        D_KV = 128
        BS, SL = (2, 512)

        def _lin(x, w, b):
            return jnp.einsum('...i,oi->...o', x, w) + b

        def _freqs(seq_len, dim, theta=10000.0):
            exps = jnp.arange(0, dim, 2, dtype=jnp.float32)
            tn = 1.0 / (theta ** exps / dim)
            m = jnp.arange(seq_len, dtype=jnp.float32)
            ang = jnp.outer(m, tn)
            return (jnp.cos(ang), jnp.sin(ang))

        def _rope(x, cos, sin):
            xe = x[..., 0::2]
            xo = x[..., 1::2]
            re = xe * cos - xo * sin
            im = xe * sin + xo * cos
            return jnp.stack([re, im], axis=-1).reshape(x.shape)

        def _init_linear(key, out_f, in_f):
            k1, k2 = jax.random.split(key)
            bound = 1.0 / np.sqrt(in_f)
            w = jax.random.uniform(k1, (out_f, in_f), jnp.float32, -bound, bound)
            b = jax.random.uniform(k2, (out_f,), jnp.float32, -bound, bound)
            return (w, b)
        key = jax.random.key(seed)
        ks = jax.random.split(key, 9)
        x = jax.random.normal(ks[0], (BS, SL, D_MODEL), jnp.float32)
        w_down_q, b_down_q = _init_linear(ks[1], D_Q, D_MODEL)
        w_up_q, b_up_q = _init_linear(ks[2], D_MODEL, D_Q)
        w_down_kv, b_down_kv = _init_linear(ks[3], D_KV, D_MODEL)
        w_up_k, b_up_k = _init_linear(ks[4], D_MODEL, D_KV)
        w_up_v, b_up_v = _init_linear(ks[5], D_MODEL, D_KV)
        wq_r, bq_r = _init_linear(ks[6], D_MODEL, D_Q)
        wk_r, bk_r = _init_linear(ks[7], D_MODEL, D_KV)
        wo, bo = _init_linear(ks[8], D_MODEL, D_MODEL)
        return dict(x=x, w_down_q=w_down_q, b_down_q=b_down_q, w_up_q=w_up_q, b_up_q=b_up_q, w_down_kv=w_down_kv, b_down_kv=b_down_kv, w_up_k=w_up_k, b_up_k=b_up_k, w_up_v=w_up_v, b_up_v=b_up_v, wq_r=wq_r, bq_r=bq_r, wk_r=wk_r, bk_r=bk_r, wo=wo, bo=bo)
    _L0_attn_all = _L0_attn_setup()
    _L0_attn_in = {k: v for k, v in _L0_attn_all.items() if k in ('w_down_q', 'b_down_q', 'w_up_q', 'b_up_q', 'w_down_kv', 'b_down_kv', 'w_up_k', 'b_up_k', 'w_up_v', 'b_up_v', 'wq_r', 'bq_r', 'wk_r', 'bk_r', 'wo', 'bo')}
    del _L0_attn_all

    def _L0_xattn_setup():
        import jax, jax.numpy as jnp
        import numpy as np
        key = jax.random.key(seed)
        k1, k2, k3, k4, k5 = jax.random.split(key, 5)
        B, D_MODEL, L = (2, 256, 512)
        HEAD_DIM = 8
        H = D_MODEL // HEAD_DIM
        return {'k': jax.random.normal(k1, (B, D_MODEL, L), dtype=jnp.float32), 'v': jax.random.normal(k2, (B, D_MODEL, L), dtype=jnp.float32), 'q': jax.random.normal(k3, (B, D_MODEL, L), dtype=jnp.float32), 'ssm_kernel': jax.random.normal(k4, (H, L), dtype=jnp.float32), 'D': jax.random.normal(k5, (H,), dtype=jnp.float32), 'head_dim': HEAD_DIM}
    _L0_xattn_all = _L0_xattn_setup()
    _L0_xattn_in = {k: v for k, v in _L0_xattn_all.items() if k in ('ssm_kernel', 'D')}
    del _L0_xattn_all

    def _L0_ffn_setup():
        import jax, jax.numpy as jnp
        import numpy as np
        B, T, D, F, E, K = (2, 256, 512, 192, 16, 2)
        key = jax.random.key(seed)
        k0, k1, k2, k3, k4 = jax.random.split(key, 5)
        scale = 0.02
        return {'x': jax.random.normal(k0, (B, T, D), dtype=jnp.float32), 'router_w': jax.random.normal(k1, (D, E), dtype=jnp.float32) * scale, 'gate_w': jax.random.normal(k2, (E, D, F), dtype=jnp.float32) * scale, 'up_w': jax.random.normal(k3, (E, D, F), dtype=jnp.float32) * scale, 'down_w': jax.random.normal(k4, (E, F, D), dtype=jnp.float32) * scale}
    _L0_ffn_all = _L0_ffn_setup()
    _L0_ffn_in = {k: v for k, v in _L0_ffn_all.items() if k in ('router_w', 'gate_w', 'up_w', 'down_w')}
    del _L0_ffn_all
    return {'x': x, 'ctx_2048': ctx_2048, 'L0_attn_w_down_q': _L0_attn_in['w_down_q'], 'L0_attn_b_down_q': _L0_attn_in['b_down_q'], 'L0_attn_w_up_q': _L0_attn_in['w_up_q'], 'L0_attn_b_up_q': _L0_attn_in['b_up_q'], 'L0_attn_w_down_kv': _L0_attn_in['w_down_kv'], 'L0_attn_b_down_kv': _L0_attn_in['b_down_kv'], 'L0_attn_w_up_k': _L0_attn_in['w_up_k'], 'L0_attn_b_up_k': _L0_attn_in['b_up_k'], 'L0_attn_w_up_v': _L0_attn_in['w_up_v'], 'L0_attn_b_up_v': _L0_attn_in['b_up_v'], 'L0_attn_wq_r': _L0_attn_in['wq_r'], 'L0_attn_bq_r': _L0_attn_in['bq_r'], 'L0_attn_wk_r': _L0_attn_in['wk_r'], 'L0_attn_bk_r': _L0_attn_in['bk_r'], 'L0_attn_wo': _L0_attn_in['wo'], 'L0_attn_bo': _L0_attn_in['bo'], 'L0_xattn_ssm_kernel': _L0_xattn_in['ssm_kernel'], 'L0_xattn_D': _L0_xattn_in['D'], 'L0_ffn_router_w': _L0_ffn_in['router_w'], 'L0_ffn_gate_w': _L0_ffn_in['gate_w'], 'L0_ffn_up_w': _L0_ffn_in['up_w'], 'L0_ffn_down_w': _L0_ffn_in['down_w']}

def reference(x, ctx_2048, L0_attn_w_down_q, L0_attn_b_down_q, L0_attn_w_up_q, L0_attn_b_up_q, L0_attn_w_down_kv, L0_attn_b_down_kv, L0_attn_w_up_k, L0_attn_b_up_k, L0_attn_w_up_v, L0_attn_b_up_v, L0_attn_wq_r, L0_attn_bq_r, L0_attn_wk_r, L0_attn_bk_r, L0_attn_wo, L0_attn_bo, L0_xattn_ssm_kernel, L0_xattn_D, L0_ffn_router_w, L0_ffn_gate_w, L0_ffn_up_w, L0_ffn_down_w):
    import jax
    import jax.numpy as jnp

    def _L0_attn_ref(x, w_down_q, b_down_q, w_up_q, b_up_q, w_down_kv, b_down_kv, w_up_k, b_up_k, w_up_v, b_up_v, wq_r, bq_r, wk_r, bk_r, wo, bo):
        import jax, jax.numpy as jnp
        import numpy as np
        D_MODEL = 512
        NUM_HEADS = 16
        D_Q = 384
        D_KV = 128
        BS, SL = (2, 512)

        def _lin(x, w, b):
            return jnp.einsum('...i,oi->...o', x, w) + b

        def _freqs(seq_len, dim, theta=10000.0):
            exps = jnp.arange(0, dim, 2, dtype=jnp.float32)
            tn = 1.0 / (theta ** exps / dim)
            m = jnp.arange(seq_len, dtype=jnp.float32)
            ang = jnp.outer(m, tn)
            return (jnp.cos(ang), jnp.sin(ang))

        def _rope(x, cos, sin):
            xe = x[..., 0::2]
            xo = x[..., 1::2]
            re = xe * cos - xo * sin
            im = xe * sin + xo * cos
            return jnp.stack([re, im], axis=-1).reshape(x.shape)

        def _init_linear(key, out_f, in_f):
            k1, k2 = jax.random.split(key)
            bound = 1.0 / np.sqrt(in_f)
            w = jax.random.uniform(k1, (out_f, in_f), jnp.float32, -bound, bound)
            b = jax.random.uniform(k2, (out_f,), jnp.float32, -bound, bound)
            return (w, b)
        bs, sl, dim = x.shape
        nh, hd = (NUM_HEADS, dim // NUM_HEADS)
        cos, sin = _freqs(sl, dim)
        ct_q = _lin(x, w_down_q, b_down_q)
        q_ct = _lin(ct_q, w_up_q, b_up_q)
        rope_q = _rope(_lin(ct_q, wq_r, bq_r), cos, sin)
        q = (q_ct + rope_q).reshape(bs, sl, nh, hd)
        ct_kv = _lin(x, w_down_kv, b_down_kv)
        k_ct = _lin(ct_kv, w_up_k, b_up_k)
        rope_k = _rope(_lin(ct_kv, wk_r, bk_r), cos, sin)
        k = (k_ct + rope_k).reshape(bs, sl, nh, hd)
        v = _lin(ct_kv, w_up_v, b_up_v).reshape(bs, sl, nh, hd)
        scores = jnp.einsum('bqhd,bkhd->bhqk', q, k) / np.sqrt(hd)
        probs = jax.nn.softmax(scores, axis=-1)
        a = jnp.einsum('bhqk,bkhd->bqhd', probs, v).reshape(bs, sl, nh * hd)
        return _lin(a, wo, bo)

    def _L0_xattn_ref(k, v, q, ssm_kernel, D, head_dim):
        import jax, jax.numpy as jnp
        import numpy as np
        B, HD, L = k.shape
        H = HD // head_dim
        fft_size = 2 * L
        k_ = k.reshape(B, H, head_dim, L)
        v_ = v.reshape(B, H, head_dim, L)
        q_ = q.reshape(B, H, head_dim, L)
        kv = jnp.einsum('bhil,bhjl->bijhl', k_, v_)
        kv_f = jnp.fft.rfft(kv, n=fft_size)
        kernel_f = jnp.fft.rfft(ssm_kernel, n=fft_size)
        y = jnp.fft.irfft(kv_f * kernel_f, n=fft_size)[..., :L]
        out = y + kv * D[None, None, None, :, None]
        out = jnp.einsum('bijhl,bhil->bjhl', out, q_)
        out = jnp.transpose(out, (0, 2, 1, 3)).reshape(B, H * head_dim, L)
        return out.astype(k.dtype)

    def _L0_ffn_ref(x, router_w, gate_w, up_w, down_w):
        import jax, jax.numpy as jnp
        import numpy as np
        B, T, D, F, E, K = (2, 256, 512, 192, 16, 2)
        scores = jnp.einsum('btd,de->bte', x, router_w).astype(jnp.float32)
        probs = jax.nn.softmax(scores, axis=-1)
        routing_weights, routing_idx = jax.lax.top_k(probs, K)
        routing_weights = routing_weights / jnp.sum(routing_weights, axis=-1, keepdims=True)
        routing_weights = routing_weights.astype(x.dtype)
        one_hot = jax.nn.one_hot(routing_idx, E, dtype=x.dtype)
        combine = jnp.einsum('btk,btke->bte', routing_weights, one_hot)
        g = jnp.einsum('btd,edf->ebtf', x, gate_w)
        u = jnp.einsum('btd,edf->ebtf', x, up_w)
        h = jax.nn.silu(g) * u
        expert_out = jnp.einsum('ebtf,efd->ebtd', h, down_w)
        out = jnp.einsum('ebtd,bte->btd', expert_out, combine)
        return out
    x = x + _L0_attn_ref(_layernorm(x, axis=-1), L0_attn_w_down_q, L0_attn_b_down_q, L0_attn_w_up_q, L0_attn_b_up_q, L0_attn_w_down_kv, L0_attn_b_down_kv, L0_attn_w_up_k, L0_attn_b_up_k, L0_attn_w_up_v, L0_attn_b_up_v, L0_attn_wq_r, L0_attn_bq_r, L0_attn_wk_r, L0_attn_bk_r, L0_attn_wo, L0_attn_bo)
    x = x + _L0_xattn_ref(ctx_2048, ctx_2048, _layernorm(x, axis=-1), L0_xattn_ssm_kernel, L0_xattn_D, 8)
    x = x + _L0_ffn_ref(_layernorm(x, axis=-1), L0_ffn_router_w, L0_ffn_gate_w, L0_ffn_up_w, L0_ffn_down_w)
    return x

_drawn_inputs = setup_inputs


def setup_inputs(seed=0):
    import zlib

    import numpy as np

    out = dict(_drawn_inputs(seed))
    spreads = {}
    factors = {'L0_attn_w_down_q': 8.0,
     'L0_attn_b_down_q': 8.0,
     'L0_attn_w_up_q': 8.0,
     'L0_attn_b_up_q': 21.412,
     'L0_attn_b_down_kv': 3.53,
     'L0_attn_w_up_k': 8.0,
     'L0_attn_b_up_k': 64.0,
     'L0_attn_wq_r': 8.0,
     'L0_attn_bq_r': 8.0,
     'L0_attn_wk_r': 8.0,
     'L0_attn_bk_r': 27.063,
     'L0_ffn_router_w': 8.0,
     'L0_ffn_gate_w': 8.0,
     'L0_ffn_up_w': 8.0,
     'L0_ffn_down_w': 8.0}
    for name, (base, spread) in spreads.items():
        noise = np.random.default_rng([zlib.crc32(name.encode()), seed]).standard_normal(out[name].shape)
        drawn = base * np.exp(spread * noise) if base else spread * noise
        out[name] = jnp.asarray(drawn.astype(out[name].dtype))
    for name, factor in factors.items():
        out[name] = (out[name] * factor).astype(out[name].dtype)
    return out
```

```python
from contextlib import ExitStack

import numpy as np

import concourse.bass as bass
from concourse import mybir

F32 = mybir.dt.float32
F16 = mybir.dt.float16
I32 = mybir.dt.int32
U32 = mybir.dt.uint32
ALU = mybir.AluOpType
ACT = mybir.ActivationFunctionType
AX = mybir.AxisListType

P = 128
NB, SL, D = 16, 256, 512
NT = SL // P
KD = D // P
DQ, DKV = 384, 128
NH, HD = 16, 32
KQ = DQ // P
ROT = 10
EPS = 1e-5
SCALE = float(1.0 / np.sqrt(HD))
SWAP = 64
UNITS = 2 * NH // 2
QUAD = 32


def rotary_table():
    exps = np.arange(0, D, 2)
    tn = np.array([np.float32(1.0) / (np.float32(10000.0 ** e) / np.float32(D)) if e < ROT else 0.0 for e in exps], np.float32)
    ang = np.outer(np.arange(SL, dtype=np.float32), tn).astype(np.float32).astype(np.float64)
    tab = np.zeros((P, SL), np.float32)
    for r in range(ROT):
        a = ang[:, r // 2]
        tab[r] = np.cos(a) - 1.0
        tab[SWAP + r] = np.sin(a) if r % 2 else -np.sin(a)
    return tab


def setup_program(nc, w, sbw, psum, tab, sel, ident):
    ctx = ExitStack()
    with ctx:
        def sb(name, shape, dt=F32):
            return ctx.enter_context(nc.sbuf_tensor(name, shape, dt))

        def sem(name):
            return ctx.enter_context(nc.semaphore(name))

        upq, rq = sb("upq", [P, KD, DQ]), sb("rq", [P, KD, DQ])
        upk, rk = sb("upk", [P, KD, DKV]), sb("rk", [P, KD, DKV])
        upv, wo = sb("upv", [P, KD, DKV]), sb("wo_nat", [P, KD, D])
        dq, dkv = sb("dq", [P, KQ, D]), sb("dkv", [P, D])
        xq, xk = sb("xq", [P, DQ]), sb("xk", [P, DKV])
        sqT, xqT = sb("sqT", [P, KQ, D]), sb("xqT", [P, KQ, P])
        b_up, b_r, b_dq = sb("b_up", [P, 2, KD]), sb("b_r", [P, 2, KD]), sb("b_dq", [P, KQ])
        b_x, b_v, bv_rep = sb("b_x", [P, 2]), sb("b_v", [P, KD]), sb("bv_rep", [P, KD, P])

        zeroed, ident_at = sem("zeroed"), sem("ident_at")
        loaded, summed = sem("loaded"), sem("summed")
        turned, kept = sem("turned"), sem("kept")
        tables, rot_in = sem("tables"), sem("rot_in")

        blk = "(o p) i -> p o i"
        block = ctx.enter_context(nc.Block())
        groups = []
        for c in range(KQ):
            groups.append(("T", [upq[:, o, c * P:(c + 1) * P] for o in range(KD)], sqT[:, c, :], 1.0))
        groups.append(("T", [xq[:, c * P:(c + 1) * P] for c in range(KQ)], xqT[:, :, :].rearrange("p c n -> p (c n)"), 1.0))
        groups.append(("T", [dkv[:, k * P:(k + 1) * P] for k in range(KD)], sbw["dkvT"][:, :, :].rearrange("p c n -> p (c n)"), 1.0))
        groups.append(("T", [upk[:, o, :] for o in range(KD)], sbw["kT_w"][:, :], 1.0))
        groups.append(("T", [upv[:, o, :] for o in range(KD)], sbw["vT_w"][:, :], 1.0))
        groups.append(("T", [xk[:, :]], sbw["xkT"][:, :], 1.0))
        for k in range(KD):
            groups.append(("T", [wo[:, o, k * P:(k + 1) * P] for o in range(KD)], sbw["woT"][:, k, :], 1.0))
        for i in range(KD):
            groups.append(("fold", i, sbw["qT_w"][:, i, :], SCALE))
        groups.append(("fold_rot", None, sbw["xqT_f"][:, :, :].rearrange("p c n -> p (c n)"), SCALE))
        groups.append(("bias_q", None, None, None))
        groups.append(("bias_o", None, None, None))
        G = len(groups)
        loads = 0

        @block.sync
        def _(sp):
            nonlocal loads
            sp.dma_start(tab[:], w["tab"]).then_inc(tables, 16)
            sp.dma_start(sel[:], w["sel"]).then_inc(tables, 16)
            for dst, src in ((upq[:], w["w_up_q"].rearrange(blk, p=P)), (rq[:], w["wq_r"].rearrange(blk, p=P)),
                             (upk[:], w["w_up_k"].rearrange(blk, p=P)), (rk[:], w["wk_r"].rearrange(blk, p=P)),
                             (upv[:], w["w_up_v"].rearrange(blk, p=P)), (wo[:], w["wo"].rearrange(blk, p=P)),
                             (dq[:], w["w_down_q"].rearrange("(c p) i -> p c i", p=P)), (dkv[:], w["w_down_kv"])):
                sp.dma_start(dst, src).then_inc(loaded, 16)
                loads += 1
            for dst, src in ((b_up[:, 0, :], "b_up_q"), (b_up[:, 1, :], "b_up_k"), (b_r[:, 0, :], "bq_r"),
                             (b_r[:, 1, :], "bk_r"), (b_dq[:], "b_down_q"), (b_v[:], "b_up_v")):
                with nc.allow_non_contiguous_dma(reason="a bias, once"):
                    sp.dma_start(dst, w[src].rearrange("(o p) -> p o", p=P)).then_inc(loaded, 16)
                loads += 1
            sp.dma_start(sbw["b_dkv"][:], w["b_down_kv"].rearrange("(p o) -> p o", o=1)).then_inc(loaded, 16)
            sp.dma_start(sbw["b_o"][:], bass.AP(w["bo"].tensor, 0, [[0, P], [1, D]])).then_inc(loaded, 16)
            loads += 2
            sp.wait_ge(zeroed, 3)
            for dst, src, n in ((xq, w["wq_r"], DQ), (xk, w["wk_r"], DKV)):
                sp.dma_start(dst[0:ROT, :], src[0:ROT, :]).then_inc(rot_in, 16)
                for odd in range(2):
                    sp.dma_start(dst[SWAP + odd:SWAP + ROT:2, :], src[1 - odd:ROT:2, :]).then_inc(rot_in, 16)
            for col, name in enumerate(("bq_r", "bk_r")):
                v = w[name].rearrange("(p o) -> p o", o=1)
                sp.dma_start(b_x[0:ROT, col:col + 1], v[0:ROT, :]).then_inc(rot_in, 16)
                for odd in range(2):
                    with nc.allow_non_contiguous_dma(reason="a bias, once"):
                        sp.dma_start(b_x[SWAP + odd:SWAP + ROT:2, col:col + 1], v[1 - odd:ROT:2, :]).then_inc(rot_in, 16)

        ROT_LOADS = 12

        @block.gpsimd
        def _(pool):
            pool.memset(ident[:], 0.0).then_inc(ident_at, 1)
            pool.wait_ge(ident_at, 1)
            pool.affine_select(out=ident[:], in_=ident[:], compare_op=ALU.not_equal, fill=1.0, base=0,
                               pattern=[[-1, P]], channel_multiplier=1).then_inc(ident_at, 1)

        @block.vector
        def _(dve):
            dve.memset(xq[:], 0.0).then_inc(zeroed, 1)
            dve.memset(xk[:], 0.0).then_inc(zeroed, 1)
            dve.memset(b_x[:], 0.0).then_inc(zeroed, 1)
            dve.wait_ge(loaded, 16 * loads)
            dve.wait_ge(rot_in, 16 * ROT_LOADS)
            dve.tensor_tensor(upq[:], upq[:], rq[:], ALU.add).then_inc(summed, 1)
            dve.tensor_tensor(upk[:], upk[:], rk[:], ALU.add).then_inc(summed, 1)
            dve.tensor_tensor(b_up[:], b_up[:], b_r[:], ALU.add).then_inc(summed, 1)
            dve.memset(bv_rep[:], 1.0).then_inc(summed, 1)
            dve.wait_ge(summed, 4)
            for k in range(KD):
                dve.tensor_scalar(bv_rep[:, k, :], bv_rep[:, k, :], b_v[:, k:k + 1], None, ALU.mult).then_inc(summed, 1)
            for g, (kind, arg, dst, scale) in enumerate(groups):
                bank = psum[g % 8]
                dve.wait_ge(turned, g + 1)
                if kind == "bias_q":
                    dve.scalar_tensor_tensor(sbw["b_q"][:], bank[:, 0:KD], 1.0, b_up[:, 0, :], ALU.mult, ALU.add).then_inc(kept, 1)
                    dve.scalar_tensor_tensor(sbw["b_xq"][:], bank[:, KD:KD + 1], 1.0, b_x[:, 0:1], ALU.mult, ALU.add).then_inc(summed, 1)
                    dve.wait_ge(kept, g + 1)
                    dve.wait_ge(summed, 5 + KD)
                    dve.tensor_scalar(sbw["b_q"][:], sbw["b_q"][:], SCALE, None, ALU.mult).then_inc(summed, 1)
                    dve.tensor_scalar(sbw["b_xq"][:], sbw["b_xq"][:], SCALE, None, ALU.mult).then_inc(summed, 1)
                    dve.tensor_copy(sbw["b_k"][:], b_up[:, 1, :]).then_inc(summed, 1)
                    dve.tensor_copy(sbw["b_xk"][:], b_x[:, 1:2]).then_inc(summed, 1)
                elif kind == "bias_o":
                    dve.tensor_tensor(sbw["b_o"][:], bank[:, :], sbw["b_o"][:], ALU.add).then_inc(kept, 1)
                else:
                    n = P * len(arg) if kind == "T" else D
                    dve.tensor_scalar(dst, bank[:, 0:n], scale, None, ALU.mult).then_inc(kept, 1)

        @block.tensor
        def _(pe):
            pe.wait_ge(ident_at, 2)
            pe.wait_ge(summed, 4 + KD)
            for g, (kind, arg, dst, scale) in enumerate(groups):
                bank = psum[g % 8]
                if g >= 8:
                    pe.wait_ge(kept, g - 7)
                if kind == "T":
                    for j, src in enumerate(arg):
                        mm = pe.transpose(bank[:, j * P:(j + 1) * P], src, ident[:])
                elif kind == "fold":
                    pe.wait_ge(kept, KQ)
                    for c in range(KQ):
                        mm = pe.matmul(bank[:, :], dq[:, c, arg * P:(arg + 1) * P], sqT[:, c, :],
                                       start=(c == 0), stop=(c == KQ - 1))
                elif kind == "fold_rot":
                    for i in range(KD):
                        for c in range(KQ):
                            mm = pe.matmul(bank[:, i * P:(i + 1) * P], dq[:, c, i * P:(i + 1) * P], xqT[:, c, :],
                                           start=(c == 0), stop=(c == KQ - 1))
                elif kind == "bias_q":
                    for o in range(KD + 1):
                        for c in range(KQ):
                            lhs = sqT[:, c, o * P:(o + 1) * P] if o < KD else xqT[:, c, :]
                            mm = pe.matmul(bank[:, o:o + 1], lhs, b_dq[:, c:c + 1], start=(c == 0), stop=(c == KQ - 1))
                else:
                    pe.wait_ge(kept, KQ + 5 + KD)
                    for k in range(KD):
                        mm = pe.matmul(bank[:, :], bv_rep[:, k, :], sbw["woT"][:, k, :], start=(k == 0), stop=(k == KD - 1))
                mm.then_inc(turned, 1)

        @block.scalar
        def _(act):
            act.wait_ge(tables, 32)


def attention_program(nc, x, x1, sbw, psum, tab, sel, ident):
    ctx = ExitStack()
    with ctx:
        def sb(name, shape, dt=F32):
            return ctx.enter_context(nc.sbuf_tensor(name, shape, dt))

        def sem(name):
            return ctx.enter_context(nc.semaphore(name))

        X = [sb(f"X{s}", [P, NT, D]) for s in range(2)]
        XB = [sb(f"XB{s}", [P, NT, D]) for s in range(2)]
        XN = sb("XN", [P, NT, D])
        stats, mv, vare, rstd = sb("stats", [P, 6]), sb("mv", [P, 2]), sb("vare", [P, 1]), sb("rstd", [P, 1])
        XT = sb("XT", [P, KD, SL])
        CK = sb("CK", [P, SL])
        RQ, RK = sb("RQ", [P, SL]), sb("RK", [P, SL])
        QH, QL = sb("QH", [P, KD, SL], F16), sb("QL", [P, KD, SL], F16)
        KH, KL = sb("KH", [P, KD, SL], F16), sb("KL", [P, KD, SL], F16)
        QS = [sb(f"QS{s}", [P, 4, KD, SL], F16) for s in range(2)]
        KS = [sb(f"KS{s}", [P, 4, KD, SL], F16) for s in range(2)]
        V = [sb(f"V{s}", [P, NT, D]) for s in range(2)]
        PR = [sb(f"PR{i}", [P, 2, SL]) for i in range(4)]
        PT = [sb(f"PT{i}", [P, 4, P]) for i in range(2)]
        AT = [sb(f"AT{s}", [P, KD, SL]) for s in range(2)]
        X1 = [sb(f"X1_{s}", [P, NT, D]) for s in range(2)]
        nmax = sb("nmax", [P, 4, 2])
        den, rden = sb("den", [P, 4, 2]), sb("rden", [P, 4, 2])

        bT, bAV, bA, bB = psum[0], psum[1], psum[2], psum[3]
        bS, bP = psum[4:6], psum[6:8]

        x_in = [sem(f"x_in{s}") for s in range(2)]
        xn_done, chain = sem("xn_done"), sem("chain")
        rstd_done, half_set = sem("rstd_done"), sem("half_set")
        may_aggr = sem("may_aggr")
        turned, xt_done = sem("xT_turned"), sem("xt_done")
        front, ctr_done, rk_done = sem("front"), sem("ctr_done"), sem("rk_done")
        q_hi, q_lo, k_hi, k_lo, v_done = sem("q_hi"), sem("q_lo"), sem("k_hi"), sem("k_lo"), sem("v_done")
        qs_in = [sem(f"qs_in{s}") for s in range(2)]
        ks_in = [sem(f"ks_in{s}") for s in range(2)]
        s_done, max_done, exp_done, rd_done, pn_done = (sem(n) for n in ("s_done", "max_done", "exp_done", "rd_done", "pn_done"))
        t_done, pte_v, pte_a, pv_done, at_done = (sem(n) for n in ("t_done", "pte_v", "pte_a", "pv_done", "at_done"))
        out_done, xb_done, x1_done = sem("out_done"), sem("xb_done"), sem("x1_done")
        x1_out = [sem(f"x1_out{s}") for s in range(2)]

        BANK = [bT, bA, bA, bB, bA, bB, bT, bB, bA, bT]
        PE_STEP = {0: [(2, 0)], 1: [(2, 1)], 2: [(3, 0)], 3: [(3, 1)], 4: [(4, 0)], 5: [(4, 1)],
                   6: [(5, None), (6, None)], 8: [(7, None)], 9: [(8, None)], 10: [(9, None)]}
        ACT_STEP = {4: 3, 7: 4, 8: 6, 9: 7, 10: 8, 11: 9}
        DVE_STEP = {2: 2, 5: 3, 7: 5, 8: 4, 9: 6, 10: 7}

        def unit(u):
            return (u // 2) % 2, 2 * (2 * (u // 4) + u % 2), u // 4

        def over_sequences(eng, body):
            body(0, 0, True, False)
            body(1, 1, False, False)
            with eng.Fori(2, NB - 2, 2) as b:
                body(b, 0, False, False)
                body(b + 1, 1, False, False)
            body(NB - 2, 0, False, False)
            body(NB - 1, 1, False, True)

        def before_last(b):
            return isinstance(b, int) and b + 2 >= NB

        block = ctx.enter_context(nc.Block())

        @block.sync
        def _(sp):
            def load(b, s):
                sp.dma_start(X[s][:], x[b].rearrange("(t p) d -> p t d", p=P)).then_inc(x_in[s], 16)

            def stack(b, s):
                if not isinstance(b, int) or b >= 2:
                    sp.wait_ge(s_done, UNITS * (b - 1))
                for hi, lo, dst, parts, ready, into in ((QH, QL, QS[s], "hhl", q_lo, qs_in[s]), (KH, KL, KS[s], "hlh", k_lo, ks_in[s])):
                    sp.wait_ge(ready, 2 * b + 2)
                    for part, which in enumerate(parts):
                        src = hi if which == "h" else lo
                        for hq in range(4):
                            sp.dma_start(dst[QUAD * part:QUAD * (part + 1), hq, :, :],
                                         src[QUAD * hq:QUAD * (hq + 1), :, :]).then_inc(into, 16)

            def store(b, s):
                for t in range(NT):
                    sp.wait_ge(x1_done, 2 * b + t + 1)
                    sp.dma_start(x1[b][t * P:(t + 1) * P, :], X1[s][:, t, :]).then_inc(x1_out[s], 16)

            def refill(b, s):
                sp.wait_ge(xn_done, 2 * b - 2)
                sp.wait_ge(xb_done, 2 * b - 2)
                load(b, s)

            load(0, 0)
            load(1, 1)
            stack(0, 0)
            refill(2, 0)

            def body(b, s, first, last, more=True):
                if not last:
                    stack(b + 1, 1 - s)
                if not first:
                    store(b - 1, 1 - s)
                if more:
                    refill(b + 3, 1 - s)

            body(0, 0, True, False)
            body(1, 1, False, False)
            with sp.Fori(2, NB - 4, 2) as b:
                body(b, 0, False, False)
                body(b + 1, 1, False, False)
            body(NB - 4, 0, False, False)
            body(NB - 3, 1, False, False, False)
            body(NB - 2, 0, False, False, False)
            body(NB - 1, 1, False, True, False)
            store(NB - 1, 1)
            sp.wait_ge(x1_out[0], 16 * NB)
            sp.wait_ge(x1_out[1], 16 * NB)

        @block.gpsimd
        def _(pool):
            def norm(b, u):
                pool.wait_ge(rd_done, UNITS * b + u + 1)
                scale = rden[:, u % 4, :].rearrange("p (j o) -> p j o", o=1).to_broadcast([P, 2, SL])
                pool.tensor_tensor(PR[u % 4][:, :, :], PR[u % 4][:, :, :], scale, ALU.mult).then_inc(pn_done, 1)

            def residual(b, s, t):
                if t == 0:
                    pool.wait_ge(x_in[s], 8 * (b + 2 - s))
                if not isinstance(b, int) or b >= 2:
                    pool.wait_ge(x1_done, 2 * b - 3 + t)
                pool.tensor_tensor(XB[s][:, t, :], X[s][:, t, :], sbw["b_o"][:], ALU.add).then_inc(xb_done, 1)

            def root(b, t):
                pool.wait_ge(chain, 3 * (2 * b + t + 1))
                pool.tensor_tensor(rstd[:], vare[:], sbw["m_half"][:], ALU.pow).then_inc(rstd_done, 1)

            pool.memset(sbw["m_half"][:], -0.5).then_inc(half_set, 1)
            pool.wait_ge(half_set, 1)
            for b in range(2):
                for t in range(NT):
                    root(b, t)
            residual(0, 0, 0)
            residual(0, 0, 1)

            def body(b, s, first, last):
                for u in range(UNITS):
                    if u >= 1:
                        norm(b, u - 1)
                    elif not first:
                        norm(b - 1, UNITS - 1)
                    if u in (4, 12) and not before_last(b):
                        root(b + 2, u // 8)
                    if u in (14, 15) and not last:
                        residual(b + 1, 1 - s, u - 14)

            over_sequences(pool, body)
            norm(NB - 1, UNITS - 1)

        @block.scalar
        def _(act):
            def piece(b, s, k):
                if k < 2:
                    act.wait_ge(turned, 2 * b + k + 1)
                    if k == 0 and (not isinstance(b, int) or b >= 1):
                        act.wait_ge(front, 8 * b)
                    bank = bT if k == 0 else bA
                    act.copy(XT[:, :, k * P:(k + 1) * P], bank[:, :].rearrange("p (k n) -> p k n", k=KD)).then_inc(xt_done, 1)
                elif k in (3, 4, 6, 7):
                    dst, bias, hi, into = (QH, "b_q", q_hi, qs_in) if k < 5 else (KH, "b_k", k_hi, ks_in)
                    m0 = 2 if k in (3, 6) else 0
                    act.wait_ge(front, 8 * b + k - 1)
                    if m0 and (not isinstance(b, int) or b >= 1):
                        act.wait_ge(into[1 - s], 96 * (b + s))
                    for j in range(2):
                        ins = act.activation(dst[:, m0 + j, :], BANK[k][:, j * SL:(j + 1) * SL], ACT.Identity,
                                             bias=sbw[bias][:, m0 + j:m0 + j + 1])
                    ins.then_inc(hi, 1)
                elif k in (8, 9):
                    act.wait_ge(front, 8 * b + k - 1)
                    if k == 8 and (not isinstance(b, int) or b >= 2):
                        act.wait_ge(pv_done, UNITS * (b - 1))
                    act.copy(V[s][:, k - 8, :], BANK[k][:, :]).then_inc(v_done, 1)

            def exps(b, u):
                act.wait_ge(max_done, UNITS * b + u + 1)
                if not isinstance(b, int) or UNITS * b + u >= 4:
                    act.wait_ge(t_done, UNITS * b + u - 3)
                for j in range(2):
                    ins = act.activation(PR[u % 4][:, j, :], bS[u % 2][:, j * SL:(j + 1) * SL], ACT.Exp,
                                         bias=nmax[:, u % 4, j:j + 1], accum_out=den[:, u % 4, j:j + 1])
                ins.then_inc(exp_done, 1)

            def keep_pt(b, u):
                act.wait_ge(t_done, UNITS * b + u + 1)
                if not isinstance(b, int) or UNITS * b + u >= 2:
                    act.wait_ge(pv_done, UNITS * b + u - 1)
                act.copy(PT[1][:, :, :].rearrange("p k n -> p (k n)"), bP[1][:, :]).then_inc(pte_a, 1)

            for k in range(10):
                piece(0, 0, k)
            for k in range(2):
                piece(1, 1, k)

            def body(b, s, first, last):
                for u in range(UNITS):
                    exps(b, u)
                    if u % 2 == 0:
                        if u >= 4:
                            keep_pt(b, u - 3)
                        elif not first:
                            keep_pt(b - 1, UNITS + u - 3)
                    if u in ACT_STEP and not last:
                        piece(b + 1, 1 - s, ACT_STEP[u])
                    if u == UNITS - 1 and not before_last(b):
                        piece(b + 2, s, 0)
                        piece(b + 2, s, 1)

            over_sequences(act, body)
            keep_pt(NB - 1, UNITS - 3)
            keep_pt(NB - 1, UNITS - 1)

        @block.vector
        def _(dve):
            def statistics(b, s, t):
                if t == 0:
                    dve.wait_ge(x_in[s], 8 * (b + 2 - s))
                base = 3 * (2 * b + t)
                dve.bn_stats(stats[:], X[s][:, t, :]).then_inc(chain, 1)
                dve.wait_ge(chain, base + 1)
                dve.sem_inc(may_aggr, 1)
                dve.bn_aggr(mv[:], stats[:]).then_inc(chain, 1)
                dve.wait_ge(chain, base + 2)
                dve.tensor_scalar(vare[:], mv[:, 1:2], EPS, None, ALU.add).then_inc(chain, 1)

            def normalise(b, s, t):
                dve.wait_ge(rstd_done, 2 * b + t + 1)
                if not isinstance(b, int) or b >= 1:
                    dve.wait_ge(turned, 2 * b - 1 + t)
                dve.tensor_scalar(XN[:, t, :], X[s][:, t, :], mv[:, 0:1], rstd[:, 0:1], ALU.subtract, ALU.mult).then_inc(xn_done, 1)

            def piece(b, s, k):
                dve.wait_ge(front, 8 * b + k - 1)
                if k == 2:
                    dve.tensor_scalar(CK[:], bA[:, 0:SL], sbw["b_dkv"][:, 0:1], None, ALU.add)
                    dve.scalar_tensor_tensor(RQ[:], bA[:, SL:2 * SL], sbw["b_xq"][:, 0:1], tab[:], ALU.add, ALU.mult).then_inc(ctr_done, 1)
                elif k == 5:
                    dve.scalar_tensor_tensor(RK[:], bB[:, 0:SL], sbw["b_xk"][:, 0:1], tab[:], ALU.add, ALU.mult).then_inc(rk_done, 1)
                else:
                    hi, lo, bias, hi_done, lo_done, into = (QH, QL, "b_q", q_hi, q_lo, qs_in) if k < 5 else (KH, KL, "b_k", k_hi, k_lo, ks_in)
                    m0 = 2 if k in (3, 6) else 0
                    dve.wait_ge(hi_done, 2 * b + (1 if m0 else 2))
                    if m0 and (not isinstance(b, int) or b >= 1):
                        dve.wait_ge(into[1 - s], 96 * (b + s))
                    bank = BANK[k]
                    for j in range(2):
                        ins = dve.scalar_tensor_tensor(lo[:, m0 + j, :], bank[:, j * SL:(j + 1) * SL],
                                                       sbw[bias][:, m0 + j:m0 + j + 1], hi[:, m0 + j, :], ALU.add, ALU.subtract)
                    ins.then_inc(lo_done, 1)

            def maxima(b, u):
                dve.wait_ge(s_done, UNITS * b + u + 1)
                dve.tensor_reduce(nmax[:, u % 4, :], bS[u % 2][:, :].rearrange("p (j n) -> p j n", j=2), AX.X, ALU.max,
                                  negate=True).then_inc(max_done, 1)

            def recip(b, u):
                dve.wait_ge(exp_done, UNITS * b + u + 1)
                dve.reciprocal(rden[:, u % 4, :], den[:, u % 4, :]).then_inc(rd_done, 1)

            def keep_pt(b, u):
                dve.wait_ge(t_done, UNITS * b + u + 1)
                if not isinstance(b, int) or UNITS * b + u >= 2:
                    dve.wait_ge(pv_done, UNITS * b + u - 1)
                dve.tensor_copy(PT[0][:, :, :].rearrange("p k n -> p (k n)"), bP[0][:, :]).then_inc(pte_v, 1)

            def keep_at(b, s, m):
                dve.wait_ge(pv_done, UNITS * b + 4 * m + 4)
                if m == 0 and (not isinstance(b, int) or b >= 2):
                    dve.wait_ge(out_done, 2 * b - 2)
                dve.tensor_copy(AT[s][:, m, :], bAV[:, 0:SL]).then_inc(at_done, 1)

            def add_residual(b, s, t):
                dve.wait_ge(out_done, 2 * b + t + 1)
                if t == 0:
                    dve.wait_ge(xb_done, 2 * b + 2)
                    if not isinstance(b, int) or b >= 2:
                        dve.wait_ge(x1_out[s], 16 * (b - s))
                dve.tensor_tensor(X1[s][:, t, :], (bA if t == 0 else bB)[:, :], XB[s][:, t, :], ALU.add).then_inc(x1_done, 1)

            for b in range(2):
                for t in range(NT):
                    statistics(b, b, t)
                    normalise(b, b, t)
            for k in range(2, 8):
                piece(0, 0, k)

            def body(b, s, first, last):
                for u in range(UNITS):
                    maxima(b, u)
                    if u >= 1:
                        recip(b, u - 1)
                    elif not first:
                        recip(b - 1, UNITS - 1)
                    if u % 2:
                        if u >= 3:
                            keep_pt(b, u - 3)
                        elif not first:
                            keep_pt(b - 1, UNITS - 2)
                    if u % 4 == 3:
                        if u >= 4:
                            keep_at(b, s, u // 4 - 1)
                        elif not first:
                            keep_at(b - 1, 1 - s, KD - 1)
                    if u in (13, 15) and not first:
                        add_residual(b - 1, 1 - s, (u - 13) // 2)
                    if not before_last(b):
                        if u in (4, 12):
                            statistics(b + 2, s, u // 8)
                        if u in (6, 14):
                            normalise(b + 2, s, u // 8)
                    if u in DVE_STEP and not last:
                        piece(b + 1, 1 - s, DVE_STEP[u])

            over_sequences(dve, body)
            recip(NB - 1, UNITS - 1)
            keep_pt(NB - 1, UNITS - 2)
            keep_at(NB - 1, 1, KD - 1)
            for t in range(NT):
                add_residual(NB - 1, 1, t)

        @block.tensor
        def _(pe):
            def piece(b, s, k, part=None):
                bank = BANK[k]
                if k < 2:
                    pe.wait_ge(xn_done, 2 * b + k + 1)
                    if k == 1 and (not isinstance(b, int) or b >= 3):
                        pe.wait_ge(x1_done, 2 * b - 5)
                    elif not isinstance(b, int) or b >= 1:
                        pe.wait_ge(v_done, 2 * b - k)
                    for j in range(KD):
                        mm = pe.transpose(bank[:, j * P:(j + 1) * P], XN[:, k, j * P:(j + 1) * P], ident[:])
                    mm.then_inc(turned, 1)
                    return

                def product(dst, weights, rot=None):
                    for j in range(KD):
                        mm = pe.matmul(dst, weights(j), XT[:, j, :], start=(j == 0), stop=(j == KD - 1 and rot is None))
                    if rot is not None:
                        mm = pe.matmul(dst, sel[:], rot[:], start=False, stop=True)
                    return mm

                def key_block(dst, m, rot=None):
                    mm = pe.matmul(dst, sbw["kT_w"][:, m * P:(m + 1) * P], CK[:], start=True, stop=rot is None)
                    if rot is not None:
                        mm = pe.matmul(dst, sel[:], rot[:], start=False, stop=True)
                    return mm

                if k == 2:
                    if part != 1:
                        pe.wait_ge(xt_done, 2 * b + 2)
                        mm = product(bank[:, 0:SL], lambda j: sbw["dkvT"][:, j, :])
                    if part != 0:
                        mm = product(bank[:, SL:2 * SL], lambda j: sbw["xqT_f"][:, j, :])
                elif k in (3, 4):
                    if part != 1:
                        if k == 4:
                            pe.wait_ge(ctr_done, b + 1)
                        elif not isinstance(b, int) or b >= 3:
                            pe.wait_ge(x1_done, 2 * b - 4)
                        elif b >= 1:
                            pe.wait_ge(k_lo, 2 * b)
                    m0 = 2 if k == 3 else 0
                    for m in range(m0, m0 + 2):
                        if part is None or part == m - m0:
                            mm = product(bank[:, (m - m0) * SL:(m - m0 + 1) * SL],
                                         lambda j: sbw["qT_w"][:, j, m * P:(m + 1) * P], RQ if m == 0 else None)
                elif k == 5:
                    pe.wait_ge(q_lo, 2 * b + 1)
                    mm = pe.matmul(bank[:, 0:SL], sbw["xkT"][:], CK[:], start=True, stop=True)
                elif k == 6:
                    for m in (2, 3):
                        mm = key_block(bank[:, (m - 2) * SL:(m - 1) * SL], m)
                elif k == 7:
                    pe.wait_ge(rk_done, b + 1)
                    for m in (0, 1):
                        mm = key_block(bank[:, m * SL:(m + 1) * SL], m, RK if m == 0 else None)
                else:
                    if k == 8:
                        pe.wait_ge(q_lo, 2 * b + 2)
                    else:
                        pe.wait_ge(k_lo, 2 * b + 1)
                    mm = pe.matmul(bank[:, :], CK[:, (k - 8) * P:(k - 7) * P], sbw["vT_w"][:], start=True, stop=True)
                if part != 0:
                    mm.then_inc(front, 1)

            def scores(b, s, u):
                if u == 0:
                    for sems in (qs_in, ks_in):
                        pe.wait_ge(sems[s], 96 * (b + 2 - s))
                if not isinstance(b, int) or UNITS * b + u >= 2:
                    pe.wait_ge(exp_done, UNITS * b + u - 1)
                t, h, m = unit(u)
                for j in range(2):
                    hq = (h + j) % 4
                    mm = pe.matmul(bS[u % 2][:, j * SL:(j + 1) * SL], QS[s][0:3 * QUAD, hq, m, t * P:(t + 1) * P],
                                   KS[s][0:3 * QUAD, hq, m, :], start=True, stop=True)
                mm.then_inc(s_done, 1)

            def turn(b, u):
                pe.wait_ge(pn_done, UNITS * b + u + 1)
                if not isinstance(b, int) or UNITS * b + u >= 2:
                    pe.wait_ge(pte_a if u % 2 else pte_v, (UNITS // 2) * b + u // 2)
                for j in range(2):
                    for kb in range(NT):
                        mm = pe.transpose(bP[u % 2][:, (2 * j + kb) * P:(2 * j + kb + 1) * P],
                                          PR[u % 4][:, j, kb * P:(kb + 1) * P], ident[:])
                mm.then_inc(t_done, 1)

            def values(b, s, u):
                pe.wait_ge(pte_a if u % 2 else pte_v, (UNITS // 2) * b + u // 2 + 1)
                t, h, m = unit(u)
                if u == 0:
                    pe.wait_ge(v_done, 2 * b + 2)
                if u % 4 == 0 and (not isinstance(b, int) or b >= 1 or m >= 1):
                    pe.wait_ge(at_done, KD * b + m)
                for j in range(2):
                    hq = (h + j) % 4
                    for kb in range(NT):
                        mm = pe.matmul(bAV[QUAD * hq:QUAD * (hq + 1), t * P:(t + 1) * P],
                                       V[s][:, kb, (h + j) * HD:(h + j + 1) * HD], PT[u % 2][:, 2 * j + kb, :],
                                       start=(kb == 0), stop=(kb == NT - 1), tile_position=(0, QUAD * hq))
                mm.then_inc(pv_done, 1)

            def output(b, s, t, part=None):
                if part != 1:
                    pe.wait_ge(at_done, KD * b + KD)
                    if before_last(b):
                        pe.wait_ge(x1_done, 2 * b - 1 + t)
                    elif t == 0:
                        pe.wait_ge(v_done, 2 * b + 5)
                    else:
                        pe.wait_ge(k_lo, 2 * b + 6)
                for j in range(KD):
                    if part is None or part == j // 2:
                        mm = pe.matmul((bA if t == 0 else bB)[:, :], AT[s][:, j, t * P:(t + 1) * P], sbw["woT"][:, j, :],
                                       start=(j == 0), stop=(j == KD - 1))
                if part != 0:
                    mm.then_inc(out_done, 1)

            for k in range(10):
                piece(0, 0, k)
            for k in range(2):
                piece(1, 1, k)

            def body(b, s, first, last):
                for u in range(UNITS):
                    scores(b, s, u)
                    for k, part in PE_STEP.get(u, ()):
                        if not last:
                            piece(b + 1, 1 - s, k, part)
                    if u in (11, 12, 13, 14) and not first:
                        output(b - 1, 1 - s, (u - 11) // 2, (u - 11) % 2)
                    if u == UNITS - 1 and not before_last(b):
                        piece(b + 2, s, 0)
                        piece(b + 2, s, 1)
                    if u >= 2:
                        turn(b, u - 2)
                    elif not first:
                        turn(b - 1, UNITS + u - 2)
                    if u >= 3:
                        values(b, s, u - 3)
                    elif not first:
                        values(b - 1, 1 - s, UNITS + u - 3)

            over_sequences(pe, body)
            b = NB - 1
            turn(b, UNITS - 2)
            values(b, 1, UNITS - 3)
            turn(b, UNITS - 1)
            values(b, 1, UNITS - 2)
            values(b, 1, UNITS - 1)
            for t in range(NT):
                output(b, 1, t)


XH_SLOTS = 4
CH = 32
CD = SL // CH
LB = D // P
NP = CD // 2 + 1
BJ = NB * CD
TAPS = P + D
NE, TOP = 16, 2


def tile_ap(t, offset, dims):
    full = t[:]
    return bass.AP(full.tensor, full.offset + offset, [list(full.ap[0])] + dims)


def convolution_program(nc, x1, ctx_in, taps, skip, router_w, x2, xn3, kpad, keep, psum, ident, m_half,
                        gate_w, up_w, WGU):
    ctx = ExitStack()
    with ctx:
        def sb(name, shape, dt=F32):
            return ctx.enter_context(nc.sbuf_tensor(name, shape, dt))

        def sem(name):
            return ctx.enter_context(nc.semaphore(name))

        scores, top8, idx8 = keep
        KP, DW = sb("KP", [CH, TAPS]), sb("DW", [CH, 1])
        RW = sb("RW", [P, KD, NE])
        XH = [sb(f"XH{i}", [P, D]) for i in range(XH_SLOTS)]
        CX = [sb(f"CX{s}", [P, D]) for s in range(2)]
        TT = [sb(f"TT{s}", [P, D]) for s in range(2)]
        XN2 = sb("XN2", [P, D])
        Q2 = [sb(f"Q2_{s}", [P, LB, 2 * BJ]) for s in range(2)]
        CR = sb("CR", [P, D])
        C2 = sb("C2", [P, LB, 2 * BJ])
        KV = [sb(f"KV{s}", [P, LB, NP * BJ]) for s in range(2)]
        Z1 = [sb(f"Z1_{i}", [P, NP, BJ]) for i in range(2)]
        Z2 = [sb(f"Z2_{i}", [P, 3, 2 * BJ]) for i in range(2)]
        X2 = [sb(f"X2_{s}", [P, D]) for s in range(2)]
        XN3 = [sb(f"XN3_{s}", [P, D]) for s in range(2)]
        X3T = sb("X3T", [P, KD, P])
        st, mv = sb("st2", [P, 2, 6]), sb("mv2", [P, 2, 2])
        vare, rstd = sb("vare2", [P, 2]), sb("rstd2", [P, 2])

        Y = [psum[:, 2 * i:2 * i + 2, :].rearrange("p k n -> p (k n)") for i in range(2)]
        OT = [psum[:, 4 + s, :] for s in range(2)]
        bQ, bC = psum[:, 6, :], psum[:, 7, :]

        k_in, k_padded, k_set, k_out = sem("k_in"), sem("k_padded"), sem("k_set"), sem("k_out")
        z_set, rw_in, wgu_in, held = sem("z_set"), sem("rw_in"), sem("wgu_in"), sem("held")
        xh_in = [sem(f"xh_in{i}") for i in range(XH_SLOTS)]
        cx_in = [sem(f"cx_in{s}") for s in range(2)]
        tt_in = [sem(f"tt_in{s}") for s in range(2)]
        chain, vare_done, rstd_done, may_aggr = sem("chain2"), sem("vare_done"), sem("rstd_done2"), sem("may_aggr2")
        xn2_done, xn3_done, x2_done = sem("xn2_done"), sem("xn3_done"), sem("x2_done")
        c_flipped, c_turned, c_done, kv_done = sem("c_flipped"), sem("c_turned"), sem("c_done"), sem("kv_done")
        q_turned, q_done = sem("q_turned"), sem("q_done")
        y_done, z_done, zt_done = sem("y_done"), sem("z_done"), sem("zt_done")
        x3_turned, x3_done, sc_ready, sc_done = sem("x3_turned"), sem("x3_done"), sem("sc_ready"), sem("sc_done")
        x2_out = [sem(f"x2_out{s}") for s in range(2)]

        def rows(t, h):
            return t[:, bass.ds(h * CD, CD), :].rearrange("b j d -> j b d")

        def over_heads(eng, body, lo=4, hi=CH - 4):
            for h in range(lo):
                body(h, h)
            with eng.Fori(0, (hi - lo) // 4) as i:
                for k in range(lo, lo + 4):
                    body(4 * i + k, k)
            for h in range(hi, CH):
                body(h, h)

        def inner(h):
            return not isinstance(h, int)

        block = ctx.enter_context(nc.Block())

        @block.sync
        def _(sp):
            with nc.allow_non_contiguous_dma(reason="a column, once"):
                sp.dma_start(DW[:], skip.rearrange("(p o) -> p o", o=1)).then_inc(k_in, 16)
            sp.dma_start(RW[:], router_w.rearrange("(k p) e -> p k e", p=P)).then_inc(rw_in, 16)
            sp.wait_ge(k_padded, 1)
            sp.dma_start(KP[:, P:TAPS], taps).then_inc(k_in, 16)
            sp.wait_ge(k_set, 1)
            sp.dma_start(kpad.ap(), KP[:]).then_inc(k_out, 16)

            def hold():
                sp.sem_inc(held, 1)

            def load_rows(h, i):
                sp.dma_start(XH[i][:], rows(x1, h)).then_inc(xh_in[i], 16)

            def load_rest(h, s):
                sp.dma_start(CX[s][:], rows(ctx_in, h)).then_inc(cx_in[s], 16)
                sp.dma_start(TT[s][:], bass.AP(kpad, h * TAPS + 1, [[1, P], [1, D]])).then_inc(tt_in[s], 16)

            def store(h, s):
                sp.wait_ge(x2_done, h + 1)
                hold()
                sp.dma_start(rows(x2, h), X2[s][:]).then_inc(x2_out[s], 16)
                sp.wait_ge(xn3_done, h + 1)
                hold()
                sp.dma_start(rows(xn3, h), XN3[s][:]).then_inc(x2_out[s], 16)

            for h in range(2):
                load_rows(h, h)
            sp.wait_ge(k_out, 16)
            for h in range(2):
                load_rest(h, h)
            load_rows(2, 2)

            def load_weights(h):
                assert NE * KD == 2 * CH
                for w, lo in ((gate_w, 0), (up_w, F)):
                    src = w.rearrange("e (k p) f -> (e k) p f", p=P)[bass.ds(2 * h, 2), :, :].rearrange("n p f -> p n f")
                    sp.dma_start(WGU[:, bass.ds(2 * h, 2), lo:lo + F], src).then_inc(wgu_in, 16)

            def body(h, k):
                load_weights(h)
                if inner(h) or h + 2 < CH:
                    sp.wait_ge(y_done, LB * (h + 1))
                    hold()
                    load_rest(h + 2, k % 2)
                if inner(h) or h >= 1:
                    store(h - 1, (k - 1) % 2)
                if inner(h) or h + 3 < CH:
                    if inner(h) or h >= 1:
                        sp.wait_ge(x2_done, h)
                        hold()
                    load_rows(h + 3, (k + 3) % 4)

            over_heads(sp, body)
            store(CH - 1, (CH - 1) % 2)
            for s in range(2):
                sp.wait_ge(x2_out[s], 16 * CH)
            sp.wait_ge(wgu_in, 32 * CH)

        @block.gpsimd
        def _(pool):
            def products(h, k):
                pool.wait_ge(c_done, h + 1)
                if inner(h) or h >= 2:
                    pool.wait_ge(y_done, LB * (h - 1))
                for m in range(LB):
                    one = tile_ap(C2, m * 2 * BJ, [[0, NP], [1, BJ]])
                    other = tile_ap(C2, m * 2 * BJ, [[NB, NP], [1, BJ]])
                    out = KV[k % 2][:, m, :].rearrange("p (d n) -> p d n", d=NP)
                    ins = pool.tensor_tensor(out, one, other, ALU.mult)
                ins.then_inc(kv_done, 1)

            def roots(h, n):
                pool.wait_ge(vare_done, n)
                pool.tensor_tensor(rstd[:], vare[:], m_half[:].to_broadcast([P, 2]), ALU.pow).then_inc(rstd_done, 1)

            pool.wait_ge(z_set, 3)
            roots(0, 1)
            products(0, 0)

            def body(h, k):
                roots(h, h + 2)
                if inner(h) or h + 1 < CH:
                    products(h + 1, k + 1)

            over_heads(pool, body)
            roots(CH, CH + 2)

        @block.scalar
        def _(act):
            def keep_c(h, k):
                act.wait_ge(c_turned, h + 1)
                if inner(h) or h >= 1:
                    act.wait_ge(kv_done, h)
                src = bC.rearrange("p (m n) -> p m n", m=LB)
                act.copy(C2[:, :, 0:BJ], src)
                act.copy(C2[:, :, BJ:2 * BJ], src).then_inc(c_done, 1)

            def keep_q(h, k):
                act.wait_ge(q_turned, h + 1)
                if inner(h) or h >= 2:
                    act.wait_ge(z_done, LB * (h - 1))
                src = bQ.rearrange("p (m n) -> p m n", m=LB)
                act.copy(Q2[k % 2][:, :, 0:BJ], src)
                act.copy(Q2[k % 2][:, :, BJ:2 * BJ], src).then_inc(q_done, 1)

            def keep_x3(h, k):
                act.wait_ge(x3_turned, h + 1)
                if inner(h) or h >= 1:
                    act.wait_ge(sc_ready, h)
                act.copy(X3T[:].rearrange("p k n -> p (k n)"), bC).then_inc(x3_done, 1)

            def flip_c(h, k):
                act.wait_ge(cx_in[k % 2], 8 * (h - k % 2) + 16)
                if inner(h) or h >= 1:
                    act.wait_ge(c_turned, h)
                act.copy(CR[:], tile_ap(CX[k % 2], D - 1, [[-1, D]])).then_inc(c_flipped, 1)

            flip_c(0, 0)
            keep_c(0, 0)
            flip_c(1, 1)
            keep_q(0, 0)

            def body(h, k):
                if inner(h) or h + 1 < CH:
                    keep_c(h + 1, k + 1)
                    keep_q(h + 1, k + 1)
                if inner(h) or h >= 1:
                    keep_x3(h - 1, k - 1)
                if inner(h) or h + 2 < CH:
                    flip_c(h + 2, k + 2)

            over_heads(act, body)
            keep_x3(CH - 1, CH - 1)

        @block.vector
        def _(dve):
            dve.memset(KP[:], 0.0).then_inc(k_padded, 1)
            dve.memset(Z2[0][:], 0.0).then_inc(z_set, 1)
            dve.memset(Z2[1][:], 0.0).then_inc(z_set, 1)
            dve.memset(mv[:], 0.0).then_inc(z_set, 1)
            dve.wait_ge(k_in, 32)
            dve.tensor_tensor(KP[:, P:P + 1], KP[:, P:P + 1], DW[:], ALU.add).then_inc(k_set, 1)
            dve.wait_ge(z_set, 3)

            def statistics(h, k, n):
                base = 3 * (n - 1) if isinstance(n, int) else 3 * n - 3
                nxt = inner(h) or h + 1 < CH
                prev = inner(h) or h >= 1
                if nxt:
                    i = (k + 1) % XH_SLOTS
                    dve.wait_ge(xh_in[i], 4 * (h + 1 - i) + 16)
                    ins = dve.bn_stats(st[:, 0, :], XH[i][:])
                if prev:
                    dve.wait_ge(x2_done, h)
                    ins = dve.bn_stats(st[:, 1, :], X2[(k - 1) % 2][:])
                ins.then_inc(chain, 1)
                dve.wait_ge(chain, base + 1)
                dve.sem_inc(may_aggr, 1)
                if nxt:
                    ins = dve.bn_aggr(mv[:, 0, :], st[:, 0, :])
                if prev:
                    ins = dve.bn_aggr(mv[:, 1, :], st[:, 1, :])
                ins.then_inc(chain, 1)
                dve.wait_ge(chain, base + 2)
                dve.tensor_scalar(vare[:], mv[:, :, 1], EPS, None, ALU.add).then_inc(vare_done, 1)

            def normalise(h, k, n):
                dve.wait_ge(rstd_done, n)
                if inner(h) or h + 1 < CH:
                    if inner(h) or h >= 0:
                        dve.wait_ge(q_turned, h + 1)
                    i = (k + 1) % XH_SLOTS
                    dve.tensor_scalar(XN2[:], XH[i][:], mv[:, 0, 0:1], rstd[:, 0:1], ALU.subtract, ALU.mult).then_inc(xn2_done, 1)
                if inner(h) or h >= 1:
                    if inner(h) or h >= 3:
                        dve.wait_ge(x2_out[(k - 1) % 2], 16 * (h - 1 - (k - 1) % 2))
                        dve.wait_ge(x3_turned, h - 2)
                    dve.tensor_scalar(XN3[(k - 1) % 2][:], X2[(k - 1) % 2][:], mv[:, 1, 0:1], rstd[:, 1:2],
                                      ALU.subtract, ALU.mult).then_inc(xn3_done, 1)
                dve.wait_ge(chain, 3 * n - 1)
                dve.sem_inc(chain, 1)

            def read_out(h, k, b):
                dve.wait_ge(y_done, LB * h + b + 1)
                if b == 0:
                    dve.wait_ge(q_done, h + 1)
                if inner(h) or LB * h + b >= 2:
                    dve.wait_ge(zt_done, LB * h + b - 1)
                y, q, base = Y[b % 2], Q2[k % 2], b * 2 * BJ
                dve.tensor_tensor(Z1[b % 2][:], y[:, 0:NP * BJ].rearrange("p (d n) -> p d n", d=NP),
                                  tile_ap(q, base, [[NB, NP], [1, BJ]]), ALU.mult)
                dve.tensor_tensor(tile_ap(Z2[b % 2], NB, [[2 * BJ + NB, 3], [1, BJ]]),
                                  y[:, BJ:4 * BJ].rearrange("p (d n) -> p d n", d=3),
                                  tile_ap(q, base, [[0, 3], [1, BJ]]), ALU.mult).then_inc(z_done, 1)

            def residual(h, k):
                dve.wait_ge(zt_done, LB * (h + 1))
                if inner(h) or h >= 2:
                    dve.wait_ge(x2_out[k % 2], 16 * (h - k % 2))
                dve.tensor_tensor(X2[k % 2][:], OT[k % 2], XH[k % 4][:], ALU.add).then_inc(x2_done, 1)

            def route(h, k):
                dve.wait_ge(sc_ready, h + 1)
                dve.tensor_copy(scores[:, bass.ds(h, 1), :].rearrange("p o e -> p (o e)"), OT[k % 2][:, 0:NE]).then_inc(sc_done, 1)

            statistics(-1, -1, 1)
            normalise(-1, -1, 1)

            def body(h, k):
                read_out(h, k, 0)
                if inner(h) or h >= 1:
                    residual(h - 1, k - 1)
                statistics(h, k, h + 2)
                read_out(h, k, 1)
                normalise(h, k, h + 2)
                read_out(h, k, 2)
                read_out(h, k, 3)
                if inner(h) or h >= 1:
                    route(h - 1, k - 1)

            over_heads(dve, body)
            residual(CH - 1, CH - 1)
            statistics(CH, CH, CH + 2)
            normalise(CH, CH, CH + 2)
            route(CH - 1, CH - 1)

        @block.tensor
        def _(pe):
            def turn_c(h, k):
                pe.wait_ge(c_flipped, h + 1)
                if inner(h) or h >= 1:
                    pe.wait_ge(c_done, h)
                if inner(h) or h >= 3:
                    pe.wait_ge(x3_done, h - 2)
                for m in range(LB):
                    mm = pe.transpose(bC[:, m * P:(m + 1) * P], CR[:, (LB - 1 - m) * P:(LB - m) * P], ident[:])
                mm.then_inc(c_turned, 1)

            def turn_q(h, k):
                pe.wait_ge(xn2_done, h + 1)
                if inner(h) or h >= 1:
                    pe.wait_ge(q_done, h)
                for m in range(LB):
                    mm = pe.transpose(bQ[:, m * P:(m + 1) * P], XN2[:, m * P:(m + 1) * P], ident[:])
                mm.then_inc(q_turned, 1)

            def turn_x3(h, k):
                pe.wait_ge(xn3_done, h + 1)
                if inner(h) or h + 2 < CH:
                    pe.wait_ge(c_done, h + 3)
                for m in range(KD):
                    mm = pe.transpose(bC[:, m * P:(m + 1) * P], XN3[k % 2][:, m * P:(m + 1) * P], ident[:])
                mm.then_inc(x3_turned, 1)

            def router(h, k):
                pe.wait_ge(x3_done, h + 1)
                pe.wait_ge(x2_done, h + 1)
                if not inner(h) and h == 0:
                    pe.wait_ge(rw_in, 16)
                for m in range(KD):
                    mm = pe.matmul(OT[k % 2][:, 0:NE], X3T[:, m, :], RW[:, m, :], start=(m == 0), stop=(m == KD - 1))
                mm.then_inc(sc_ready, 1)

            def convolve(h, k, b):
                if b == 0:
                    pe.wait_ge(kv_done, h + 1)
                    pe.wait_ge(tt_in[k % 2], 8 * (h - k % 2) + 16)
                if inner(h) or LB * h + b >= 2:
                    pe.wait_ge(z_done, LB * h + b - 1)
                for m in range(b + 1):
                    w = TT[k % 2][:, (b - m) * P:(b - m + 1) * P]
                    for lo, hi in ((0, 512), (512, NP * BJ)):
                        mm = pe.matmul(Y[b % 2][:, lo:hi], w, KV[k % 2][:, m, lo:hi], start=(m == 0), stop=(m == b))
                mm.then_inc(y_done, 1)

            def gather(h, k, b):
                pe.wait_ge(z_done, LB * h + b + 1)
                if b == 0 and (inner(h) or h >= 2):
                    pe.wait_ge(sc_done, h - 1)
                parts = [Z1[b % 2][:, d, :] for d in range(NP)]
                parts += [Z2[b % 2][:, d, e * BJ:(e + 1) * BJ] for d in range(3) for e in range(2)]
                for i, z in enumerate(parts):
                    mm = pe.matmul(OT[k % 2][:, b * P:(b + 1) * P], z, ident[:], start=(i == 0),
                                   stop=(i == len(parts) - 1), is_transpose=True)
                mm.then_inc(zt_done, 1)

            turn_c(0, 0)
            turn_q(0, 0)

            def body(h, k):
                nxt, prev = inner(h) or h + 1 < CH, inner(h) or h >= 1
                convolve(h, k, 0)
                if prev:
                    gather(h - 1, k - 1, 3)
                if nxt:
                    turn_c(h + 1, k + 1)
                convolve(h, k, 1)
                gather(h, k, 0)
                convolve(h, k, 2)
                gather(h, k, 1)
                if nxt:
                    turn_q(h + 1, k + 1)
                if prev:
                    turn_x3(h - 1, k - 1)
                convolve(h, k, 3)
                gather(h, k, 2)
                if prev:
                    router(h - 1, k - 1)

            over_heads(pe, body)
            gather(CH - 1, CH - 1, 3)
            turn_x3(CH - 1, CH - 1)
            router(CH - 1, CH - 1)


F = 192
FB = 96
FK = F // FB
TOKENS = NB * SL
PAIRS = TOKENS * TOP
TILES = PAIRS // P + NE - 1
HT = CH


def routing_tables():
    t = {}
    t["count_e"] = np.tile(np.arange(NE, dtype=np.float32), (P, 1))
    t["count_p"] = np.tile(np.arange(P, dtype=np.float32), (P, 1))
    t["count_128"] = np.tile(np.arange(HT, dtype=np.float32) * P, (P, 1))
    p, h = np.arange(P)[:, None], np.arange(HT)[None, :]
    t["row"] = ((p % NB) * SL + h * CD + p // NB).astype(np.float32)
    t["before"] = (np.arange(P)[:, None] < np.arange(P)[None, :]).astype(np.float32)
    t["carry"] = np.tile((np.arange(NE * HT) % HT != 0).astype(np.float32), (P, 1))
    names = list(t)
    at = dict(zip(names, np.cumsum([0] + [t[n].shape[1] for n in names])))
    return np.ascontiguousarray(np.concatenate([t[n] for n in names], 1)), {n: (int(at[n]), int(at[n] + t[n].shape[1])) for n in names}


def routing_program(nc, consts, spans, down_w, keep, WD, route, psum):
    ctx = ExitStack()
    with ctx:
        def sb(name, shape, dt=F32):
            return ctx.enter_context(nc.sbuf_tensor(name, shape, dt))

        def sem(name):
            return ctx.enter_context(nc.semaphore(name))

        scores, top8, idx8 = keep
        slots, weight, listed, expert = route
        K = sb("consts", [P, consts.shape[1]])
        c = {n: K[:, lo:hi] for n, (lo, hi) in spans.items()}
        gap, ex, den = sb("gap", [P, HT]), sb("ex", [P, HT]), sb("den3", [P, HT])
        pick = sb("pick", [P, TOP, HT])
        hot = sb("hot", [P, TOP, NE, HT])
        mask, work = sb("mask", [P, NE, HT]), sb("work", [P, NE, HT])
        incl, ones = sb("incl", [P, NE, HT]), sb("ones", [P, P])
        tiles, end, start = sb("tiles", [P, NE]), sb("end", [P, NE]), sb("start", [P, NE])
        slot_f = sb("slot_f", [P, TOP, HT])
        part_i, part_f = sb("part_i", [P, 2, TOP * HT], I32), sb("part_f", [P, 2, TOP * HT])
        R, T = [sb(f"R{i}", [P, P]) for i in range(4)], [sb(f"T{i}", [P, TILES]) for i in range(4)]
        cmp, exp_f = sb("cmp", [P, TILES, NE]), sb("exp_f", [P, TILES])

        consts_in, wd_in, gap_done, ex_done, step = sem("consts_in"), sem("wd_in"), sem("gap_done"), sem("ex_done"), sem("step")
        masked, counted, spread, added = sem("masked"), sem("counted"), sem("spread"), sem("added")
        bank_before, bank_all, bank_list = psum[:, 0, :], psum[:, 1, :], psum[:, 2, :]

        def over(ap_tile, dims, off=0):
            return tile_ap(ap_tile, off, dims)

        block = ctx.enter_context(nc.Block())

        @block.sync
        def _(sp):
            sp.dma_start(K[:], consts.ap()).then_inc(consts_in, 16)
            for e in range(NE):
                sp.dma_start(WD[:, e, :, :], down_w[e].rearrange("(c p) n -> p c n", p=FB)).then_inc(wd_in, 16)
            sp.wait_ge(wd_in, 16 * NE)

        @block.scalar
        def _(act):
            act.wait_ge(gap_done, 1)
            act.activation(ex[:], gap[:], ACT.Exp).then_inc(ex_done, 1)

        @block.vector
        def _(dve):
            n = 0

            def then(ins):
                nonlocal n
                n += 1
                ins.then_inc(step, 1)
                dve.wait_ge(step, n)

            for h in range(HT):
                dve.max(top8[:, h, :], scores[:, h, :]).then_inc(step, 1)
            n = HT
            dve.wait_ge(step, n)
            for h in range(HT):
                ins = dve.max_index(idx8[:, h, :], top8[:, h, :], scores[:, h, :])
            then(ins)
            dve.tensor_tensor(gap[:], top8[:, :, 1], top8[:, :, 0], ALU.subtract).then_inc(gap_done, 1)
            then(dve.tensor_copy(pick[:].rearrange("p c h -> p h c"), idx8[:, :, 0:TOP]))
            then(dve.memset(ones[:], 1.0))
            dve.wait_ge(consts_in, 16)
            for j in range(TOP):
                ins = dve.tensor_tensor(hot[:, j, :, :], over(K, [[1, NE], [0, HT]], spans["count_e"][0]),
                                        over(pick, [[0, NE], [1, HT]], j * HT), ALU.is_equal)
            then(ins)
            then(dve.tensor_tensor(mask[:], hot[:, 0, :, :], hot[:, 1, :, :], ALU.add))
            dve.sem_inc(masked, 1)
            dve.wait_ge(ex_done, 1)
            then(dve.tensor_scalar(den[:], ex[:], 1.0, None, ALU.add))
            then(dve.reciprocal(weight[:, 0, :], den[:]))
            then(dve.tensor_tensor(weight[:, 1, :], ex[:], weight[:, 0, :], ALU.mult))
            dve.wait_ge(counted, 1)
            flat = "p e h -> p (e h)"
            then(dve.tensor_tensor_scan(incl[:].rearrange(flat), c["carry"], bank_all, 0.0, ALU.mult, ALU.add))
            then(dve.tensor_tensor(work[:].rearrange(flat), incl[:].rearrange(flat), bank_all, ALU.subtract))
            then(dve.tensor_tensor(work[:].rearrange(flat), bank_before, work[:].rearrange(flat), ALU.add))
            then(dve.tensor_tensor(mask[:], over(incl, [[HT, NE], [0, HT]], HT - 1),
                                   over(K, [[0, NE], [1, HT]], spans["count_128"][0]), ALU.is_gt))
            then(dve.tensor_reduce(tiles[:], mask[:], AX.X, ALU.add))
            then(dve.tensor_tensor_scan(end[:], ones[:, 0:NE], tiles[:], 0.0, ALU.mult, ALU.add))
            then(dve.tensor_tensor(start[:], end[:], tiles[:], ALU.subtract))
            then(dve.scalar_tensor_tensor(work[:], over(start, [[1, NE], [0, HT]]), float(P), work[:], ALU.mult, ALU.add))
            for j in range(TOP):
                then(dve.tensor_tensor(mask[:], hot[:, j, :, :], work[:], ALU.mult))
                then(dve.tensor_reduce(slot_f[:, j, :], mask[:].rearrange("p e h -> p h e"), AX.X, ALU.add))
            then(dve.tensor_copy(slots[:], slot_f[:]))
            all_slots = slots[:].rearrange("p c h -> p (c h)")
            then(dve.tensor_scalar(part_i[:, 0, :], all_slots, 7, None, ALU.arith_shift_right))
            then(dve.tensor_scalar(part_i[:, 1, :], all_slots, P - 1, None, ALU.bitwise_and))
            then(dve.tensor_copy(part_f[:], part_i[:]))
            then(dve.tensor_tensor(cmp[:], over(end, [[0, TILES], [1, NE]]),
                                   over(K, [[1, TILES], [0, NE]], spans["count_p"][0]), ALU.is_le))
            then(dve.tensor_reduce(exp_f[:], cmp[:], AX.X, ALU.add))
            then(dve.tensor_scalar(exp_f[:], exp_f[:], float(NE - 1), None, ALU.min))
            then(dve.tensor_copy(expert[:], exp_f[:]))
            for i in range(TOP * HT):
                if i >= 4:
                    dve.wait_ge(added, i - 3)
                dve.tensor_scalar(R[i % 4][:], c["count_p"], part_f[:, 1, i:i + 1], None, ALU.is_equal)
                h = i % HT
                lo = spans["row"][0]
                dve.tensor_scalar(T[i % 4][:], c["count_p"][:, 0:TILES], part_f[:, 0, i:i + 1], K[:, lo + h:lo + h + 1],
                                  ALU.is_equal, ALU.mult).then_inc(spread, 1)
            dve.wait_ge(added, TOP * HT)
            then(dve.tensor_copy(listed[:], bank_list[:, 0:TILES]))

        @block.tensor
        def _(pe):
            pe.wait_ge(masked, 1)
            m = mask[:].rearrange("p e h -> p (e h)")
            pe.matmul(bank_before, c["before"], m, start=True, stop=True)
            pe.matmul(bank_all, ones[:], m, start=True, stop=True).then_inc(counted, 1)
            for i in range(TOP * HT):
                pe.wait_ge(spread, i + 1)
                pe.matmul(bank_list[:, 0:TILES], R[i % 4][:], T[i % 4][:], start=(i == 0), stop=(i == TOP * HT - 1)).then_inc(added, 1)


def experts_program(nc, xn3, y, WGU, WD, route, psum, ident):
    ctx = ExitStack()
    with ctx:
        def sb(name, shape, dt=F32):
            return ctx.enter_context(nc.sbuf_tensor(name, shape, dt))

        def sem(name):
            return ctx.enter_context(nc.semaphore(name))

        slots, weight, listed, expert = route
        col = [sb(f"col{i}", [P, 1], I32) for i in range(4)]
        G = [sb(f"G{i}", [P, D]) for i in range(4)]
        GT = [sb(f"GT{i}", [P, KD, P]) for i in range(2)]
        SG, HM = [sb(f"SG{i}", [P, F]) for i in range(2)], [sb(f"HM{i}", [P, F]) for i in range(2)]
        HTT = [sb(f"HT{i}", [FB, FK, P]) for i in range(2)]
        YO = [sb(f"YO{i}", [P, D]) for i in range(2)]

        bG = [psum[:, i, :] for i in range(2)]
        bGU = [psum[:, 2 + i, :] for i in range(2)]
        bH = [psum[:, 4 + i, :] for i in range(2)]
        bY = [psum[:, 6 + i, :] for i in range(2)]

        col_done = sem("col_done")
        g_in = [sem(f"g_in{i}") for i in range(4)]
        g_turned, gt_done, gu_done, sg_done, hm_done = (sem(n) for n in ("g_turned", "gt_done", "gu_done", "sg_done", "hm_done"))
        h_turned, ht_done, dn_done, yo_done, held = (sem(n) for n in ("h_turned", "ht_done", "dn_done", "yo_done", "held3"))
        y_out = [sem(f"y_out{i}") for i in range(2)]

        LO, HI = 4, TILES - 3
        assert (HI - LO) % 4 == 0

        def over_tiles(eng, body):
            for t in range(LO):
                body(t, t)
            with eng.Fori(0, (HI - LO) // 4) as i:
                for k in range(LO, LO + 4):
                    body(4 * i + k, k)
            for t in range(HI, TILES):
                body(t, t)

        def inner(t):
            return not isinstance(t, int)

        block = ctx.enter_context(nc.Block())

        @block.gpsimd
        def _(pool):
            def fetch(t, k):
                if inner(t) or t >= 4:
                    pool.wait_ge(g_turned, t - 3)
                    pool.sem_inc(held, 1)
                pool.tensor_copy(col[k % 4][:], listed[:, bass.ds(t, 1)]).then_inc(col_done, 1)
                pool.wait_ge(col_done, t + 1)
                pool.sem_inc(held, 1)
                pool.indirect_dma_start(G[k % 4][:], None, xn3, bass.IndirectOffsetOnAxis(ap=col[k % 4][:, 0:1], axis=0)).then_inc(g_in[k % 4], 16)

            over_tiles(pool, fetch)

        @block.sync
        def _(sp):
            def store(t, k):
                sp.wait_ge(yo_done, t + 1)
                sp.sem_inc(held, 1)
                sp.dma_start(y[bass.ds(t * P, P), :], YO[k % 2][:]).then_inc(y_out[k % 2], 16)

            over_tiles(sp, store)
            for i in range(2):
                sp.wait_ge(y_out[i], 16 * ((TILES + 1 - i) // 2))

        @block.scalar
        def _(act):
            def keep_g(t, k):
                act.wait_ge(g_turned, t + 1)
                if inner(t) or t >= 2:
                    act.wait_ge(gu_done, t - 1)
                act.copy(GT[k % 2][:].rearrange("p k n -> p (k n)"), bG[k % 2]).then_inc(gt_done, 1)

            def silu(t, k):
                act.wait_ge(gu_done, t + 1)
                if inner(t) or t >= 2:
                    act.wait_ge(hm_done, t - 1)
                act.activation(SG[k % 2][:], bGU[k % 2][:, 0:F], ACT.Silu).then_inc(sg_done, 1)

            def keep_y(t, k):
                act.wait_ge(dn_done, t + 1)
                if inner(t) or t >= 2:
                    act.wait_ge(y_out[k % 2], 8 * (t - k % 2))
                act.copy(YO[k % 2][:], bY[k % 2]).then_inc(yo_done, 1)

            keep_g(0, 0)

            def body(t, k):
                silu(t, k)
                if inner(t) or t + 1 < TILES:
                    keep_g(t + 1, k + 1)
                if inner(t) or t >= 1:
                    keep_y(t - 1, k - 1)

            over_tiles(act, body)
            keep_y(TILES - 1, TILES - 1)

        @block.vector
        def _(dve):
            def body(t, k):
                dve.wait_ge(sg_done, t + 1)
                if inner(t) or t >= 2:
                    dve.wait_ge(h_turned, t - 1)
                dve.tensor_tensor(HM[k % 2][:], bGU[k % 2][:, F:2 * F], SG[k % 2][:], ALU.mult).then_inc(hm_done, 1)
                dve.wait_ge(h_turned, t + 1)
                if inner(t) or t >= 2:
                    dve.wait_ge(dn_done, t - 1)
                dve.tensor_copy(HTT[k % 2][:].rearrange("p c n -> p (c n)"), bH[k % 2][0:FB, 0:FK * P]).then_inc(ht_done, 1)

            over_tiles(dve, body)

        @block.tensor
        def _(pe):
            def turn_g(t, k):
                pe.wait_ge(g_in[k % 4], 4 * (t - k % 4) + 16)
                if inner(t) or t >= 2:
                    pe.wait_ge(gt_done, t - 1)
                for m in range(KD):
                    mm = pe.transpose(bG[k % 2][:, m * P:(m + 1) * P], G[k % 4][:, m * P:(m + 1) * P], ident[:])
                mm.then_inc(g_turned, 1)

            def gate_up(t, k):
                e = pe.value_load(expert[0:1, bass.ds(t, 1)], min_val=0, max_val=NE - 1)
                pe.wait_ge(gt_done, t + 1)
                if inner(t) or t >= 2:
                    pe.wait_ge(hm_done, t - 1)
                for m in range(KD):
                    mm = pe.matmul(bGU[k % 2][:, 0:2 * F], GT[k % 2][:, m, :], WGU[:, bass.ds(e * KD + m, 1), :].rearrange("p o n -> p (o n)"),
                                   start=(m == 0), stop=(m == KD - 1))
                mm.then_inc(gu_done, 1)

            def turn_h(t, k):
                pe.wait_ge(hm_done, t + 1)
                if inner(t) or t >= 2:
                    pe.wait_ge(ht_done, t - 1)
                for m in range(FK):
                    mm = pe.transpose(bH[k % 2][0:FB, m * P:(m + 1) * P], HM[k % 2][:, m * FB:(m + 1) * FB], ident[:])
                mm.then_inc(h_turned, 1)

            def down(t, k):
                e = pe.value_load(expert[0:1, bass.ds(t, 1)], min_val=0, max_val=NE - 1)
                pe.wait_ge(ht_done, t + 1)
                if inner(t) or t >= 2:
                    pe.wait_ge(yo_done, t - 1)
                for m in range(FK):
                    mm = pe.matmul(bY[k % 2], HTT[k % 2][:, m, :], WD[:, bass.ds(e, 1), m, :].rearrange("p o n -> p (o n)"),
                                   start=(m == 0), stop=(m == FK - 1))
                mm.then_inc(dn_done, 1)

            turn_g(0, 0)

            def body(t, k):
                gate_up(t, k)
                if inner(t) or t + 1 < TILES:
                    turn_g(t + 1, k + 1)
                if inner(t) or t >= 1:
                    down(t - 1, k - 1)
                turn_h(t, k)

            over_tiles(pe, body)
            down(TILES - 1, TILES - 1)


def combine_program(nc, x2, y, out, route):
    ctx = ExitStack()
    with ctx:
        def sb(name, shape, dt=F32):
            return ctx.enter_context(nc.sbuf_tensor(name, shape, dt))

        def sem(name):
            return ctx.enter_context(nc.semaphore(name))

        slots, weight, listed, expert = route
        N = 4
        col = [sb(f"slot{i}", [P, TOP], I32) for i in range(N)]
        Y1, Y2 = [sb(f"Y1_{i}", [P, D]) for i in range(N)], [sb(f"Y2_{i}", [P, D]) for i in range(N)]
        X, O = [sb(f"X2in{i}", [P, D]) for i in range(N)], [sb(f"O{i}", [P, D]) for i in range(N)]
        w = [sb(f"w{i}", [P, TOP]) for i in range(N)]
        cols_done, w_done, first, done, held = sem("cols_done"), sem("w_done"), sem("first"), sem("done"), sem("held4")
        y_in = [sem(f"y_in{i}") for i in range(N)]
        x_in = [sem(f"x2_in{i}") for i in range(N)]
        stored = [sem(f"stored{i}") for i in range(N)]

        def over_tiles(eng, body):
            for h in range(N):
                body(h, h)
            with eng.Fori(0, HT // N - 1) as i:
                for k in range(N):
                    body(4 * i + (k + N), k)

        def inner(h):
            return not isinstance(h, int)

        def rows(t, h):
            return t[:, bass.ds(h * CD, CD), :].rearrange("b j d -> j b d")

        block = ctx.enter_context(nc.Block())

        @block.gpsimd
        def _(pool):
            def body(h, k):
                if inner(h):
                    pool.wait_ge(done, h - N + 1)
                    pool.sem_inc(held, 1)
                pool.tensor_copy(col[k][:], slots[:, :, bass.ds(h, 1)].rearrange("p c o -> p (c o)")).then_inc(cols_done, 1)
                pool.wait_ge(cols_done, h + 1)
                pool.sem_inc(held, 1)
                for j, dst in enumerate((Y1[k], Y2[k])):
                    pool.indirect_dma_start(dst[:], None, y, bass.IndirectOffsetOnAxis(ap=col[k][:, j:j + 1], axis=0)).then_inc(y_in[k], 16)

            over_tiles(pool, body)

        @block.sync
        def _(sp):
            def load(h, k):
                if inner(h):
                    sp.wait_ge(done, h - N + 1)
                    sp.sem_inc(held, 1)
                sp.dma_start(X[k][:], rows(x2, h)).then_inc(x_in[k], 16)

            over_tiles(sp, load)

        @block.scalar
        def _(act):
            def store(h, k):
                act.wait_ge(done, h + 1)
                act.sem_inc(held, 1)
                act.dma_start(rows(out, h), O[k][:]).then_inc(stored[k], 16)

            over_tiles(act, store)
            for k in range(N):
                act.wait_ge(stored[k], 16 * HT // N)

        @block.vector
        def _(dve):
            def body(h, k):
                if inner(h):
                    dve.wait_ge(stored[k], 4 * (h - k))
                dve.tensor_copy(w[k][:], weight[:, :, bass.ds(h, 1)].rearrange("p c o -> p (c o)")).then_inc(w_done, 1)
                dve.wait_ge(w_done, h + 1)
                dve.wait_ge(x_in[k], 4 * (h - k) + 16)
                dve.wait_ge(y_in[k], 8 * (h - k) + 32)
                dve.scalar_tensor_tensor(O[k][:], Y1[k][:], w[k][:, 0:1], X[k][:], ALU.mult, ALU.add).then_inc(first, 1)
                dve.wait_ge(first, h + 1)
                dve.scalar_tensor_tensor(O[k][:], Y2[k][:], w[k][:, 1:2], O[k][:], ALU.mult, ALU.add).then_inc(done, 1)

            over_tiles(dve, body)


def program(nc, a, out):
    with ExitStack() as ctx:
        def sb(name, shape, dt=F32):
            return ctx.enter_context(nc.sbuf_tensor(name, shape, dt))

        psum = ctx.enter_context(nc.psum_tensor("psum", [P, 8, 512], F32))
        banks = [psum[:, i, :] for i in range(8)]
        ident, tab, sel = sb("ident", [P, P]), sb("rot_tab", [P, SL]), sb("rot_sel", [P, P])
        m_half = sb("m_half", [P, 1])
        keep = (sb("scores", [P, CH, NE]), sb("top8", [P, CH, 8]), sb("idx8", [P, CH, 8], U32))
        x1 = nc.dram_tensor("x1", [NB, SL, D], F32).ap()
        x2 = nc.dram_tensor("x2", [NB, SL, D], F32).ap()
        xn3 = nc.dram_tensor("xn3", [NB, SL, D], F32).ap()
        kpad = nc.dram_tensor("kpad", [CH, TAPS], F32)
        pick = np.zeros((P, P), np.float32)
        for r in range(ROT):
            pick[r, r] = pick[SWAP + r, r] = 1.0
        w = {n[8:]: v for n, v in a.items() if n.startswith("L0_attn_")}
        w["tab"] = nc.inline_tensor(rotary_table(), name="c_tab").ap()
        w["sel"] = nc.inline_tensor(pick, name="c_sel").ap()
        with ExitStack() as inner:
            def wsb(name, shape):
                return inner.enter_context(nc.sbuf_tensor(name, shape, F32))
            sbw = {"qT_w": wsb("qT_w", [P, KD, D]), "dkvT": wsb("dkvT", [P, KD, P]), "kT_w": wsb("kT_w", [P, D]),
                   "vT_w": wsb("vT_w", [P, D]), "woT": wsb("woT", [P, KD, D]), "xqT_f": wsb("xqT_f", [P, KD, P]),
                   "xkT": wsb("xkT", [P, P]), "b_q": wsb("b_q", [P, KD]), "b_k": wsb("b_k", [P, KD]),
                   "b_xq": wsb("b_xq", [P, 1]), "b_xk": wsb("b_xk", [P, 1]), "b_dkv": wsb("b_dkv", [P, 1]),
                   "b_o": wsb("b_o", [P, D]), "m_half": m_half}
            setup_program(nc, w, sbw, banks, tab, sel, ident)
            attention_program(nc, a["x"], x1, sbw, banks, tab, sel, ident)
        WGU = sb("WGU", [P, NE * KD, 2 * F])
        convolution_program(nc, x1, a["ctx_2048"], a["L0_xattn_ssm_kernel"], a["L0_xattn_D"], a["L0_ffn_router_w"],
                            x2, xn3, kpad, keep, psum, ident, m_half, a["L0_ffn_gate_w"], a["L0_ffn_up_w"], WGU)
        WD = sb("WD", [FB, NE, FK, D])
        route = (sb("slots", [P, TOP, HT], I32), sb("weight", [P, TOP, HT]), sb("listed", [P, TILES], I32), sb("expert", [P, TILES], I32))
        table, spans = routing_tables()
        y = nc.dram_tensor("y", [TILES * P, D], F32).ap()
        routing_program(nc, nc.inline_tensor(table, name="c_route"), spans, a["L0_ffn_down_w"], keep, WD, route, psum)
        experts_program(nc, xn3.rearrange("b t d -> (b t) d"), y, WGU, WD, route, psum, ident)
        combine_program(nc, x2, y, out, route)


STAGE = 3

_INS = ['x', 'ctx_2048', 'L0_attn_w_down_q', 'L0_attn_b_down_q', 'L0_attn_w_up_q', 'L0_attn_b_up_q', 'L0_attn_w_down_kv',
        'L0_attn_b_down_kv', 'L0_attn_w_up_k', 'L0_attn_b_up_k', 'L0_attn_w_up_v', 'L0_attn_b_up_v', 'L0_attn_wq_r',
        'L0_attn_bq_r', 'L0_attn_wk_r', 'L0_attn_bk_r', 'L0_attn_wo', 'L0_attn_bo', 'L0_xattn_ssm_kernel', 'L0_xattn_D',
        'L0_ffn_router_w', 'L0_ffn_gate_w', 'L0_ffn_up_w', 'L0_ffn_down_w']


def kernel(**inputs):
    import numpy as _np
    import concourse.bacc as _bacc
    from concourse import mybir as _mybir
    from concourse.bass_utils import run_bass_kernel_spmd as _run

    nc = _bacc.Bacc("TRN2", target_bir_lowering=False, num_devices=1)
    arrays, args = {}, {}
    for name in _INS:
        a = _np.ascontiguousarray(inputs[name])
        arrays[f"in_{name}_dram"] = a
        args[name] = nc.dram_tensor(f"in_{name}_dram", a.shape, _mybir.dt.from_np(a.dtype), kind="ExternalInput").ap()
    out = nc.dram_tensor("out_0_dram", (16, 256, 512), _mybir.dt.float32, kind="ExternalOutput").ap()
    program(nc, args, out)
    r = _run(nc, [arrays], core_ids=[0])
    return r.results[0]["out_0_dram"]
```

```python
from contextlib import ExitStack

import numpy as np

import concourse.bass as bass
from concourse import mybir

F32 = mybir.dt.float32
F16 = mybir.dt.float16
I32 = mybir.dt.int32
U32 = mybir.dt.uint32
ALU = mybir.AluOpType
ACT = mybir.ActivationFunctionType
AX = mybir.AxisListType

P = 128
NB, SL, D = 16, 256, 512
NT = SL // P
KD = D // P
DQ, DKV = 384, 128
NH, HD = 16, 32
KQ = DQ // P
ROT = 10
EPS = 1e-5
SCALE = float(1.0 / np.sqrt(HD))
SWAP = 64
UNITS = 2 * NH // 2
QUAD = 32


def rotary_table():
    exps = np.arange(0, D, 2)
    tn = np.array([np.float32(1.0) / (np.float32(10000.0 ** e) / np.float32(D)) if e < ROT else 0.0 for e in exps], np.float32)
    ang = np.outer(np.arange(SL, dtype=np.float32), tn).astype(np.float32).astype(np.float64)
    tab = np.zeros((P, SL), np.float32)
    for r in range(ROT):
        a = ang[:, r // 2]
        tab[r] = np.cos(a) - 1.0
        tab[SWAP + r] = np.sin(a) if r % 2 else -np.sin(a)
    return tab


def setup_program(nc, w, sbw, psum, tab, sel, ident):
    ctx = ExitStack()
    with ctx:
        def sb(name, shape, dt=F32):
            return ctx.enter_context(nc.sbuf_tensor(name, shape, dt))

        def sem(name):
            return ctx.enter_context(nc.semaphore(name))

        upq, rq = sb("upq", [P, KD, DQ]), sb("rq", [P, KD, DQ])
        upk, rk = sb("upk", [P, KD, DKV]), sb("rk", [P, KD, DKV])
        upv, wo = sb("upv", [P, KD, DKV]), sb("wo_nat", [P, KD, D])
        dq, dkv = sb("dq", [P, KQ, D]), sb("dkv", [P, D])
        xq, xk = sb("xq", [P, DQ]), sb("xk", [P, DKV])
        sqT, xqT = sb("sqT", [P, KQ, D]), sb("xqT", [P, KQ, P])
        b_up, b_r, b_dq = sb("b_up", [P, 2, KD]), sb("b_r", [P, 2, KD]), sb("b_dq", [P, KQ])
        b_x, b_v, bv_rep = sb("b_x", [P, 2]), sb("b_v", [P, KD]), sb("bv_rep", [P, KD, P])

        zeroed, ident_at = sem("zeroed"), sem("ident_at")
        loaded, summed = sem("loaded"), sem("summed")
        turned, kept = sem("turned"), sem("kept")
        tables, rot_in = sem("tables"), sem("rot_in")

        blk = "(o p) i -> p o i"
        block = ctx.enter_context(nc.Block())
        groups = []
        for c in range(KQ):
            groups.append(("T", [upq[:, o, c * P:(c + 1) * P] for o in range(KD)], sqT[:, c, :], 1.0))
        groups.append(("T", [xq[:, c * P:(c + 1) * P] for c in range(KQ)], xqT[:, :, :].rearrange("p c n -> p (c n)"), 1.0))
        groups.append(("T", [dkv[:, k * P:(k + 1) * P] for k in range(KD)], sbw["dkvT"][:, :, :].rearrange("p c n -> p (c n)"), 1.0))
        groups.append(("T", [upk[:, o, :] for o in range(KD)], sbw["kT_w"][:, :], 1.0))
        groups.append(("T", [upv[:, o, :] for o in range(KD)], sbw["vT_w"][:, :], 1.0))
        groups.append(("T", [xk[:, :]], sbw["xkT"][:, :], 1.0))
        for k in range(KD):
            groups.append(("T", [wo[:, o, k * P:(k + 1) * P] for o in range(KD)], sbw["woT"][:, k, :], 1.0))
        for i in range(KD):
            groups.append(("fold", i, sbw["qT_w"][:, i, :], SCALE))
        groups.append(("fold_rot", None, sbw["xqT_f"][:, :, :].rearrange("p c n -> p (c n)"), SCALE))
        groups.append(("bias_q", None, None, None))
        groups.append(("bias_o", None, None, None))
        G = len(groups)
        loads = 0

        @block.sync
        def _(sp):
            nonlocal loads
            sp.dma_start(tab[:], w["tab"]).then_inc(tables, 16)
            sp.dma_start(sel[:], w["sel"]).then_inc(tables, 16)
            for dst, src in ((upq[:], w["w_up_q"].rearrange(blk, p=P)), (rq[:], w["wq_r"].rearrange(blk, p=P)),
                             (upk[:], w["w_up_k"].rearrange(blk, p=P)), (rk[:], w["wk_r"].rearrange(blk, p=P)),
                             (upv[:], w["w_up_v"].rearrange(blk, p=P)), (wo[:], w["wo"].rearrange(blk, p=P)),
                             (dq[:], w["w_down_q"].rearrange("(c p) i -> p c i", p=P)), (dkv[:], w["w_down_kv"])):
                sp.dma_start(dst, src).then_inc(loaded, 16)
                loads += 1
            for dst, src in ((b_up[:, 0, :], "b_up_q"), (b_up[:, 1, :], "b_up_k"), (b_r[:, 0, :], "bq_r"),
                             (b_r[:, 1, :], "bk_r"), (b_dq[:], "b_down_q"), (b_v[:], "b_up_v")):
                with nc.allow_non_contiguous_dma(reason="a bias, once"):
                    sp.dma_start(dst, w[src].rearrange("(o p) -> p o", p=P)).then_inc(loaded, 16)
                loads += 1
            sp.dma_start(sbw["b_dkv"][:], w["b_down_kv"].rearrange("(p o) -> p o", o=1)).then_inc(loaded, 16)
            sp.dma_start(sbw["b_o"][:], bass.AP(w["bo"].tensor, 0, [[0, P], [1, D]])).then_inc(loaded, 16)
            loads += 2
            sp.wait_ge(zeroed, 3)
            for dst, src, n in ((xq, w["wq_r"], DQ), (xk, w["wk_r"], DKV)):
                sp.dma_start(dst[0:ROT, :], src[0:ROT, :]).then_inc(rot_in, 16)
                for odd in range(2):
                    sp.dma_start(dst[SWAP + odd:SWAP + ROT:2, :], src[1 - odd:ROT:2, :]).then_inc(rot_in, 16)
            for col, name in enumerate(("bq_r", "bk_r")):
                v = w[name].rearrange("(p o) -> p o", o=1)
                sp.dma_start(b_x[0:ROT, col:col + 1], v[0:ROT, :]).then_inc(rot_in, 16)
                for odd in range(2):
                    with nc.allow_non_contiguous_dma(reason="a bias, once"):
                        sp.dma_start(b_x[SWAP + odd:SWAP + ROT:2, col:col + 1], v[1 - odd:ROT:2, :]).then_inc(rot_in, 16)

        ROT_LOADS = 12

        @block.gpsimd
        def _(pool):
            pool.memset(ident[:], 0.0).then_inc(ident_at, 1)
            pool.wait_ge(ident_at, 1)
            pool.affine_select(out=ident[:], in_=ident[:], compare_op=ALU.not_equal, fill=1.0, base=0,
                               pattern=[[-1, P]], channel_multiplier=1).then_inc(ident_at, 1)

        @block.vector
        def _(dve):
            dve.memset(xq[:], 0.0).then_inc(zeroed, 1)
            dve.memset(xk[:], 0.0).then_inc(zeroed, 1)
            dve.memset(b_x[:], 0.0).then_inc(zeroed, 1)
            dve.wait_ge(loaded, 16 * loads)
            dve.wait_ge(rot_in, 16 * ROT_LOADS)
            dve.tensor_tensor(upq[:], upq[:], rq[:], ALU.add).then_inc(summed, 1)
            dve.tensor_tensor(upk[:], upk[:], rk[:], ALU.add).then_inc(summed, 1)
            dve.tensor_tensor(b_up[:], b_up[:], b_r[:], ALU.add).then_inc(summed, 1)
            dve.memset(bv_rep[:], 1.0).then_inc(summed, 1)
            dve.wait_ge(summed, 4)
            for k in range(KD):
                dve.tensor_scalar(bv_rep[:, k, :], bv_rep[:, k, :], b_v[:, k:k + 1], None, ALU.mult).then_inc(summed, 1)
            for g, (kind, arg, dst, scale) in enumerate(groups):
                bank = psum[g % 8]
                dve.wait_ge(turned, g + 1)
                if kind == "bias_q":
                    dve.scalar_tensor_tensor(sbw["b_q"][:], bank[:, 0:KD], 1.0, b_up[:, 0, :], ALU.mult, ALU.add).then_inc(kept, 1)
                    dve.scalar_tensor_tensor(sbw["b_xq"][:], bank[:, KD:KD + 1], 1.0, b_x[:, 0:1], ALU.mult, ALU.add).then_inc(summed, 1)
                    dve.wait_ge(kept, g + 1)
                    dve.wait_ge(summed, 5 + KD)
                    dve.tensor_scalar(sbw["b_q"][:], sbw["b_q"][:], SCALE, None, ALU.mult).then_inc(summed, 1)
                    dve.tensor_scalar(sbw["b_xq"][:], sbw["b_xq"][:], SCALE, None, ALU.mult).then_inc(summed, 1)
                    dve.tensor_copy(sbw["b_k"][:], b_up[:, 1, :]).then_inc(summed, 1)
                    dve.tensor_copy(sbw["b_xk"][:], b_x[:, 1:2]).then_inc(summed, 1)
                elif kind == "bias_o":
                    dve.tensor_tensor(sbw["b_o"][:], bank[:, :], sbw["b_o"][:], ALU.add).then_inc(kept, 1)
                else:
                    n = P * len(arg) if kind == "T" else D
                    dve.tensor_scalar(dst, bank[:, 0:n], scale, None, ALU.mult).then_inc(kept, 1)

        @block.tensor
        def _(pe):
            pe.wait_ge(ident_at, 2)
            pe.wait_ge(summed, 4 + KD)
            for g, (kind, arg, dst, scale) in enumerate(groups):
                bank = psum[g % 8]
                if g >= 8:
                    pe.wait_ge(kept, g - 7)
                if kind == "T":
                    for j, src in enumerate(arg):
                        mm = pe.transpose(bank[:, j * P:(j + 1) * P], src, ident[:])
                elif kind == "fold":
                    pe.wait_ge(kept, KQ)
                    for c in range(KQ):
                        mm = pe.matmul(bank[:, :], dq[:, c, arg * P:(arg + 1) * P], sqT[:, c, :],
                                       start=(c == 0), stop=(c == KQ - 1))
                elif kind == "fold_rot":
                    for i in range(KD):
                        for c in range(KQ):
                            mm = pe.matmul(bank[:, i * P:(i + 1) * P], dq[:, c, i * P:(i + 1) * P], xqT[:, c, :],
                                           start=(c == 0), stop=(c == KQ - 1))
                elif kind == "bias_q":
                    for o in range(KD + 1):
                        for c in range(KQ):
                            lhs = sqT[:, c, o * P:(o + 1) * P] if o < KD else xqT[:, c, :]
                            mm = pe.matmul(bank[:, o:o + 1], lhs, b_dq[:, c:c + 1], start=(c == 0), stop=(c == KQ - 1))
                else:
                    pe.wait_ge(kept, KQ + 5 + KD)
                    for k in range(KD):
                        mm = pe.matmul(bank[:, :], bv_rep[:, k, :], sbw["woT"][:, k, :], start=(k == 0), stop=(k == KD - 1))
                mm.then_inc(turned, 1)

        @block.scalar
        def _(act):
            act.wait_ge(tables, 32)


def attention_program(nc, x, x1, sbw, psum, tab, sel, ident):
    ctx = ExitStack()
    with ctx:
        def sb(name, shape, dt=F32):
            return ctx.enter_context(nc.sbuf_tensor(name, shape, dt))

        def sem(name):
            return ctx.enter_context(nc.semaphore(name))

        X = [sb(f"X{s}", [P, NT, D]) for s in range(2)]
        XB = [sb(f"XB{s}", [P, NT, D]) for s in range(2)]
        XN = sb("XN", [P, NT, D])
        stats, mv, vare, rstd = sb("stats", [P, 6]), sb("mv", [P, 2]), sb("vare", [P, 1]), sb("rstd", [P, 1])
        XT = sb("XT", [P, KD, SL])
        CK = sb("CK", [P, SL])
        RQ, RK = sb("RQ", [P, SL]), sb("RK", [P, SL])
        QH, QL = sb("QH", [P, KD, SL], F16), sb("QL", [P, KD, SL], F16)
        KH, KL = sb("KH", [P, KD, SL], F16), sb("KL", [P, KD, SL], F16)
        QS = [sb(f"QS{s}", [P, 4, KD, SL], F16) for s in range(2)]
        KS = [sb(f"KS{s}", [P, 4, KD, SL], F16) for s in range(2)]
        V = [sb(f"V{s}", [P, NT, D]) for s in range(2)]
        PR = [sb(f"PR{i}", [P, 2, SL]) for i in range(4)]
        PT = [sb(f"PT{i}", [P, 4, P]) for i in range(2)]
        AT = [sb(f"AT{s}", [P, KD, SL]) for s in range(2)]
        X1 = [sb(f"X1_{s}", [P, NT, D]) for s in range(2)]
        nmax = sb("nmax", [P, 4, 2])
        den, rden = sb("den", [P, 4, 2]), sb("rden", [P, 4, 2])

        bT, bAV, bA, bB = psum[0], psum[1], psum[2], psum[3]
        bS, bP = psum[4:6], psum[6:8]

        x_in = [sem(f"x_in{s}") for s in range(2)]
        xn_done, chain = sem("xn_done"), sem("chain")
        rstd_done, half_set = sem("rstd_done"), sem("half_set")
        may_aggr = sem("may_aggr")
        turned, xt_done = sem("xT_turned"), sem("xt_done")
        front, ctr_done, rk_done = sem("front"), sem("ctr_done"), sem("rk_done")
        q_hi, q_lo, k_hi, k_lo, v_done = sem("q_hi"), sem("q_lo"), sem("k_hi"), sem("k_lo"), sem("v_done")
        qs_in = [sem(f"qs_in{s}") for s in range(2)]
        ks_in = [sem(f"ks_in{s}") for s in range(2)]
        s_done, max_done, exp_done, rd_done, pn_done = (sem(n) for n in ("s_done", "max_done", "exp_done", "rd_done", "pn_done"))
        t_done, pte_v, pte_a, pv_done, at_done = (sem(n) for n in ("t_done", "pte_v", "pte_a", "pv_done", "at_done"))
        out_done, xb_done, x1_done = sem("out_done"), sem("xb_done"), sem("x1_done")
        x1_out = [sem(f"x1_out{s}") for s in range(2)]

        BANK = [bT, bA, bA, bB, bA, bB, bT, bB, bA, bT]
        PE_STEP = {0: [(2, 0)], 1: [(2, 1)], 2: [(3, 0)], 3: [(3, 1)], 4: [(4, 0)], 5: [(4, 1)],
                   6: [(5, None), (6, None)], 8: [(7, None)], 9: [(8, None)], 10: [(9, None)]}
        ACT_STEP = {4: 3, 7: 4, 8: 6, 9: 7, 10: 8, 11: 9}
        DVE_STEP = {2: 2, 5: 3, 7: 5, 8: 4, 9: 6, 10: 7}

        def unit(u):
            return (u // 2) % 2, 2 * (2 * (u // 4) + u % 2), u // 4

        def over_sequences(eng, body):
            body(0, 0, True, False)
            body(1, 1, False, False)
            with eng.Fori(2, NB - 2, 2) as b:
                body(b, 0, False, False)
                body(b + 1, 1, False, False)
            body(NB - 2, 0, False, False)
            body(NB - 1, 1, False, True)

        def before_last(b):
            return isinstance(b, int) and b + 2 >= NB

        block = ctx.enter_context(nc.Block())

        @block.sync
        def _(sp):
            def load(b, s):
                sp.dma_start(X[s][:], x[b].rearrange("(t p) d -> p t d", p=P)).then_inc(x_in[s], 16)

            def stack(b, s):
                if not isinstance(b, int) or b >= 2:
                    sp.wait_ge(s_done, UNITS * (b - 1))
                for hi, lo, dst, parts, ready, into in ((QH, QL, QS[s], "hhl", q_lo, qs_in[s]), (KH, KL, KS[s], "hlh", k_lo, ks_in[s])):
                    sp.wait_ge(ready, 2 * b + 2)
                    for part, which in enumerate(parts):
                        src = hi if which == "h" else lo
                        for hq in range(4):
                            sp.dma_start(dst[QUAD * part:QUAD * (part + 1), hq, :, :],
                                         src[QUAD * hq:QUAD * (hq + 1), :, :]).then_inc(into, 16)

            def store(b, s):
                for t in range(NT):
                    sp.wait_ge(x1_done, 2 * b + t + 1)
                    sp.dma_start(x1[b][t * P:(t + 1) * P, :], X1[s][:, t, :]).then_inc(x1_out[s], 16)

            def refill(b, s):
                sp.wait_ge(xn_done, 2 * b - 2)
                sp.wait_ge(xb_done, 2 * b - 2)
                load(b, s)

            load(0, 0)
            load(1, 1)
            stack(0, 0)
            refill(2, 0)

            def body(b, s, first, last, more=True):
                if not last:
                    stack(b + 1, 1 - s)
                if not first:
                    store(b - 1, 1 - s)
                if more:
                    refill(b + 3, 1 - s)

            body(0, 0, True, False)
            body(1, 1, False, False)
            with sp.Fori(2, NB - 4, 2) as b:
                body(b, 0, False, False)
                body(b + 1, 1, False, False)
            body(NB - 4, 0, False, False)
            body(NB - 3, 1, False, False, False)
            body(NB - 2, 0, False, False, False)
            body(NB - 1, 1, False, True, False)
            store(NB - 1, 1)
            sp.wait_ge(x1_out[0], 16 * NB)
            sp.wait_ge(x1_out[1], 16 * NB)

        @block.gpsimd
        def _(pool):
            def norm(b, u):
                pool.wait_ge(rd_done, UNITS * b + u + 1)
                scale = rden[:, u % 4, :].rearrange("p (j o) -> p j o", o=1).to_broadcast([P, 2, SL])
                pool.tensor_tensor(PR[u % 4][:, :, :], PR[u % 4][:, :, :], scale, ALU.mult).then_inc(pn_done, 1)

            def residual(b, s, t):
                if t == 0:
                    pool.wait_ge(x_in[s], 8 * (b + 2 - s))
                if not isinstance(b, int) or b >= 2:
                    pool.wait_ge(x1_done, 2 * b - 3 + t)
                pool.tensor_tensor(XB[s][:, t, :], X[s][:, t, :], sbw["b_o"][:], ALU.add).then_inc(xb_done, 1)

            def root(b, t):
                pool.wait_ge(chain, 3 * (2 * b + t + 1))
                pool.tensor_tensor(rstd[:], vare[:], sbw["m_half"][:], ALU.pow).then_inc(rstd_done, 1)

            pool.memset(sbw["m_half"][:], -0.5).then_inc(half_set, 1)
            pool.wait_ge(half_set, 1)
            for b in range(2):
                for t in range(NT):
                    root(b, t)
            residual(0, 0, 0)
            residual(0, 0, 1)

            def body(b, s, first, last):
                for u in range(UNITS):
                    if u >= 1:
                        norm(b, u - 1)
                    elif not first:
                        norm(b - 1, UNITS - 1)
                    if u in (4, 12) and not before_last(b):
                        root(b + 2, u // 8)
                    if u in (14, 15) and not last:
                        residual(b + 1, 1 - s, u - 14)

            over_sequences(pool, body)
            norm(NB - 1, UNITS - 1)

        @block.scalar
        def _(act):
            def piece(b, s, k):
                if k < 2:
                    act.wait_ge(turned, 2 * b + k + 1)
                    if k == 0 and (not isinstance(b, int) or b >= 1):
                        act.wait_ge(front, 8 * b)
                    bank = bT if k == 0 else bA
                    act.copy(XT[:, :, k * P:(k + 1) * P], bank[:, :].rearrange("p (k n) -> p k n", k=KD)).then_inc(xt_done, 1)
                elif k in (3, 4, 6, 7):
                    dst, bias, hi, into = (QH, "b_q", q_hi, qs_in) if k < 5 else (KH, "b_k", k_hi, ks_in)
                    m0 = 2 if k in (3, 6) else 0
                    act.wait_ge(front, 8 * b + k - 1)
                    if m0 and (not isinstance(b, int) or b >= 1):
                        act.wait_ge(into[1 - s], 96 * (b + s))
                    for j in range(2):
                        ins = act.activation(dst[:, m0 + j, :], BANK[k][:, j * SL:(j + 1) * SL], ACT.Identity,
                                             bias=sbw[bias][:, m0 + j:m0 + j + 1])
                    ins.then_inc(hi, 1)
                elif k in (8, 9):
                    act.wait_ge(front, 8 * b + k - 1)
                    if k == 8 and (not isinstance(b, int) or b >= 2):
                        act.wait_ge(pv_done, UNITS * (b - 1))
                    act.copy(V[s][:, k - 8, :], BANK[k][:, :]).then_inc(v_done, 1)

            def exps(b, u):
                act.wait_ge(max_done, UNITS * b + u + 1)
                if not isinstance(b, int) or UNITS * b + u >= 4:
                    act.wait_ge(t_done, UNITS * b + u - 3)
                for j in range(2):
                    ins = act.activation(PR[u % 4][:, j, :], bS[u % 2][:, j * SL:(j + 1) * SL], ACT.Exp,
                                         bias=nmax[:, u % 4, j:j + 1], accum_out=den[:, u % 4, j:j + 1])
                ins.then_inc(exp_done, 1)

            def keep_pt(b, u):
                act.wait_ge(t_done, UNITS * b + u + 1)
                if not isinstance(b, int) or UNITS * b + u >= 2:
                    act.wait_ge(pv_done, UNITS * b + u - 1)
                act.copy(PT[1][:, :, :].rearrange("p k n -> p (k n)"), bP[1][:, :]).then_inc(pte_a, 1)

            for k in range(10):
                piece(0, 0, k)
            for k in range(2):
                piece(1, 1, k)

            def body(b, s, first, last):
                for u in range(UNITS):
                    exps(b, u)
                    if u % 2 == 0:
                        if u >= 4:
                            keep_pt(b, u - 3)
                        elif not first:
                            keep_pt(b - 1, UNITS + u - 3)
                    if u in ACT_STEP and not last:
                        piece(b + 1, 1 - s, ACT_STEP[u])
                    if u == UNITS - 1 and not before_last(b):
                        piece(b + 2, s, 0)
                        piece(b + 2, s, 1)

            over_sequences(act, body)
            keep_pt(NB - 1, UNITS - 3)
            keep_pt(NB - 1, UNITS - 1)

        @block.vector
        def _(dve):
            def statistics(b, s, t):
                if t == 0:
                    dve.wait_ge(x_in[s], 8 * (b + 2 - s))
                base = 3 * (2 * b + t)
                dve.bn_stats(stats[:], X[s][:, t, :]).then_inc(chain, 1)
                dve.wait_ge(chain, base + 1)
                dve.sem_inc(may_aggr, 1)
                dve.bn_aggr(mv[:], stats[:]).then_inc(chain, 1)
                dve.wait_ge(chain, base + 2)
                dve.tensor_scalar(vare[:], mv[:, 1:2], EPS, None, ALU.add).then_inc(chain, 1)

            def normalise(b, s, t):
                dve.wait_ge(rstd_done, 2 * b + t + 1)
                if not isinstance(b, int) or b >= 1:
                    dve.wait_ge(turned, 2 * b - 1 + t)
                dve.tensor_scalar(XN[:, t, :], X[s][:, t, :], mv[:, 0:1], rstd[:, 0:1], ALU.subtract, ALU.mult).then_inc(xn_done, 1)

            def piece(b, s, k):
                dve.wait_ge(front, 8 * b + k - 1)
                if k == 2:
                    dve.tensor_scalar(CK[:], bA[:, 0:SL], sbw["b_dkv"][:, 0:1], None, ALU.add)
                    dve.scalar_tensor_tensor(RQ[:], bA[:, SL:2 * SL], sbw["b_xq"][:, 0:1], tab[:], ALU.add, ALU.mult).then_inc(ctr_done, 1)
                elif k == 5:
                    dve.scalar_tensor_tensor(RK[:], bB[:, 0:SL], sbw["b_xk"][:, 0:1], tab[:], ALU.add, ALU.mult).then_inc(rk_done, 1)
                else:
                    hi, lo, bias, hi_done, lo_done, into = (QH, QL, "b_q", q_hi, q_lo, qs_in) if k < 5 else (KH, KL, "b_k", k_hi, k_lo, ks_in)
                    m0 = 2 if k in (3, 6) else 0
                    dve.wait_ge(hi_done, 2 * b + (1 if m0 else 2))
                    if m0 and (not isinstance(b, int) or b >= 1):
                        dve.wait_ge(into[1 - s], 96 * (b + s))
                    bank = BANK[k]
                    for j in range(2):
                        ins = dve.scalar_tensor_tensor(lo[:, m0 + j, :], bank[:, j * SL:(j + 1) * SL],
                                                       sbw[bias][:, m0 + j:m0 + j + 1], hi[:, m0 + j, :], ALU.add, ALU.subtract)
                    ins.then_inc(lo_done, 1)

            def maxima(b, u):
                dve.wait_ge(s_done, UNITS * b + u + 1)
                dve.tensor_reduce(nmax[:, u % 4, :], bS[u % 2][:, :].rearrange("p (j n) -> p j n", j=2), AX.X, ALU.max,
                                  negate=True).then_inc(max_done, 1)

            def recip(b, u):
                dve.wait_ge(exp_done, UNITS * b + u + 1)
                dve.reciprocal(rden[:, u % 4, :], den[:, u % 4, :]).then_inc(rd_done, 1)

            def keep_pt(b, u):
                dve.wait_ge(t_done, UNITS * b + u + 1)
                if not isinstance(b, int) or UNITS * b + u >= 2:
                    dve.wait_ge(pv_done, UNITS * b + u - 1)
                dve.tensor_copy(PT[0][:, :, :].rearrange("p k n -> p (k n)"), bP[0][:, :]).then_inc(pte_v, 1)

            def keep_at(b, s, m):
                dve.wait_ge(pv_done, UNITS * b + 4 * m + 4)
                if m == 0 and (not isinstance(b, int) or b >= 2):
                    dve.wait_ge(out_done, 2 * b - 2)
                dve.tensor_copy(AT[s][:, m, :], bAV[:, 0:SL]).then_inc(at_done, 1)

            def add_residual(b, s, t):
                dve.wait_ge(out_done, 2 * b + t + 1)
                if t == 0:
                    dve.wait_ge(xb_done, 2 * b + 2)
                    if not isinstance(b, int) or b >= 2:
                        dve.wait_ge(x1_out[s], 16 * (b - s))
                dve.tensor_tensor(X1[s][:, t, :], (bA if t == 0 else bB)[:, :], XB[s][:, t, :], ALU.add).then_inc(x1_done, 1)

            for b in range(2):
                for t in range(NT):
                    statistics(b, b, t)
                    normalise(b, b, t)
            for k in range(2, 8):
                piece(0, 0, k)

            def body(b, s, first, last):
                for u in range(UNITS):
                    maxima(b, u)
                    if u >= 1:
                        recip(b, u - 1)
                    elif not first:
                        recip(b - 1, UNITS - 1)
                    if u % 2:
                        if u >= 3:
                            keep_pt(b, u - 3)
                        elif not first:
                            keep_pt(b - 1, UNITS - 2)
                    if u % 4 == 3:
                        if u >= 4:
                            keep_at(b, s, u // 4 - 1)
                        elif not first:
                            keep_at(b - 1, 1 - s, KD - 1)
                    if u in (13, 15) and not first:
                        add_residual(b - 1, 1 - s, (u - 13) // 2)
                    if not before_last(b):
                        if u in (4, 12):
                            statistics(b + 2, s, u // 8)
                        if u in (6, 14):
                            normalise(b + 2, s, u // 8)
                    if u in DVE_STEP and not last:
                        piece(b + 1, 1 - s, DVE_STEP[u])

            over_sequences(dve, body)
            recip(NB - 1, UNITS - 1)
            keep_pt(NB - 1, UNITS - 2)
            keep_at(NB - 1, 1, KD - 1)
            for t in range(NT):
                add_residual(NB - 1, 1, t)

        @block.tensor
        def _(pe):
            def piece(b, s, k, part=None):
                bank = BANK[k]
                if k < 2:
                    pe.wait_ge(xn_done, 2 * b + k + 1)
                    if k == 1 and (not isinstance(b, int) or b >= 3):
                        pe.wait_ge(x1_done, 2 * b - 5)
                    elif not isinstance(b, int) or b >= 1:
                        pe.wait_ge(v_done, 2 * b - k)
                    for j in range(KD):
                        mm = pe.transpose(bank[:, j * P:(j + 1) * P], XN[:, k, j * P:(j + 1) * P], ident[:])
                    mm.then_inc(turned, 1)
                    return

                def product(dst, weights, rot=None):
                    for j in range(KD):
                        mm = pe.matmul(dst, weights(j), XT[:, j, :], start=(j == 0), stop=(j == KD - 1 and rot is None))
                    if rot is not None:
                        mm = pe.matmul(dst, sel[:], rot[:], start=False, stop=True)
                    return mm

                def key_block(dst, m, rot=None):
                    mm = pe.matmul(dst, sbw["kT_w"][:, m * P:(m + 1) * P], CK[:], start=True, stop=rot is None)
                    if rot is not None:
                        mm = pe.matmul(dst, sel[:], rot[:], start=False, stop=True)
                    return mm

                if k == 2:
                    if part != 1:
                        pe.wait_ge(xt_done, 2 * b + 2)
                        mm = product(bank[:, 0:SL], lambda j: sbw["dkvT"][:, j, :])
                    if part != 0:
                        mm = product(bank[:, SL:2 * SL], lambda j: sbw["xqT_f"][:, j, :])
                elif k in (3, 4):
                    if part != 1:
                        if k == 4:
                            pe.wait_ge(ctr_done, b + 1)
                        elif not isinstance(b, int) or b >= 3:
                            pe.wait_ge(x1_done, 2 * b - 4)
                        elif b >= 1:
                            pe.wait_ge(k_lo, 2 * b)
                    m0 = 2 if k == 3 else 0
                    for m in range(m0, m0 + 2):
                        if part is None or part == m - m0:
                            mm = product(bank[:, (m - m0) * SL:(m - m0 + 1) * SL],
                                         lambda j: sbw["qT_w"][:, j, m * P:(m + 1) * P], RQ if m == 0 else None)
                elif k == 5:
                    pe.wait_ge(q_lo, 2 * b + 1)
                    mm = pe.matmul(bank[:, 0:SL], sbw["xkT"][:], CK[:], start=True, stop=True)
                elif k == 6:
                    for m in (2, 3):
                        mm = key_block(bank[:, (m - 2) * SL:(m - 1) * SL], m)
                elif k == 7:
                    pe.wait_ge(rk_done, b + 1)
                    for m in (0, 1):
                        mm = key_block(bank[:, m * SL:(m + 1) * SL], m, RK if m == 0 else None)
                else:
                    if k == 8:
                        pe.wait_ge(q_lo, 2 * b + 2)
                    else:
                        pe.wait_ge(k_lo, 2 * b + 1)
                    mm = pe.matmul(bank[:, :], CK[:, (k - 8) * P:(k - 7) * P], sbw["vT_w"][:], start=True, stop=True)
                if part != 0:
                    mm.then_inc(front, 1)

            def scores(b, s, u):
                if u == 0:
                    for sems in (qs_in, ks_in):
                        pe.wait_ge(sems[s], 96 * (b + 2 - s))
                if not isinstance(b, int) or UNITS * b + u >= 2:
                    pe.wait_ge(exp_done, UNITS * b + u - 1)
                t, h, m = unit(u)
                for j in range(2):
                    hq = (h + j) % 4
                    mm = pe.matmul(bS[u % 2][:, j * SL:(j + 1) * SL], QS[s][0:3 * QUAD, hq, m, t * P:(t + 1) * P],
                                   KS[s][0:3 * QUAD, hq, m, :], start=True, stop=True)
                mm.then_inc(s_done, 1)

            def turn(b, u):
                pe.wait_ge(pn_done, UNITS * b + u + 1)
                if not isinstance(b, int) or UNITS * b + u >= 2:
                    pe.wait_ge(pte_a if u % 2 else pte_v, (UNITS // 2) * b + u // 2)
                for j in range(2):
                    for kb in range(NT):
                        mm = pe.transpose(bP[u % 2][:, (2 * j + kb) * P:(2 * j + kb + 1) * P],
                                          PR[u % 4][:, j, kb * P:(kb + 1) * P], ident[:])
                mm.then_inc(t_done, 1)

            def values(b, s, u):
                pe.wait_ge(pte_a if u % 2 else pte_v, (UNITS // 2) * b + u // 2 + 1)
                t, h, m = unit(u)
                if u == 0:
                    pe.wait_ge(v_done, 2 * b + 2)
                if u % 4 == 0 and (not isinstance(b, int) or b >= 1 or m >= 1):
                    pe.wait_ge(at_done, KD * b + m)
                for j in range(2):
                    hq = (h + j) % 4
                    for kb in range(NT):
                        mm = pe.matmul(bAV[QUAD * hq:QUAD * (hq + 1), t * P:(t + 1) * P],
                                       V[s][:, kb, (h + j) * HD:(h + j + 1) * HD], PT[u % 2][:, 2 * j + kb, :],
                                       start=(kb == 0), stop=(kb == NT - 1), tile_position=(0, QUAD * hq))
                mm.then_inc(pv_done, 1)

            def output(b, s, t, part=None):
                if part != 1:
                    pe.wait_ge(at_done, KD * b + KD)
                    if before_last(b):
                        pe.wait_ge(x1_done, 2 * b - 1 + t)
                    elif t == 0:
                        pe.wait_ge(v_done, 2 * b + 5)
                    else:
                        pe.wait_ge(k_lo, 2 * b + 6)
                for j in range(KD):
                    if part is None or part == j // 2:
                        mm = pe.matmul((bA if t == 0 else bB)[:, :], AT[s][:, j, t * P:(t + 1) * P], sbw["woT"][:, j, :],
                                       start=(j == 0), stop=(j == KD - 1))
                if part != 0:
                    mm.then_inc(out_done, 1)

            for k in range(10):
                piece(0, 0, k)
            for k in range(2):
                piece(1, 1, k)

            def body(b, s, first, last):
                for u in range(UNITS):
                    scores(b, s, u)
                    for k, part in PE_STEP.get(u, ()):
                        if not last:
                            piece(b + 1, 1 - s, k, part)
                    if u in (11, 12, 13, 14) and not first:
                        output(b - 1, 1 - s, (u - 11) // 2, (u - 11) % 2)
                    if u == UNITS - 1 and not before_last(b):
                        piece(b + 2, s, 0)
                        piece(b + 2, s, 1)
                    if u >= 2:
                        turn(b, u - 2)
                    elif not first:
                        turn(b - 1, UNITS + u - 2)
                    if u >= 3:
                        values(b, s, u - 3)
                    elif not first:
                        values(b - 1, 1 - s, UNITS + u - 3)

            over_sequences(pe, body)
            b = NB - 1
            turn(b, UNITS - 2)
            values(b, 1, UNITS - 3)
            turn(b, UNITS - 1)
            values(b, 1, UNITS - 2)
            values(b, 1, UNITS - 1)
            for t in range(NT):
                output(b, 1, t)


XH_SLOTS = 4
CH = 32
CD = SL // CH
LB = D // P
NP = CD // 2
BJ = NB * CD
HJ = BJ // 2
PW = NP * BJ + HJ
WRAP = (NP - 1) * NB
ZS = 4
TAPS = P + D
NE, TOP = 16, 2


def part_ap(full, offset, dims):
    return bass.AP(full.tensor, full.offset + offset, [list(full.ap[0])] + dims)


def tile_ap(t, offset, dims):
    return part_ap(t[:], offset, dims)


def convolution_program(nc, x1, ctx_in, taps, skip, router_w, x2, xn3, kpad, keep, psum, ident, m_half,
                        gate_w, up_w, WGU):
    ctx = ExitStack()
    with ctx:
        def sb(name, shape, dt=F32):
            return ctx.enter_context(nc.sbuf_tensor(name, shape, dt))

        def sem(name):
            return ctx.enter_context(nc.semaphore(name))

        scores, top8, idx8 = keep
        KP, DW = sb("KP", [CH, TAPS]), sb("DW", [CH, 1])
        KPH, KPL = sb("KPH", [CH, TAPS], F16), sb("KPL", [CH, TAPS], F16)
        RW = sb("RW", [P, KD, NE])
        WS = [sb(f"WS{s}", [P, 2, 2 * F]) for s in range(2)]
        XH = [sb(f"XH{i}", [P, D]) for i in range(XH_SLOTS)]
        CX = [sb(f"CX{s}", [P, D]) for s in range(2)]
        TH, TL = ([sb(f"T{n}{s}", [P, D], F16) for s in range(2)] for n in "HL")
        XN2 = sb("XN2", [P, D])
        Q2 = [sb(f"Q2_{s}", [P, LB, 2 * BJ]) for s in range(2)]
        CR = sb("CR", [P, D])
        C2 = sb("C2", [P, LB, 2 * BJ])
        KV = sb("KV", [P, LB, PW])
        VH, VL = ([sb(f"V{n}{s}", [P, LB, PW], F16) for s in range(2)] for n in "HL")
        Z1 = [sb(f"Z1_{i}", [P, NP + 1, BJ]) for i in range(ZS)]
        Z2 = [sb(f"Z2_{i}", [P, NP - 1, BJ + WRAP]) for i in range(2)]
        X2 = [sb(f"X2_{s}", [P, D]) for s in range(2)]
        XN3 = [sb(f"XN3_{s}", [P, D]) for s in range(2)]
        X3T = sb("X3T", [P, KD, P])
        st, mv = sb("st2", [P, 2, 6]), sb("mv2", [P, 2, 2])
        vare, rstd = sb("vare2", [P, 2]), sb("rstd2", [P, 2])
        nmean, shift = sb("nmean2", [P, 2]), sb("shift2", [P, 2])

        Y = [psum[:, 2 * i:2 * i + 2, :].rearrange("p k n -> p (k n)") for i in range(2)]
        OT = [psum[:, 4 + s, :] for s in range(2)]
        bQ, bC = psum[:, 6, :], psum[:, 7, :]

        k_in, k_padded, k_set, k_out = sem("k_in"), sem("k_padded"), sem("k_set"), sem("k_out")
        z_set, rw_in, held = sem("z_set"), sem("rw_in"), sem("held")
        w_in, w_hi, w_lo = [sem(f"w_in{s}") for s in range(2)], sem("w_hi"), sem("w_lo")
        xh_in = [sem(f"xh_in{i}") for i in range(XH_SLOTS)]
        cx_in = [sem(f"cx_in{s}") for s in range(2)]
        tt_in = [sem(f"tt_in{s}") for s in range(2)]
        chain, vare_done, rstd_done, may_aggr = sem("chain2"), sem("vare_done"), sem("rstd_done2"), sem("may_aggr2")
        xn2_done, xn3_done, x2_done = sem("xn2_done"), sem("xn3_done"), sem("x2_done")
        c_flipped, c_turned, c_done = sem("c_flipped"), sem("c_turned"), sem("c_done")
        prod_done, sq_done, kv_hi, kv_lo = sem("prod_done"), sem("sq_done"), sem("kv_hi"), sem("kv_lo")
        ps_done, kp_hi, kv_lo3, rooted, wrapped = sem("ps_done"), sem("kp_hi"), sem("kv_lo3"), sem("rooted2"), sem("wrapped")
        q_turned, q_done = sem("q_turned"), sem("q_done")
        y_done, z_done, zt_done = sem("y_done"), sem("z_done"), sem("zt_done")
        x3_turned, x3_done, sc_ready, sc_done = sem("x3_turned"), sem("x3_done"), sem("sc_ready"), sem("sc_done")
        x2_out = [sem(f"x2_out{s}") for s in range(2)]

        def rows(t, h):
            return t[:, bass.ds(h * CD, CD), :].rearrange("b j d -> j b d")

        def over_heads(eng, body, lo=4, hi=CH - 4):
            for h in range(lo):
                body(h, h)
            with eng.Fori(0, (hi - lo) // 4) as i:
                for k in range(lo, lo + 4):
                    body(4 * i + k, k)
            for h in range(hi, CH):
                body(h, h)

        def inner(h):
            return not isinstance(h, int)

        block = ctx.enter_context(nc.Block())

        @block.sync
        def _(sp):
            with nc.allow_non_contiguous_dma(reason="a column, once"):
                sp.dma_start(DW[:], skip.rearrange("(p o) -> p o", o=1)).then_inc(k_in, 16)
            sp.dma_start(RW[:], router_w.rearrange("(k p) e -> p k e", p=P)).then_inc(rw_in, 16)
            sp.wait_ge(k_padded, 1)
            sp.dma_start(KP[:, P:TAPS], taps).then_inc(k_in, 16)
            sp.wait_ge(kp_hi, 1)
            sp.dma_start(kpad[0].ap(), KPH[:]).then_inc(k_out, 16)
            sp.wait_ge(k_set, 2)
            sp.dma_start(kpad[1].ap(), KPL[:]).then_inc(k_out, 16)

            def hold():
                sp.sem_inc(held, 1)

            def load_rows(h, i):
                sp.dma_start(XH[i][:], rows(x1, h)).then_inc(xh_in[i], 16)

            def load_c(h, s):
                sp.dma_start(CX[s][:], rows(ctx_in, h)).then_inc(cx_in[s], 16)

            def load_taps(h, s):
                for part, tile in zip(kpad, (TH[s], TL[s])):
                    sp.dma_start(tile[:], bass.AP(part, h * TAPS + 1, [[1, P], [1, D]])).then_inc(tt_in[s], 16)

            def store_x2(h, s):
                sp.wait_ge(x2_done, h + 1)
                hold()
                sp.dma_start(rows(x2, h), X2[s][:]).then_inc(x2_out[s], 16)

            def store_xn3(h, s):
                sp.wait_ge(xn3_done, h + 1)
                hold()
                sp.dma_start(rows(xn3, h), XN3[s][:]).then_inc(x2_out[s], 16)

            for h in range(2):
                load_rows(h, h)
                load_c(h, h)
            sp.wait_ge(k_out, 32)
            for h in range(2):
                load_taps(h, h)
            load_rows(2, 2)
            sp.wait_ge(c_flipped, 1)
            load_c(2, 0)

            def load_weights(h, s):
                if inner(h) or h >= 2:
                    sp.wait_ge(w_lo, h - 1)
                    hold()
                assert NE * KD == 2 * CH
                for w, lo in ((gate_w, 0), (up_w, F)):
                    src = w.rearrange("e (k p) f -> (e k) p f", p=P)[bass.ds(2 * h, 2), :, :].rearrange("n p f -> p n f")
                    sp.dma_start(WS[s][:, :, lo:lo + F], src).then_inc(w_in[s], 16)

            def body(h, k):
                if inner(h) or h + 3 < CH:
                    sp.wait_ge(c_flipped, h + 2)
                    hold()
                    load_c(h + 3, (k + 3) % 2)
                load_weights(h, k % 2)
                if inner(h) or h >= 1:
                    store_x2(h - 1, (k - 1) % 2)
                if inner(h) or h + 3 < CH:
                    if inner(h) or h >= 1:
                        sp.wait_ge(x2_done, h)
                        hold()
                    load_rows(h + 3, (k + 3) % 4)
                if inner(h) or h >= 1:
                    store_xn3(h - 1, (k - 1) % 2)
                if inner(h) or h + 2 < CH:
                    sp.wait_ge(y_done, LB * (h + 1))
                    hold()
                    load_taps(h + 2, k % 2)

            over_heads(sp, body)
            store_x2(CH - 1, (CH - 1) % 2)
            store_xn3(CH - 1, (CH - 1) % 2)
            for s in range(2):
                sp.wait_ge(x2_out[s], 16 * CH)

        @block.gpsimd
        def _(pool):
            def products(h, m):
                pool.wait_ge(c_done, h + 1)
                if m < 3 and (inner(h) or h >= 1):
                    pool.wait_ge(kv_lo, 3 * h - 2 + m)
                pool.tensor_tensor(KV[:, m, BJ:NP * BJ].rearrange("p (d n) -> p d n", d=NP - 1),
                                   tile_ap(C2, m * 2 * BJ, [[0, NP - 1], [1, BJ]]),
                                   tile_ap(C2, m * 2 * BJ + NB, [[NB, NP - 1], [1, BJ]]), ALU.mult)
                pool.tensor_tensor(KV[:, m, NP * BJ:PW], C2[:, m, 0:HJ], C2[:, m, HJ:BJ], ALU.mult).then_inc(prod_done, 1)

            def low(h, k):
                pool.wait_ge(kv_hi, LB * (h + 1))
                pool.tensor_tensor(VL[k % 2][:, 3, :], KV[:, 3, :], VH[k % 2][:, 3, :], ALU.subtract).then_inc(kv_lo3, 1)

            def presum(h, b):
                pool.wait_ge(z_done, LB * h + b + 1)
                z = Z1[b % ZS][:, 1:NP, :]
                pool.tensor_tensor(z, z, Z2[b % 2][:, :, 0:BJ], ALU.add).then_inc(ps_done, 1)

            def roots(h, n):
                pool.wait_ge(vare_done, n)
                if inner(h) or h >= 1:
                    pool.wait_ge(xn2_done, h + 1 if inner(h) else min(h + 1, CH))
                if inner(h) or h >= 2:
                    pool.wait_ge(xn3_done, h - 1)
                pool.tensor_tensor(rstd[:], vare[:], m_half[:].to_broadcast([P, 2]), ALU.pow).then_inc(rooted, 1)
                pool.wait_ge(rooted, n)
                pool.tensor_tensor(shift[:], nmean[:], rstd[:], ALU.mult).then_inc(rstd_done, 1)

            pool.wait_ge(z_set, 1)
            roots(0, 1)
            for m in range(3):
                products(0, m)

            def body(h, k):
                nxt = inner(h) or h + 1 < CH
                if inner(h) or h >= 1:
                    presum(h - 1, 3)
                products(h, 3)
                presum(h, 0)
                low(h, k)
                if nxt:
                    products(h + 1, 0)
                roots(h, h + 2)
                if nxt:
                    products(h + 1, 1)
                presum(h, 1)
                presum(h, 2)
                if nxt:
                    products(h + 1, 2)

            over_heads(pool, body)
            presum(CH - 1, 3)
            roots(CH, CH + 2)

        @block.scalar
        def _(act):
            def keep_c(h, k):
                act.wait_ge(c_turned, h + 1)
                if inner(h) or h >= 1:
                    act.wait_ge(prod_done, LB * h)
                src = bC.rearrange("p (m n) -> p m n", m=LB)
                act.copy(C2[:, :, 0:BJ], src)
                act.copy(C2[:, :, BJ:2 * BJ], src).then_inc(c_done, 1)

            def keep_q(h, k):
                act.wait_ge(q_turned, h + 1)
                if inner(h) or h >= 2:
                    act.wait_ge(z_done, LB * (h - 1))
                src = bQ.rearrange("p (m n) -> p m n", m=LB)
                act.copy(Q2[k % 2][:, :, 0:BJ], src)
                act.copy(Q2[k % 2][:, :, BJ:2 * BJ], src).then_inc(q_done, 1)

            def keep_x3(h, k):
                act.wait_ge(x3_turned, h + 1)
                if inner(h) or h >= 1:
                    act.wait_ge(sc_ready, h)
                act.copy(X3T[:].rearrange("p k n -> p (k n)"), bC).then_inc(x3_done, 1)

            def flip_c(h, k):
                act.wait_ge(cx_in[k % 2], 8 * (h - k % 2) + 16)
                if inner(h) or h >= 1:
                    act.wait_ge(c_turned, h)
                act.copy(CR[:], tile_ap(CX[k % 2], D - 1, [[-1, D]])).then_inc(c_flipped, 1)

            def squares(h):
                act.wait_ge(c_done, h + 1)
                if inner(h) or h >= 1:
                    act.wait_ge(kv_lo, 3 * h)
                    act.wait_ge(kv_lo3, h)
                act.activation(KV[:, :, 0:BJ], C2[:, :, 0:BJ], ACT.Square).then_inc(sq_done, 1)

            def high(h, k, m):
                act.wait_ge(prod_done, LB * h + m + 1)
                if m == 0:
                    act.wait_ge(sq_done, h + 1)
                    if inner(h) or h >= 2:
                        act.wait_ge(y_done, LB * (h - 1))
                act.copy(VH[k % 2][:, m, :], KV[:, m, :]).then_inc(kv_hi, 1)

            def normalise(h, k, n):
                act.wait_ge(rstd_done, n)
                if inner(h) or h + 1 < CH:
                    if inner(h) or h >= 0:
                        act.wait_ge(q_turned, h + 1)
                    act.activation(XN2[:], XH[(k + 1) % XH_SLOTS][:], ACT.Identity, bias=shift[:, 0:1],
                                   scale=rstd[:, 0:1]).then_inc(xn2_done, 1)
                if inner(h) or h >= 1:
                    if inner(h) or h >= 3:
                        act.wait_ge(x2_out[(k - 1) % 2], 16 * (h - 1 - (k - 1) % 2))
                        act.wait_ge(x3_turned, h - 2)
                    act.activation(XN3[(k - 1) % 2][:], X2[(k - 1) % 2][:], ACT.Identity, bias=shift[:, 1:2],
                                   scale=rstd[:, 1:2]).then_inc(xn3_done, 1)

            def split_w(h, k):
                act.wait_ge(w_in[k % 2], 16 * (h - k % 2) + 32)
                act.copy(WGU[0][:, bass.ds(2 * h, 2), :], WS[k % 2][:]).then_inc(w_hi, 1)

            normalise(-1, -1, 1)
            flip_c(0, 0)
            keep_c(0, 0)
            flip_c(1, 1)
            squares(0)
            high(0, 0, 0)
            high(0, 0, 1)
            keep_q(0, 0)

            def body(h, k):
                nxt = inner(h) or h + 1 < CH
                high(h, k, 2)
                high(h, k, 3)
                if nxt:
                    keep_c(h + 1, k + 1)
                if inner(h) or h + 2 < CH:
                    flip_c(h + 2, k + 2)
                if nxt:
                    squares(h + 1)
                    high(h + 1, k + 1, 0)
                normalise(h, k, h + 2)
                if nxt:
                    high(h + 1, k + 1, 1)
                if inner(h) or h >= 1:
                    split_w(h - 1, k - 1)
                if nxt:
                    keep_q(h + 1, k + 1)
                if inner(h) or h >= 1:
                    keep_x3(h - 1, k - 1)

            over_heads(act, body)
            split_w(CH - 1, CH - 1)
            normalise(CH, CH, CH + 2)
            keep_x3(CH - 1, CH - 1)

        @block.vector
        def _(dve):
            dve.memset(KP[:], 0.0).then_inc(k_padded, 1)
            dve.memset(mv[:], 0.0).then_inc(z_set, 1)
            dve.wait_ge(k_in, 32)
            dve.tensor_tensor(KP[:, P:P + 1], KP[:, P:P + 1], DW[:], ALU.add).then_inc(k_set, 1)
            dve.wait_ge(k_set, 1)
            dve.tensor_copy(KPH[:], KP[:]).then_inc(kp_hi, 1)
            dve.wait_ge(kp_hi, 1)
            dve.tensor_tensor(KPL[:], KP[:], KPH[:], ALU.subtract).then_inc(k_set, 1)
            dve.wait_ge(z_set, 1)

            def statistics(h, k, n):
                base = 2 * n - 2
                nxt = inner(h) or h + 1 < CH
                prev = inner(h) or h >= 1
                if nxt:
                    i = (k + 1) % XH_SLOTS
                    dve.wait_ge(xh_in[i], 4 * (h + 1 - i) + 16)
                    ins = dve.bn_stats(st[:, 0, :], XH[i][:])
                if prev:
                    dve.wait_ge(x2_done, h)
                    ins = dve.bn_stats(st[:, 1, :], X2[(k - 1) % 2][:])
                ins.then_inc(chain, 1)
                dve.wait_ge(chain, base + 1)
                dve.sem_inc(may_aggr, 1)
                if nxt:
                    ins = dve.bn_aggr(mv[:, 0, :], st[:, 0, :])
                if prev:
                    ins = dve.bn_aggr(mv[:, 1, :], st[:, 1, :])
                ins.then_inc(chain, 1)
                dve.wait_ge(chain, base + 2)
                if not isinstance(n, int) or n >= 2:
                    dve.wait_ge(rstd_done, n - 1)
                dve.tensor_scalar(nmean[:], mv[:, :, 0], -1.0, None, ALU.mult)
                dve.tensor_scalar(vare[:], mv[:, :, 1], EPS, None, ALU.add).then_inc(vare_done, 1)

            def low(h, k, m):
                dve.wait_ge(kv_hi, LB * h + m + 1)
                dve.tensor_tensor(VL[k % 2][:, m, :], KV[:, m, :], VH[k % 2][:, m, :], ALU.subtract).then_inc(kv_lo, 1)

            def read_out(h, k, b):
                dve.wait_ge(y_done, LB * h + b + 1)
                if b == 0:
                    dve.wait_ge(q_done, h + 1)
                if inner(h) or LB * h + b >= ZS:
                    dve.wait_ge(zt_done, LB * h + b + 1 - ZS)
                if inner(h) or LB * h + b >= 2:
                    dve.wait_ge(ps_done, LB * h + b - 1)
                y, q, base = Y[b % 2], Q2[k % 2], b * 2 * BJ
                z = Z2[b % 2]
                dve.tensor_tensor(z[:, :, 0:WRAP], part_ap(y, 2 * BJ - NB, [[BJ - NB, NP - 1], [1, WRAP]]),
                                  tile_ap(q, base + BJ - NB, [[-NB, NP - 1], [1, WRAP]]), ALU.mult).then_inc(wrapped, 1)
                dve.tensor_tensor(Z1[b % ZS][:, 0:NP, :], y[:, 0:NP * BJ].rearrange("p (d n) -> p d n", d=NP),
                                  tile_ap(q, base, [[NB, NP], [1, BJ]]), ALU.mult)
                dve.tensor_tensor(Z1[b % ZS][:, NP, :].rearrange("p (r n) -> p r n", r=2),
                                  part_ap(y, NP * BJ, [[0, 2], [1, HJ]]),
                                  tile_ap(q, base + HJ, [[HJ, 2], [1, HJ]]), ALU.mult)
                dve.wait_ge(wrapped, LB * h + b + 1)
                ins = dve.tensor_tensor(tile_ap(z, NB, [[BJ + WRAP + NB, NP - 1], [1, BJ]]),
                                        y[:, BJ:NP * BJ].rearrange("p (d n) -> p d n", d=NP - 1),
                                        tile_ap(q, base, [[0, NP - 1], [1, BJ]]), ALU.mult)
                ins.then_inc(z_done, 1)

            def residual(h, k):
                dve.wait_ge(zt_done, LB * (h + 1))
                if inner(h) or h >= 2:
                    dve.wait_ge(x2_out[k % 2], 16 * (h - k % 2))
                dve.tensor_tensor(X2[k % 2][:], OT[k % 2], XH[k % 4][:], ALU.add).then_inc(x2_done, 1)

            def route(h, k):
                dve.wait_ge(sc_ready, h + 1)
                dve.tensor_copy(scores[:, bass.ds(h, 1), :].rearrange("p o e -> p (o e)"), OT[k % 2][:, 0:NE]).then_inc(sc_done, 1)

            def split_w(h, k):
                dve.wait_ge(w_hi, h + 1)
                dve.tensor_tensor(WGU[1][:, bass.ds(2 * h, 2), :], WS[k % 2][:], WGU[0][:, bass.ds(2 * h, 2), :],
                                  ALU.subtract).then_inc(w_lo, 1)

            statistics(-1, -1, 1)
            low(0, 0, 0)
            low(0, 0, 1)

            def body(h, k):
                nxt = inner(h) or h + 1 < CH
                read_out(h, k, 0)
                if inner(h) or h >= 2:
                    route(h - 2, k)
                    split_w(h - 2, k)
                low(h, k, 2)
                read_out(h, k, 1)
                if inner(h) or h >= 1:
                    residual(h - 1, k - 1)
                statistics(h, k, h + 2)
                read_out(h, k, 2)
                if nxt:
                    low(h + 1, k + 1, 0)
                    low(h + 1, k + 1, 1)
                read_out(h, k, 3)

            over_heads(dve, body)
            residual(CH - 1, CH - 1)
            statistics(CH, CH, CH + 2)
            split_w(CH - 2, CH - 2)
            split_w(CH - 1, CH - 1)
            route(CH - 2, CH - 2)
            route(CH - 1, CH - 1)

        @block.tensor
        def _(pe):
            def turn_c(h, k):
                pe.wait_ge(c_flipped, h + 1)
                if inner(h) or h >= 1:
                    pe.wait_ge(c_done, h)
                if inner(h) or h >= 3:
                    pe.wait_ge(x3_done, h - 2)
                for m in range(LB):
                    mm = pe.transpose(bC[:, m * P:(m + 1) * P], CR[:, (LB - 1 - m) * P:(LB - m) * P], ident[:])
                mm.then_inc(c_turned, 1)

            def turn_q(h, k):
                pe.wait_ge(xn2_done, h + 1)
                if inner(h) or h >= 1:
                    pe.wait_ge(q_done, h)
                for m in range(LB):
                    mm = pe.transpose(bQ[:, m * P:(m + 1) * P], XN2[:, m * P:(m + 1) * P], ident[:])
                mm.then_inc(q_turned, 1)

            def turn_x3(h, k):
                pe.wait_ge(xn3_done, h + 1)
                if inner(h) or h + 2 < CH:
                    pe.wait_ge(c_done, h + 3)
                for m in range(KD):
                    mm = pe.transpose(bC[:, m * P:(m + 1) * P], XN3[k % 2][:, m * P:(m + 1) * P], ident[:])
                mm.then_inc(x3_turned, 1)

            def router(h, k):
                pe.wait_ge(x3_done, h + 1)
                pe.wait_ge(x2_done, h + 1)
                if not inner(h) and h == 0:
                    pe.wait_ge(rw_in, 16)
                for m in range(KD):
                    mm = pe.matmul(OT[k % 2][:, 0:NE], X3T[:, m, :], RW[:, m, :], start=(m == 0), stop=(m == KD - 1))
                mm.then_inc(sc_ready, 1)

            def convolve(h, k, b):
                if b < 3:
                    pe.wait_ge(kv_lo, 3 * h + b + 1)
                else:
                    pe.wait_ge(kv_lo3, h + 1)
                if b == 0:
                    pe.wait_ge(tt_in[k % 2], 16 * (h - k % 2) + 32)
                if inner(h) or LB * h + b >= 2:
                    pe.wait_ge(z_done, LB * h + b - 1)
                for m in range(b + 1):
                    for i, (taps_part, kv_part) in enumerate(((TH, VH), (TH, VL), (TL, VH))):
                        w = taps_part[k % 2][:, (b - m) * P:(b - m + 1) * P]
                        for lo, hi in ((0, NP * BJ), (NP * BJ, PW)):
                            mm = pe.matmul(Y[b % 2][:, lo:hi], w, kv_part[k % 2][:, m, lo:hi],
                                           start=(m == 0 and i == 0), stop=(m == b and i == 2))
                mm.then_inc(y_done, 1)

            def gather(h, k, b):
                pe.wait_ge(ps_done, LB * h + b + 1)
                if b == 0 and (inner(h) or h >= 2):
                    pe.wait_ge(sc_done, h - 1)
                for d in range(NP + 1):
                    mm = pe.matmul(OT[k % 2][:, b * P:(b + 1) * P], Z1[b % ZS][:, d, :], ident[:], start=(d == 0),
                                   stop=(d == NP), is_transpose=True)
                mm.then_inc(zt_done, 1)

            turn_c(0, 0)
            turn_q(0, 0)

            def body(h, k):
                nxt, prev = inner(h) or h + 1 < CH, inner(h) or h >= 1
                convolve(h, k, 0)
                if inner(h) or h >= 2:
                    router(h - 2, k)
                if prev:
                    gather(h - 1, k - 1, 2)
                if nxt:
                    turn_c(h + 1, k + 1)
                convolve(h, k, 1)
                if prev:
                    gather(h - 1, k - 1, 3)
                convolve(h, k, 2)
                gather(h, k, 0)
                convolve(h, k, 3)
                if nxt:
                    turn_q(h + 1, k + 1)
                if prev:
                    turn_x3(h - 1, k - 1)
                gather(h, k, 1)

            over_heads(pe, body)
            router(CH - 2, CH - 2)
            gather(CH - 1, CH - 1, 2)
            gather(CH - 1, CH - 1, 3)
            turn_x3(CH - 1, CH - 1)
            router(CH - 1, CH - 1)


F = 192
FB = 96
FK = F // FB
TOKENS = NB * SL
PAIRS = TOKENS * TOP
TILES = PAIRS // P + NE - 1
HT = CH


WDS = 4


def routing_tables():
    t = {}
    t["count_e"] = np.tile(np.arange(NE, dtype=np.float32), (P, 1))
    t["count_p"] = np.tile(np.arange(P, dtype=np.float32), (P, 1))
    t["count_128"] = np.tile(np.arange(HT, dtype=np.float32) * P, (P, 1))
    p, h = np.arange(P)[:, None], np.arange(HT)[None, :]
    t["row"] = ((p % NB) * SL + h * CD + p // NB).astype(np.float32)
    t["before"] = (np.arange(P)[:, None] < np.arange(P)[None, :]).astype(np.float32)
    t["carry"] = np.tile((np.arange(NE * HT) % HT != 0).astype(np.float32), (P, 1))
    names = list(t)
    at = dict(zip(names, np.cumsum([0] + [t[n].shape[1] for n in names])))
    return np.ascontiguousarray(np.concatenate([t[n] for n in names], 1)), {n: (int(at[n]), int(at[n] + t[n].shape[1])) for n in names}


def routing_program(nc, consts, spans, down_w, keep, WD, route, psum):
    ctx = ExitStack()
    with ctx:
        def sb(name, shape, dt=F32):
            return ctx.enter_context(nc.sbuf_tensor(name, shape, dt))

        def sem(name):
            return ctx.enter_context(nc.semaphore(name))

        scores, top8, idx8 = keep
        slots, weight, listed, expert = route
        K = sb("consts", [P, consts.shape[1]])
        c = {n: K[:, lo:hi] for n, (lo, hi) in spans.items()}
        gap, ex, den = sb("gap", [P, HT]), sb("ex", [P, HT]), sb("den3", [P, HT])
        pick = sb("pick", [P, TOP, HT])
        hot = sb("hot", [P, TOP, NE, HT])
        mask, work = sb("mask", [P, NE, HT]), sb("work", [P, NE, HT])
        incl, ones = sb("incl", [P, NE, HT]), sb("ones", [P, P])
        tiles, end, start = sb("tiles", [P, NE]), sb("end", [P, NE]), sb("start", [P, NE])
        slot_f = sb("slot_f", [P, TOP, HT])
        part_i, part_f = sb("part_i", [P, 2, TOP * HT], I32), sb("part_f", [P, 2, TOP * HT])
        R, T = [sb(f"R{i}", [P, P]) for i in range(4)], [sb(f"T{i}", [P, TILES]) for i in range(4)]
        WS = [sb(f"WDS{i}", [FB, FK, D]) for i in range(WDS)]
        cmp, exp_f = sb("cmp", [P, TILES, NE]), sb("exp_f", [P, TILES])

        wd_in, wd_hi, wd_lo = [sem(f"wd_in{i}") for i in range(WDS)], sem("wd_hi"), sem("wd_lo")
        consts_in, gap_done, ex_done, step = sem("consts_in"), sem("gap_done"), sem("ex_done"), sem("step")
        masked, counted, spread, added = sem("masked"), sem("counted"), sem("spread"), sem("added")
        bank_before, bank_all, bank_list = psum[:, 0, :], psum[:, 1, :], psum[:, 2, :]

        def over(ap_tile, dims, off=0):
            return tile_ap(ap_tile, off, dims)

        block = ctx.enter_context(nc.Block())

        @block.sync
        def _(sp):
            sp.dma_start(K[:], consts.ap()).then_inc(consts_in, 16)
            for e in range(NE):
                if e >= WDS:
                    sp.wait_ge(wd_lo, e - WDS + 1)
                sp.dma_start(WS[e % WDS][:], down_w[e].rearrange("(c p) n -> p c n", p=FB)).then_inc(wd_in[e % WDS], 16)

        @block.scalar
        def _(act):
            def split(e):
                act.wait_ge(wd_in[e % WDS], 16 * (e // WDS + 1))
                act.copy(WD[0][:, e, :, :], WS[e % WDS][:]).then_inc(wd_hi, 1)

            for e in range(4):
                split(e)
            act.wait_ge(gap_done, 1)
            act.activation(ex[:], gap[:], ACT.Exp).then_inc(ex_done, 1)
            for e in range(4, NE):
                split(e)

        @block.gpsimd
        def _(pool):
            for e in range(NE):
                pool.wait_ge(wd_hi, e + 1)
                pool.tensor_tensor(WD[1][:, e, :, :], WS[e % WDS][:], WD[0][:, e, :, :], ALU.subtract).then_inc(wd_lo, 1)

        @block.vector
        def _(dve):
            n = 0

            def then(ins):
                nonlocal n
                n += 1
                ins.then_inc(step, 1)
                dve.wait_ge(step, n)

            for h in range(HT):
                dve.max(top8[:, h, :], scores[:, h, :]).then_inc(step, 1)
            n = HT
            dve.wait_ge(step, n)
            for h in range(HT):
                ins = dve.max_index(idx8[:, h, :], top8[:, h, :], scores[:, h, :])
            then(ins)
            dve.tensor_tensor(gap[:], top8[:, :, 1], top8[:, :, 0], ALU.subtract).then_inc(gap_done, 1)
            then(dve.tensor_copy(pick[:].rearrange("p c h -> p h c"), idx8[:, :, 0:TOP]))
            then(dve.memset(ones[:], 1.0))
            dve.wait_ge(consts_in, 16)
            for j in range(TOP):
                ins = dve.tensor_tensor(hot[:, j, :, :], over(K, [[1, NE], [0, HT]], spans["count_e"][0]),
                                        over(pick, [[0, NE], [1, HT]], j * HT), ALU.is_equal)
            then(ins)
            then(dve.tensor_tensor(mask[:], hot[:, 0, :, :], hot[:, 1, :, :], ALU.add))
            dve.sem_inc(masked, 1)
            dve.wait_ge(ex_done, 1)
            then(dve.tensor_scalar(den[:], ex[:], 1.0, None, ALU.add))
            then(dve.reciprocal(weight[:, 0, :], den[:]))
            then(dve.tensor_tensor(weight[:, 1, :], ex[:], weight[:, 0, :], ALU.mult))
            dve.wait_ge(counted, 1)
            flat = "p e h -> p (e h)"
            then(dve.tensor_tensor_scan(incl[:].rearrange(flat), c["carry"], bank_all, 0.0, ALU.mult, ALU.add))
            then(dve.tensor_tensor(work[:].rearrange(flat), incl[:].rearrange(flat), bank_all, ALU.subtract))
            then(dve.tensor_tensor(work[:].rearrange(flat), bank_before, work[:].rearrange(flat), ALU.add))
            then(dve.tensor_tensor(mask[:], over(incl, [[HT, NE], [0, HT]], HT - 1),
                                   over(K, [[0, NE], [1, HT]], spans["count_128"][0]), ALU.is_gt))
            then(dve.tensor_reduce(tiles[:], mask[:], AX.X, ALU.add))
            then(dve.tensor_tensor_scan(end[:], ones[:, 0:NE], tiles[:], 0.0, ALU.mult, ALU.add))
            then(dve.tensor_tensor(start[:], end[:], tiles[:], ALU.subtract))
            then(dve.scalar_tensor_tensor(work[:], over(start, [[1, NE], [0, HT]]), float(P), work[:], ALU.mult, ALU.add))
            for j in range(TOP):
                then(dve.tensor_tensor(mask[:], hot[:, j, :, :], work[:], ALU.mult))
                then(dve.tensor_reduce(slot_f[:, j, :], mask[:].rearrange("p e h -> p h e"), AX.X, ALU.add))
            then(dve.tensor_copy(slots[:], slot_f[:]))
            all_slots = slots[:].rearrange("p c h -> p (c h)")
            then(dve.tensor_scalar(part_i[:, 0, :], all_slots, 7, None, ALU.arith_shift_right))
            then(dve.tensor_scalar(part_i[:, 1, :], all_slots, P - 1, None, ALU.bitwise_and))
            then(dve.tensor_copy(part_f[:], part_i[:]))
            then(dve.tensor_tensor(cmp[:], over(end, [[0, TILES], [1, NE]]),
                                   over(K, [[1, TILES], [0, NE]], spans["count_p"][0]), ALU.is_le))
            then(dve.tensor_reduce(exp_f[:], cmp[:], AX.X, ALU.add))
            then(dve.tensor_scalar(exp_f[:], exp_f[:], float(NE - 1), None, ALU.min))
            then(dve.tensor_copy(expert[:], exp_f[:]))
            for i in range(TOP * HT):
                if i >= 4:
                    dve.wait_ge(added, i - 3)
                dve.tensor_scalar(R[i % 4][:], c["count_p"], part_f[:, 1, i:i + 1], None, ALU.is_equal)
                h = i % HT
                lo = spans["row"][0]
                dve.tensor_scalar(T[i % 4][:], c["count_p"][:, 0:TILES], part_f[:, 0, i:i + 1], K[:, lo + h:lo + h + 1],
                                  ALU.is_equal, ALU.mult).then_inc(spread, 1)
            dve.wait_ge(added, TOP * HT)
            then(dve.tensor_copy(listed[:], bank_list[:, 0:TILES]))

        @block.tensor
        def _(pe):
            pe.wait_ge(masked, 1)
            m = mask[:].rearrange("p e h -> p (e h)")
            pe.matmul(bank_before, c["before"], m, start=True, stop=True)
            pe.matmul(bank_all, ones[:], m, start=True, stop=True).then_inc(counted, 1)
            for i in range(TOP * HT):
                pe.wait_ge(spread, i + 1)
                pe.matmul(bank_list[:, 0:TILES], R[i % 4][:], T[i % 4][:], start=(i == 0), stop=(i == TOP * HT - 1)).then_inc(added, 1)


def experts_program(nc, xn3, y, WGU, WD, route, psum, ident):
    ctx = ExitStack()
    with ctx:
        def sb(name, shape, dt=F32):
            return ctx.enter_context(nc.sbuf_tensor(name, shape, dt))

        def sem(name):
            return ctx.enter_context(nc.semaphore(name))

        slots, weight, listed, expert = route
        col = [sb(f"col{i}", [P, 1], I32) for i in range(4)]
        G = [sb(f"G{i}", [P, D]) for i in range(4)]
        GH, GL = ([sb(f"G{n}{i}", [P, KD, P], F16) for i in range(2)] for n in "HL")
        SG, HM = [sb(f"SG{i}", [P, F]) for i in range(2)], [sb(f"HM{i}", [P, F]) for i in range(2)]
        HH, HL = ([sb(f"H{n}{i}", [FB, FK, P], F16) for i in range(2)] for n in "HL")
        YO = [sb(f"YO{i}", [P, D]) for i in range(2)]

        bG = [psum[:, i, :] for i in range(2)]
        bGU = [psum[:, 2 + i, :] for i in range(2)]
        bH = [psum[:, 4 + i, :] for i in range(2)]
        bY = [psum[:, 6 + i, :] for i in range(2)]

        col_done = sem("col_done")
        g_in = [sem(f"g_in{i}") for i in range(4)]
        g_turned, gt_done, gu_done, sg_done, hm_done = (sem(n) for n in ("g_turned", "gt_done", "gu_done", "sg_done", "hm_done"))
        g_hi, h_hi = sem("g_hi"), sem("h_hi")
        h_turned, ht_done, dn_done, yo_done, held = (sem(n) for n in ("h_turned", "ht_done", "dn_done", "yo_done", "held3"))
        y_out = [sem(f"y_out{i}") for i in range(2)]

        LO, HI = 4, TILES - 3
        assert (HI - LO) % 4 == 0

        def over_tiles(eng, body):
            for t in range(LO):
                body(t, t)
            with eng.Fori(0, (HI - LO) // 4) as i:
                for k in range(LO, LO + 4):
                    body(4 * i + k, k)
            for t in range(HI, TILES):
                body(t, t)

        def inner(t):
            return not isinstance(t, int)

        block = ctx.enter_context(nc.Block())

        @block.gpsimd
        def _(pool):
            def fetch(t, k):
                if inner(t) or t >= 4:
                    pool.wait_ge(g_turned, t - 3)
                    pool.sem_inc(held, 1)
                pool.tensor_copy(col[k % 4][:], listed[:, bass.ds(t, 1)]).then_inc(col_done, 1)
                pool.wait_ge(col_done, t + 1)
                pool.sem_inc(held, 1)
                pool.indirect_dma_start(G[k % 4][:], None, xn3, bass.IndirectOffsetOnAxis(ap=col[k % 4][:, 0:1], axis=0)).then_inc(g_in[k % 4], 16)

            over_tiles(pool, fetch)

        @block.sync
        def _(sp):
            def store(t, k):
                sp.wait_ge(yo_done, t + 1)
                sp.sem_inc(held, 1)
                sp.dma_start(y[bass.ds(t * P, P), :], YO[k % 2][:]).then_inc(y_out[k % 2], 16)

            over_tiles(sp, store)
            for i in range(2):
                sp.wait_ge(y_out[i], 16 * ((TILES + 1 - i) // 2))

        @block.scalar
        def _(act):
            def keep_g(t, k):
                act.wait_ge(g_turned, t + 1)
                if inner(t) or t >= 2:
                    act.wait_ge(gu_done, t - 1)
                act.copy(GH[k % 2][:].rearrange("p k n -> p (k n)"), bG[k % 2]).then_inc(g_hi, 1)

            def keep_h(t, k):
                act.wait_ge(h_turned, t + 1)
                if inner(t) or t >= 2:
                    act.wait_ge(dn_done, t - 1)
                act.copy(HH[k % 2][:].rearrange("p c n -> p (c n)"), bH[k % 2][0:FB, 0:FK * P]).then_inc(h_hi, 1)

            def silu(t, k):
                act.wait_ge(gu_done, t + 1)
                if inner(t) or t >= 2:
                    act.wait_ge(hm_done, t - 1)
                act.activation(SG[k % 2][:], bGU[k % 2][:, 0:F], ACT.Silu).then_inc(sg_done, 1)

            def keep_y(t, k):
                act.wait_ge(dn_done, t + 1)
                if inner(t) or t >= 2:
                    act.wait_ge(y_out[k % 2], 8 * (t - k % 2))
                act.copy(YO[k % 2][:], bY[k % 2]).then_inc(yo_done, 1)

            keep_g(0, 0)
            keep_g(1, 1)

            def body(t, k):
                silu(t, k)
                if inner(t) or t + 2 < TILES:
                    keep_g(t + 2, k + 2)
                keep_h(t, k)
                if inner(t) or t >= 1:
                    keep_y(t - 1, k - 1)

            over_tiles(act, body)
            keep_y(TILES - 1, TILES - 1)

        @block.vector
        def _(dve):
            def low_g(t, k):
                dve.wait_ge(g_hi, t + 1)
                dve.tensor_tensor(GL[k % 2][:].rearrange("p k n -> p (k n)"), bG[k % 2],
                                  GH[k % 2][:].rearrange("p k n -> p (k n)"), ALU.subtract).then_inc(gt_done, 1)

            def product(t, k):
                dve.wait_ge(sg_done, t + 1)
                if inner(t) or t >= 2:
                    dve.wait_ge(h_turned, t - 1)
                dve.tensor_tensor(HM[k % 2][:], bGU[k % 2][:, F:2 * F], SG[k % 2][:], ALU.mult).then_inc(hm_done, 1)

            def low_h(t, k):
                dve.wait_ge(h_hi, t + 1)
                dve.tensor_tensor(HL[k % 2][:].rearrange("p c n -> p (c n)"), bH[k % 2][0:FB, 0:FK * P],
                                  HH[k % 2][:].rearrange("p c n -> p (c n)"), ALU.subtract).then_inc(ht_done, 1)

            low_g(0, 0)
            low_g(1, 1)

            def body(t, k):
                product(t, k)
                if inner(t) or t + 2 < TILES:
                    low_g(t + 2, k + 2)
                low_h(t, k)

            over_tiles(dve, body)

        @block.tensor
        def _(pe):
            def turn_g(t, k):
                pe.wait_ge(g_in[k % 4], 4 * (t - k % 4) + 16)
                if inner(t) or t >= 2:
                    pe.wait_ge(gt_done, t - 1)
                for m in range(KD):
                    mm = pe.transpose(bG[k % 2][:, m * P:(m + 1) * P], G[k % 4][:, m * P:(m + 1) * P], ident[:])
                mm.then_inc(g_turned, 1)

            def gate_up(t, k):
                e = pe.value_load(expert[0:1, bass.ds(t, 1)], min_val=0, max_val=NE - 1)
                pe.wait_ge(gt_done, t + 1)
                if inner(t) or t >= 2:
                    pe.wait_ge(hm_done, t - 1)
                for m in range(KD):
                    for i, (g, w) in enumerate(((GH, WGU[0]), (GH, WGU[1]), (GL, WGU[0]))):
                        mm = pe.matmul(bGU[k % 2][:, 0:2 * F], g[k % 2][:, m, :], w[:, bass.ds(e * KD + m, 1), :].rearrange("p o n -> p (o n)"),
                                       start=(m == 0 and i == 0), stop=(m == KD - 1 and i == 2))
                mm.then_inc(gu_done, 1)

            def turn_h(t, k):
                pe.wait_ge(hm_done, t + 1)
                if inner(t) or t >= 2:
                    pe.wait_ge(ht_done, t - 1)
                for m in range(FK):
                    mm = pe.transpose(bH[k % 2][0:FB, m * P:(m + 1) * P], HM[k % 2][:, m * FB:(m + 1) * FB], ident[:])
                mm.then_inc(h_turned, 1)

            def down(t, k):
                e = pe.value_load(expert[0:1, bass.ds(t, 1)], min_val=0, max_val=NE - 1)
                pe.wait_ge(ht_done, t + 1)
                if inner(t) or t >= 2:
                    pe.wait_ge(yo_done, t - 1)
                for m in range(FK):
                    for i, (h, w) in enumerate(((HH, WD[0]), (HH, WD[1]), (HL, WD[0]))):
                        mm = pe.matmul(bY[k % 2], h[k % 2][:, m, :], w[:, bass.ds(e, 1), m, :].rearrange("p o n -> p (o n)"),
                                       start=(m == 0 and i == 0), stop=(m == FK - 1 and i == 2))
                mm.then_inc(dn_done, 1)

            turn_g(0, 0)
            turn_g(1, 1)

            def body(t, k):
                gate_up(t, k)
                if inner(t) or t + 2 < TILES:
                    turn_g(t + 2, k + 2)
                if inner(t) or t >= 1:
                    down(t - 1, k - 1)
                turn_h(t, k)

            over_tiles(pe, body)
            down(TILES - 1, TILES - 1)


def combine_program(nc, x2, y, out, route):
    ctx = ExitStack()
    with ctx:
        def sb(name, shape, dt=F32):
            return ctx.enter_context(nc.sbuf_tensor(name, shape, dt))

        def sem(name):
            return ctx.enter_context(nc.semaphore(name))

        slots, weight, listed, expert = route
        N = 4
        col = [sb(f"slot{i}", [P, TOP], I32) for i in range(N)]
        Y1, Y2 = [sb(f"Y1_{i}", [P, D]) for i in range(N)], [sb(f"Y2_{i}", [P, D]) for i in range(N)]
        X, O = [sb(f"X2in{i}", [P, D]) for i in range(N)], [sb(f"O{i}", [P, D]) for i in range(N)]
        w = [sb(f"w{i}", [P, TOP]) for i in range(N)]
        cols_done, w_done, first, done, held = sem("cols_done"), sem("w_done"), sem("first"), sem("done"), sem("held4")
        y_in = [sem(f"y_in{i}") for i in range(N)]
        x_in = [sem(f"x2_in{i}") for i in range(N)]
        stored = [sem(f"stored{i}") for i in range(N)]

        def over_tiles(eng, body):
            for h in range(N):
                body(h, h)
            with eng.Fori(0, HT // N - 1) as i:
                for k in range(N):
                    body(4 * i + (k + N), k)

        def inner(h):
            return not isinstance(h, int)

        def rows(t, h):
            return t[:, bass.ds(h * CD, CD), :].rearrange("b j d -> j b d")

        block = ctx.enter_context(nc.Block())

        @block.gpsimd
        def _(pool):
            def body(h, k):
                if inner(h):
                    pool.wait_ge(done, h - N + 1)
                    pool.sem_inc(held, 1)
                pool.tensor_copy(col[k][:], slots[:, :, bass.ds(h, 1)].rearrange("p c o -> p (c o)")).then_inc(cols_done, 1)
                pool.wait_ge(cols_done, h + 1)
                pool.sem_inc(held, 1)
                for j, dst in enumerate((Y1[k], Y2[k])):
                    pool.indirect_dma_start(dst[:], None, y, bass.IndirectOffsetOnAxis(ap=col[k][:, j:j + 1], axis=0)).then_inc(y_in[k], 16)

            over_tiles(pool, body)

        @block.sync
        def _(sp):
            def load(h, k):
                if inner(h):
                    sp.wait_ge(done, h - N + 1)
                    sp.sem_inc(held, 1)
                sp.dma_start(X[k][:], rows(x2, h)).then_inc(x_in[k], 16)

            over_tiles(sp, load)

        @block.scalar
        def _(act):
            def store(h, k):
                act.wait_ge(done, h + 1)
                act.sem_inc(held, 1)
                act.dma_start(rows(out, h), O[k][:]).then_inc(stored[k], 16)

            over_tiles(act, store)
            for k in range(N):
                act.wait_ge(stored[k], 16 * HT // N)

        @block.vector
        def _(dve):
            def body(h, k):
                if inner(h):
                    dve.wait_ge(stored[k], 4 * (h - k))
                dve.tensor_copy(w[k][:], weight[:, :, bass.ds(h, 1)].rearrange("p c o -> p (c o)")).then_inc(w_done, 1)
                dve.wait_ge(w_done, h + 1)
                dve.wait_ge(x_in[k], 4 * (h - k) + 16)
                dve.wait_ge(y_in[k], 8 * (h - k) + 32)
                dve.scalar_tensor_tensor(O[k][:], Y1[k][:], w[k][:, 0:1], X[k][:], ALU.mult, ALU.add).then_inc(first, 1)
                dve.wait_ge(first, h + 1)
                dve.scalar_tensor_tensor(O[k][:], Y2[k][:], w[k][:, 1:2], O[k][:], ALU.mult, ALU.add).then_inc(done, 1)

            over_tiles(dve, body)


def program(nc, a, out):
    with ExitStack() as ctx:
        def sb(name, shape, dt=F32):
            return ctx.enter_context(nc.sbuf_tensor(name, shape, dt))

        psum = ctx.enter_context(nc.psum_tensor("psum", [P, 8, 512], F32))
        banks = [psum[:, i, :] for i in range(8)]
        ident, tab, sel = sb("ident", [P, P]), sb("rot_tab", [P, SL]), sb("rot_sel", [P, P])
        m_half = sb("m_half", [P, 1])
        keep = (sb("scores", [P, CH, NE]), sb("top8", [P, CH, 8]), sb("idx8", [P, CH, 8], U32))
        x1 = nc.dram_tensor("x1", [NB, SL, D], F32).ap()
        x2 = nc.dram_tensor("x2", [NB, SL, D], F32).ap()
        xn3 = nc.dram_tensor("xn3", [NB, SL, D], F32).ap()
        kpad = [nc.dram_tensor(f"kpad_{n}", [CH, TAPS], F16) for n in ("hi", "lo")]
        pick = np.zeros((P, P), np.float32)
        for r in range(ROT):
            pick[r, r] = pick[SWAP + r, r] = 1.0
        w = {n[8:]: v for n, v in a.items() if n.startswith("L0_attn_")}
        w["tab"] = nc.inline_tensor(rotary_table(), name="c_tab").ap()
        w["sel"] = nc.inline_tensor(pick, name="c_sel").ap()
        with ExitStack() as inner:
            def wsb(name, shape):
                return inner.enter_context(nc.sbuf_tensor(name, shape, F32))
            sbw = {"qT_w": wsb("qT_w", [P, KD, D]), "dkvT": wsb("dkvT", [P, KD, P]), "kT_w": wsb("kT_w", [P, D]),
                   "vT_w": wsb("vT_w", [P, D]), "woT": wsb("woT", [P, KD, D]), "xqT_f": wsb("xqT_f", [P, KD, P]),
                   "xkT": wsb("xkT", [P, P]), "b_q": wsb("b_q", [P, KD]), "b_k": wsb("b_k", [P, KD]),
                   "b_xq": wsb("b_xq", [P, 1]), "b_xk": wsb("b_xk", [P, 1]), "b_dkv": wsb("b_dkv", [P, 1]),
                   "b_o": wsb("b_o", [P, D]), "m_half": m_half}
            setup_program(nc, w, sbw, banks, tab, sel, ident)
            attention_program(nc, a["x"], x1, sbw, banks, tab, sel, ident)
        WGU = [sb(f"WGU{n}", [P, NE * KD, 2 * F], F16) for n in "HL"]
        convolution_program(nc, x1, a["ctx_2048"], a["L0_xattn_ssm_kernel"], a["L0_xattn_D"], a["L0_ffn_router_w"],
                            x2, xn3, kpad, keep, psum, ident, m_half, a["L0_ffn_gate_w"], a["L0_ffn_up_w"], WGU)
        WD = [sb(f"WD{n}", [FB, NE, FK, D], F16) for n in "HL"]
        route = (sb("slots", [P, TOP, HT], I32), sb("weight", [P, TOP, HT]), sb("listed", [P, TILES], I32), sb("expert", [P, TILES], I32))
        table, spans = routing_tables()
        y = nc.dram_tensor("y", [TILES * P, D], F32).ap()
        routing_program(nc, nc.inline_tensor(table, name="c_route"), spans, a["L0_ffn_down_w"], keep, WD, route, psum)
        experts_program(nc, xn3.rearrange("b t d -> (b t) d"), y, WGU, WD, route, psum, ident)
        combine_program(nc, x2, y, out, route)


STAGE = 3

_INS = ['x', 'ctx_2048', 'L0_attn_w_down_q', 'L0_attn_b_down_q', 'L0_attn_w_up_q', 'L0_attn_b_up_q', 'L0_attn_w_down_kv',
        'L0_attn_b_down_kv', 'L0_attn_w_up_k', 'L0_attn_b_up_k', 'L0_attn_w_up_v', 'L0_attn_b_up_v', 'L0_attn_wq_r',
        'L0_attn_bq_r', 'L0_attn_wk_r', 'L0_attn_bk_r', 'L0_attn_wo', 'L0_attn_bo', 'L0_xattn_ssm_kernel', 'L0_xattn_D',
        'L0_ffn_router_w', 'L0_ffn_gate_w', 'L0_ffn_up_w', 'L0_ffn_down_w']


def kernel(**inputs):
    import numpy as _np
    import concourse.bacc as _bacc
    from concourse import mybir as _mybir
    from concourse.bass_utils import run_bass_kernel_spmd as _run

    nc = _bacc.Bacc("TRN2", target_bir_lowering=False, num_devices=1)
    arrays, args = {}, {}
    for name in _INS:
        a = _np.ascontiguousarray(inputs[name])
        arrays[f"in_{name}_dram"] = a
        args[name] = nc.dram_tensor(f"in_{name}_dram", a.shape, _mybir.dt.from_np(a.dtype), kind="ExternalInput").ap()
    out = nc.dram_tensor("out_0_dram", (16, 256, 512), _mybir.dt.float32, kind="ExternalOutput").ap()
    program(nc, args, out)
    r = _run(nc, [arrays], core_ids=[0])
    return r.results[0]["out_0_dram"]
```

```python
from contextlib import ExitStack

import numpy as np

import concourse.bass as bass
from concourse import mybir

F32 = mybir.dt.float32
F16 = mybir.dt.float16
I32 = mybir.dt.int32
U32 = mybir.dt.uint32
ALU = mybir.AluOpType
ACT = mybir.ActivationFunctionType
AX = mybir.AxisListType

P = 128
NB, SL, D = 16, 256, 512
NT = SL // P
KD = D // P
DQ, DKV = 384, 128
NH, HD = 16, 32
KQ = DQ // P
ROT = 10
EPS = 1e-5
SCALE = float(1.0 / np.sqrt(HD))
SWAP = 64
UNITS = 2 * NH // 2
QUAD = 32
CH = 32
TAPS = P + D
PASSES = ((0, 0), (0, 1), (1, 0))


def rotary_table():
    exps = np.arange(0, D, 2)
    tn = np.array([np.float32(1.0) / (np.float32(10000.0 ** e) / np.float32(D)) if e < ROT else 0.0 for e in exps], np.float32)
    ang = np.outer(np.arange(SL, dtype=np.float32), tn).astype(np.float32).astype(np.float64)
    tab = np.zeros((P, SL), np.float32)
    for r in range(ROT):
        a = ang[:, r // 2]
        tab[r] = np.cos(a) - 1.0
        tab[SWAP + r] = np.sin(a) if r % 2 else -np.sin(a)
    return tab


def setup_program(nc, w, taps, skip, kpad, sbw, parts, psum, tab, sel, ident):
    ctx = ExitStack()
    with ctx:
        def sb(name, shape, dt=F32):
            return ctx.enter_context(nc.sbuf_tensor(name, shape, dt))

        def sem(name):
            return ctx.enter_context(nc.semaphore(name))

        upq, rq = sb("upq", [P, KD, DQ]), sb("rq", [P, KD, DQ])
        upk, rk = sb("upk", [P, KD, DKV]), sb("rk", [P, KD, DKV])
        upv, wo = sb("upv", [P, KD, DKV]), sb("wo_nat", [P, KD, D])
        dq, dkv = sb("dq", [P, KQ, D]), sb("dkv", [P, D])
        xq, xk = sb("xq", [P, DQ]), sb("xk", [P, DKV])
        sqT, xqT = sb("sqT", [P, KQ, D]), sb("xqT", [P, KQ, P])
        b_up, b_r, b_dq = sb("b_up", [P, 2, KD]), sb("b_r", [P, 2, KD]), sb("b_dq", [P, KQ])
        b_x, b_v, bv_rep = sb("b_x", [P, 2]), sb("b_v", [P, KD]), sb("bv_rep", [P, KD, P])

        KP, DW = sb("KP", [CH, TAPS]), sb("DW", [CH, 1])
        KPH, KPL = sb("KPH", [CH, TAPS], F16), sb("KPL", [CH, TAPS], F16)
        k_in, k_padded, k_set, k_hi, k_out = sem("k_in"), sem("k_padded"), sem("k_set"), sem("kp_hi"), sem("k_out")
        zeroed, ident_at = sem("zeroed"), sem("ident_at")
        loaded, summed = sem("loaded"), sem("summed")
        turned, kept = sem("turned"), sem("kept")
        tables, rot_in, w_hi = sem("tables"), sem("rot_in"), sem("w_hi1")

        blk = "(o p) i -> p o i"
        block = ctx.enter_context(nc.Block())
        flat, whole = (lambda t: t[:, :, :].rearrange("p c n -> p (c n)")), (lambda t: t[:, :])

        def block_of(k):
            return lambda t: t[:, k, :]

        groups = []
        for c in range(KQ):
            groups.append(("T", [upq[:, o, c * P:(c + 1) * P] for o in range(KD)], None, sqT[:, c, :], 1.0))
        groups.append(("T", [xq[:, c * P:(c + 1) * P] for c in range(KQ)], None, flat(xqT), 1.0))
        groups.append(("T", [dkv[:, k * P:(k + 1) * P] for k in range(KD)], "dkvT", flat, 1.0))
        groups.append(("T", [upk[:, o, :] for o in range(KD)], "kT_w", whole, 1.0))
        groups.append(("T", [upv[:, o, :] for o in range(KD)], "vT_w", whole, 1.0))
        groups.append(("T", [xk[:, :]], "xkT", whole, 1.0))
        for k in range(KD):
            groups.append(("T", [wo[:, o, k * P:(k + 1) * P] for o in range(KD)], "woT", block_of(k), 1.0))
        for i in range(KD):
            groups.append(("fold", i, "qT_w", block_of(i), SCALE))
        groups.append(("fold_rot", None, "xqT_f", flat, SCALE))
        groups.append(("bias_q", None, None, None, None))
        groups.append(("bias_o", None, None, None, None))
        split = [(g, name, view) for g, (_, _, name, view, _) in enumerate(groups) if name]
        G = len(groups)
        loads = 0

        @block.sync
        def _(sp):
            nonlocal loads
            with nc.allow_non_contiguous_dma(reason="a column, once"):
                sp.dma_start(DW[:], skip.rearrange("(p o) -> p o", o=1)).then_inc(k_in, 16)
            sp.wait_ge(k_padded, 1)
            sp.dma_start(KP[:, P:TAPS], taps).then_inc(k_in, 16)
            sp.dma_start(tab[:], w["tab"]).then_inc(tables, 16)
            sp.dma_start(sel[:], w["sel"]).then_inc(tables, 16)
            for dst, src in ((upq[:], w["w_up_q"].rearrange(blk, p=P)), (rq[:], w["wq_r"].rearrange(blk, p=P)),
                             (upk[:], w["w_up_k"].rearrange(blk, p=P)), (rk[:], w["wk_r"].rearrange(blk, p=P)),
                             (upv[:], w["w_up_v"].rearrange(blk, p=P)), (wo[:], w["wo"].rearrange(blk, p=P)),
                             (dq[:], w["w_down_q"].rearrange("(c p) i -> p c i", p=P)), (dkv[:], w["w_down_kv"])):
                sp.dma_start(dst, src).then_inc(loaded, 16)
                loads += 1
            for dst, src in ((b_up[:, 0, :], "b_up_q"), (b_up[:, 1, :], "b_up_k"), (b_r[:, 0, :], "bq_r"),
                             (b_r[:, 1, :], "bk_r"), (b_dq[:], "b_down_q"), (b_v[:], "b_up_v")):
                with nc.allow_non_contiguous_dma(reason="a bias, once"):
                    sp.dma_start(dst, w[src].rearrange("(o p) -> p o", p=P)).then_inc(loaded, 16)
                loads += 1
            sp.dma_start(sbw["b_dkv"][:], w["b_down_kv"].rearrange("(p o) -> p o", o=1)).then_inc(loaded, 16)
            sp.dma_start(sbw["b_o"][:], bass.AP(w["bo"].tensor, 0, [[0, P], [1, D]])).then_inc(loaded, 16)
            loads += 2
            sp.wait_ge(zeroed, 3)
            for dst, src, n in ((xq, w["wq_r"], DQ), (xk, w["wk_r"], DKV)):
                sp.dma_start(dst[0:ROT, :], src[0:ROT, :]).then_inc(rot_in, 16)
                for odd in range(2):
                    sp.dma_start(dst[SWAP + odd:SWAP + ROT:2, :], src[1 - odd:ROT:2, :]).then_inc(rot_in, 16)
            for col, name in enumerate(("bq_r", "bk_r")):
                v = w[name].rearrange("(p o) -> p o", o=1)
                sp.dma_start(b_x[0:ROT, col:col + 1], v[0:ROT, :]).then_inc(rot_in, 16)
                for odd in range(2):
                    with nc.allow_non_contiguous_dma(reason="a bias, once"):
                        sp.dma_start(b_x[SWAP + odd:SWAP + ROT:2, col:col + 1], v[1 - odd:ROT:2, :]).then_inc(rot_in, 16)

            sp.wait_ge(k_hi, 1)
            sp.dma_start(kpad[0].ap(), KPH[:]).then_inc(k_out, 16)
            sp.wait_ge(k_set, 2)
            sp.dma_start(kpad[1].ap(), KPL[:]).then_inc(k_out, 16)
            sp.wait_ge(k_out, 32)

        ROT_LOADS = 12

        @block.gpsimd
        def _(pool):
            pool.memset(ident[:], 0.0).then_inc(ident_at, 1)
            pool.wait_ge(ident_at, 1)
            pool.affine_select(out=ident[:], in_=ident[:], compare_op=ALU.not_equal, fill=1.0, base=0,
                               pattern=[[-1, P]], channel_multiplier=1).then_inc(ident_at, 1)

        @block.vector
        def _(dve):
            def low(i):
                _, name, view = split[i]
                hi, lo = parts[name]
                dve.wait_ge(w_hi, i + 1)
                dve.tensor_tensor(view(lo), view(sbw[name]), view(hi), ALU.subtract)

            dve.memset(KP[:], 0.0).then_inc(k_padded, 1)
            dve.memset(xq[:], 0.0).then_inc(zeroed, 1)
            dve.memset(xk[:], 0.0).then_inc(zeroed, 1)
            dve.memset(b_x[:], 0.0).then_inc(zeroed, 1)
            dve.wait_ge(k_in, 32)
            dve.tensor_tensor(KP[:, P:P + 1], KP[:, P:P + 1], DW[:], ALU.add).then_inc(k_set, 1)
            dve.wait_ge(k_set, 1)
            dve.tensor_copy(KPH[:], KP[:]).then_inc(k_hi, 1)
            dve.wait_ge(k_hi, 1)
            dve.tensor_tensor(KPL[:], KP[:], KPH[:], ALU.subtract).then_inc(k_set, 1)
            dve.wait_ge(loaded, 16 * loads)
            dve.wait_ge(rot_in, 16 * ROT_LOADS)
            dve.tensor_tensor(upq[:], upq[:], rq[:], ALU.add).then_inc(summed, 1)
            dve.tensor_tensor(upk[:], upk[:], rk[:], ALU.add).then_inc(summed, 1)
            dve.tensor_tensor(b_up[:], b_up[:], b_r[:], ALU.add).then_inc(summed, 1)
            dve.memset(bv_rep[:], 1.0).then_inc(summed, 1)
            dve.wait_ge(summed, 4)
            for k in range(KD):
                dve.tensor_scalar(bv_rep[:, k, :], bv_rep[:, k, :], b_v[:, k:k + 1], None, ALU.mult).then_inc(summed, 1)
            lows = 0
            for g, (kind, arg, name, view, scale) in enumerate(groups):
                bank = psum[g % 8]
                if lows < len(split) and split[lows][0] <= g - 2:
                    low(lows)
                    lows += 1
                dve.wait_ge(turned, g + 1)
                if kind == "bias_q":
                    dve.scalar_tensor_tensor(sbw["b_q"][:], bank[:, 0:KD], 1.0, b_up[:, 0, :], ALU.mult, ALU.add).then_inc(kept, 1)
                    dve.scalar_tensor_tensor(sbw["b_xq"][:], bank[:, KD:KD + 1], 1.0, b_x[:, 0:1], ALU.mult, ALU.add).then_inc(summed, 1)
                    dve.wait_ge(kept, g + 1)
                    dve.wait_ge(summed, 5 + KD)
                    dve.tensor_scalar(sbw["b_q"][:], sbw["b_q"][:], SCALE, None, ALU.mult).then_inc(summed, 1)
                    dve.tensor_scalar(sbw["b_xq"][:], sbw["b_xq"][:], SCALE, None, ALU.mult).then_inc(summed, 1)
                    dve.tensor_copy(sbw["b_k"][:], b_up[:, 1, :]).then_inc(summed, 1)
                    dve.tensor_copy(sbw["b_xk"][:], b_x[:, 1:2]).then_inc(summed, 1)
                elif kind == "bias_o":
                    dve.tensor_tensor(sbw["b_o"][:], bank[:, :], sbw["b_o"][:], ALU.add).then_inc(kept, 1)
                else:
                    n = P * len(arg) if kind == "T" else D
                    dst = view(sbw[name]) if name else view
                    dve.tensor_scalar(dst, bank[:, 0:n], scale, None, ALU.mult).then_inc(kept, 1)

            for i in range(lows, len(split)):
                low(i)

        @block.tensor
        def _(pe):
            pe.wait_ge(ident_at, 2)
            pe.wait_ge(summed, 4 + KD)
            for g, (kind, arg, _, _, _) in enumerate(groups):
                bank = psum[g % 8]
                if g >= 8:
                    pe.wait_ge(kept, g - 7)
                if kind == "T":
                    for j, src in enumerate(arg):
                        mm = pe.transpose(bank[:, j * P:(j + 1) * P], src, ident[:])
                elif kind == "fold":
                    pe.wait_ge(kept, KQ)
                    for c in range(KQ):
                        mm = pe.matmul(bank[:, :], dq[:, c, arg * P:(arg + 1) * P], sqT[:, c, :],
                                       start=(c == 0), stop=(c == KQ - 1))
                elif kind == "fold_rot":
                    for i in range(KD):
                        for c in range(KQ):
                            mm = pe.matmul(bank[:, i * P:(i + 1) * P], dq[:, c, i * P:(i + 1) * P], xqT[:, c, :],
                                           start=(c == 0), stop=(c == KQ - 1))
                elif kind == "bias_q":
                    for o in range(KD + 1):
                        for c in range(KQ):
                            lhs = sqT[:, c, o * P:(o + 1) * P] if o < KD else xqT[:, c, :]
                            mm = pe.matmul(bank[:, o:o + 1], lhs, b_dq[:, c:c + 1], start=(c == 0), stop=(c == KQ - 1))
                else:
                    pe.wait_ge(kept, KQ + 5 + KD)
                    for k in range(KD):
                        mm = pe.matmul(bank[:, :], bv_rep[:, k, :], sbw["woT"][:, k, :], start=(k == 0), stop=(k == KD - 1))
                mm.then_inc(turned, 1)

        @block.scalar
        def _(act):
            for g, name, view in split:
                act.wait_ge(kept, g + 1)
                act.copy(view(parts[name][0]), view(sbw[name])).then_inc(w_hi, 1)
            act.wait_ge(tables, 32)


def attention_program(nc, x, x1, sbw, parts, psum, tab, sel, ident):
    ctx = ExitStack()
    with ctx:
        def sb(name, shape, dt=F32):
            return ctx.enter_context(nc.sbuf_tensor(name, shape, dt))

        def sem(name):
            return ctx.enter_context(nc.semaphore(name))

        X = [sb(f"X{s}", [P, NT, D]) for s in range(2)]
        XB = [sb(f"XB{s}", [P, NT, D]) for s in range(2)]
        XN = sb("XN", [P, NT, D])
        stats, mv, vare, rstd = sb("stats", [P, 6]), sb("mv", [P, 2]), sb("vare", [P, 1]), sb("rstd", [P, 1])
        XT = [sb(f"XT{n}", [P, KD, SL], F16) for n in "HL"]
        CK = [sb(f"CK{n}", [P, SL], F16) for n in "HL"]
        RQ, RK = sb("RQ", [P, SL]), sb("RK", [P, SL])
        QH, QL = sb("QH", [P, KD, SL], F16), sb("QL", [P, KD, SL], F16)
        KH, KL = sb("KH", [P, KD, SL], F16), sb("KL", [P, KD, SL], F16)
        QS = [sb(f"QS{s}", [P, 4, KD, SL], F16) for s in range(2)]
        KS = [sb(f"KS{s}", [P, 4, KD, SL], F16) for s in range(2)]
        V = [sb(f"V{s}", [P, NT, D]) for s in range(2)]
        PR = [sb(f"PR{i}", [P, 2, SL]) for i in range(4)]
        PT = [sb(f"PT{i}", [P, 4, P]) for i in range(2)]
        ATH, ATL = ([sb(f"AT{n}{s}", [P, KD, SL], F16) for s in range(2)] for n in "HL")
        X1 = [sb(f"X1_{s}", [P, NT, D]) for s in range(2)]
        nmax = sb("nmax", [P, 4, 2])
        den, rden = sb("den", [P, 4, 2]), sb("rden", [P, 4, 2])

        bT, bAV, bA, bB = psum[0], psum[1], psum[2], psum[3]
        bS, bP = psum[4:6], psum[6:8]

        x_in = [sem(f"x_in{s}") for s in range(2)]
        xn_done, chain = sem("xn_done"), sem("chain")
        rstd_done, half_set = sem("rstd_done"), sem("half_set")
        may_aggr = sem("may_aggr")
        turned, xt_hi, xt_done = sem("xT_turned"), sem("xt_hi"), sem("xt_done")
        ck_hi, at_hi = sem("ck_hi"), sem("at_hi")
        front, ctr_done, rk_done = sem("front"), sem("ctr_done"), sem("rk_done")
        q_hi, q_lo, k_hi, k_lo, v_done = sem("q_hi"), sem("q_lo"), sem("k_hi"), sem("k_lo"), sem("v_done")
        qs_in = [sem(f"qs_in{s}") for s in range(2)]
        ks_in = [sem(f"ks_in{s}") for s in range(2)]
        s_done, max_done, exp_done, rd_done, pn_done = (sem(n) for n in ("s_done", "max_done", "exp_done", "rd_done", "pn_done"))
        t_done, pte_v, pte_a, pv_done, at_done = (sem(n) for n in ("t_done", "pte_v", "pte_a", "pv_done", "at_done"))
        out_done, xb_done, x1_done = sem("out_done"), sem("xb_done"), sem("x1_done")
        x1_out = [sem(f"x1_out{s}") for s in range(2)]

        BANK = [bT, bA, bA, bB, bA, bB, bT, bB, bA, bT]
        PE_STEP = {0: [(2, 0)], 1: [(2, 1)], 2: [(3, 0)], 3: [(3, 1)], 4: [(4, 0)], 5: [(4, 1)],
                   6: [(5, None)], 7: [(6, None)], 8: [(7, None)], 9: [(8, None)], 10: [(9, None)]}
        ACT_STEP = {2: 2, 4: 3, 7: 4, 8: 6, 9: 7, 10: 8, 11: 9}
        DVE_STEP = {3: 2, 5: 3, 7: 5, 8: 4, 9: 6, 10: 7}

        def unit(u):
            return (u // 2) % 2, 2 * (2 * (u // 4) + u % 2), u // 4

        def over_sequences(eng, body):
            body(0, 0, True, False)
            body(1, 1, False, False)
            with eng.Fori(2, NB - 2, 2) as b:
                body(b, 0, False, False)
                body(b + 1, 1, False, False)
            body(NB - 2, 0, False, False)
            body(NB - 1, 1, False, True)

        def before_last(b):
            return isinstance(b, int) and b + 2 >= NB

        block = ctx.enter_context(nc.Block())

        @block.sync
        def _(sp):
            def load(b, s):
                sp.dma_start(X[s][:], x[b].rearrange("(t p) d -> p t d", p=P)).then_inc(x_in[s], 16)

            def stack(b, s):
                if not isinstance(b, int) or b >= 2:
                    sp.wait_ge(s_done, UNITS * (b - 1))
                for hi, lo, dst, parts, ready, into in ((QH, QL, QS[s], "hhl", q_lo, qs_in[s]), (KH, KL, KS[s], "hlh", k_lo, ks_in[s])):
                    sp.wait_ge(ready, 2 * b + 2)
                    for part, which in enumerate(parts):
                        src = hi if which == "h" else lo
                        for hq in range(4):
                            sp.dma_start(dst[QUAD * part:QUAD * (part + 1), hq, :, :],
                                         src[QUAD * hq:QUAD * (hq + 1), :, :]).then_inc(into, 16)

            def store(b, s):
                for t in range(NT):
                    sp.wait_ge(x1_done, 2 * b + t + 1)
                    sp.dma_start(x1[b][t * P:(t + 1) * P, :], X1[s][:, t, :]).then_inc(x1_out[s], 16)

            def refill(b, s):
                sp.wait_ge(xn_done, 2 * b - 2)
                sp.wait_ge(xb_done, 2 * b - 2)
                load(b, s)

            load(0, 0)
            load(1, 1)
            stack(0, 0)
            refill(2, 0)

            def body(b, s, first, last, more=True):
                if not last:
                    stack(b + 1, 1 - s)
                if not first:
                    store(b - 1, 1 - s)
                if more:
                    refill(b + 3, 1 - s)

            body(0, 0, True, False)
            body(1, 1, False, False)
            with sp.Fori(2, NB - 4, 2) as b:
                body(b, 0, False, False)
                body(b + 1, 1, False, False)
            body(NB - 4, 0, False, False)
            body(NB - 3, 1, False, False, False)
            body(NB - 2, 0, False, False, False)
            body(NB - 1, 1, False, True, False)
            store(NB - 1, 1)
            sp.wait_ge(x1_out[0], 16 * NB)
            sp.wait_ge(x1_out[1], 16 * NB)

        @block.gpsimd
        def _(pool):
            def norm(b, u):
                pool.wait_ge(rd_done, UNITS * b + u + 1)
                scale = rden[:, u % 4, :].rearrange("p (j o) -> p j o", o=1).to_broadcast([P, 2, SL])
                pool.tensor_tensor(PR[u % 4][:, :, :], PR[u % 4][:, :, :], scale, ALU.mult).then_inc(pn_done, 1)

            def residual(b, s, t):
                if t == 0:
                    pool.wait_ge(x_in[s], 8 * (b + 2 - s))
                if not isinstance(b, int) or b >= 2:
                    pool.wait_ge(x1_done, 2 * b - 3 + t)
                pool.tensor_tensor(XB[s][:, t, :], X[s][:, t, :], sbw["b_o"][:], ALU.add).then_inc(xb_done, 1)

            def root(b, t):
                pool.wait_ge(chain, 3 * (2 * b + t + 1))
                pool.tensor_tensor(rstd[:], vare[:], sbw["m_half"][:], ALU.pow).then_inc(rstd_done, 1)

            pool.memset(sbw["m_half"][:], -0.5).then_inc(half_set, 1)
            pool.wait_ge(half_set, 1)
            for b in range(2):
                for t in range(NT):
                    root(b, t)
            residual(0, 0, 0)
            residual(0, 0, 1)

            def body(b, s, first, last):
                for u in range(UNITS):
                    if u >= 1:
                        norm(b, u - 1)
                    elif not first:
                        norm(b - 1, UNITS - 1)
                    if u in (4, 12) and not before_last(b):
                        root(b + 2, u // 8)
                    if u in (14, 15) and not last:
                        residual(b + 1, 1 - s, u - 14)

            over_sequences(pool, body)
            norm(NB - 1, UNITS - 1)

        @block.scalar
        def _(act):
            def piece(b, s, k):
                if k < 2:
                    act.wait_ge(turned, 2 * b + k + 1)
                    if k == 0 and (not isinstance(b, int) or b >= 1):
                        act.wait_ge(front, 8 * b)
                    bank = bT if k == 0 else bA
                    act.copy(XT[0][:, :, k * P:(k + 1) * P], bank[:, :].rearrange("p (k n) -> p k n", k=KD)).then_inc(xt_hi, 1)
                elif k == 2:
                    act.wait_ge(front, 8 * b + 1)
                    act.activation(CK[0][:], bA[:, 0:SL], ACT.Identity, bias=sbw["b_dkv"][:, 0:1]).then_inc(ck_hi, 1)
                elif k in (3, 4, 6, 7):
                    dst, bias, hi, into = (QH, "b_q", q_hi, qs_in) if k < 5 else (KH, "b_k", k_hi, ks_in)
                    m0 = 2 if k in (3, 6) else 0
                    act.wait_ge(front, 8 * b + k - 1)
                    if m0 and (not isinstance(b, int) or b >= 1):
                        act.wait_ge(into[1 - s], 96 * (b + s))
                    for j in range(2):
                        ins = act.activation(dst[:, m0 + j, :], BANK[k][:, j * SL:(j + 1) * SL], ACT.Identity,
                                             bias=sbw[bias][:, m0 + j:m0 + j + 1])
                    ins.then_inc(hi, 1)
                elif k in (8, 9):
                    act.wait_ge(front, 8 * b + k - 1)
                    if k == 8 and (not isinstance(b, int) or b >= 2):
                        act.wait_ge(pv_done, UNITS * (b - 1))
                    act.copy(V[s][:, k - 8, :], BANK[k][:, :]).then_inc(v_done, 1)

            def keep_at(b, s, m):
                act.wait_ge(pv_done, UNITS * b + 4 * m + 4)
                if m == 0 and (not isinstance(b, int) or b >= 2):
                    act.wait_ge(out_done, 2 * b - 2)
                act.copy(ATH[s][:, m, :], bAV[:, 0:SL]).then_inc(at_hi, 1)

            def exps(b, u):
                act.wait_ge(max_done, UNITS * b + u + 1)
                if not isinstance(b, int) or UNITS * b + u >= 4:
                    act.wait_ge(t_done, UNITS * b + u - 3)
                for j in range(2):
                    ins = act.activation(PR[u % 4][:, j, :], bS[u % 2][:, j * SL:(j + 1) * SL], ACT.Exp,
                                         bias=nmax[:, u % 4, j:j + 1], accum_out=den[:, u % 4, j:j + 1])
                ins.then_inc(exp_done, 1)

            def keep_pt(b, u):
                act.wait_ge(t_done, UNITS * b + u + 1)
                if not isinstance(b, int) or UNITS * b + u >= 2:
                    act.wait_ge(pv_done, UNITS * b + u - 1)
                act.copy(PT[1][:, :, :].rearrange("p k n -> p (k n)"), bP[1][:, :]).then_inc(pte_a, 1)

            for k in range(10):
                piece(0, 0, k)
            for k in range(2):
                piece(1, 1, k)

            def body(b, s, first, last):
                for u in range(UNITS):
                    if u % 2 == 0:
                        if u >= 4:
                            keep_pt(b, u - 3)
                        elif not first:
                            keep_pt(b - 1, UNITS + u - 3)
                    if u % 4 == 3:
                        if u >= 4:
                            keep_at(b, s, u // 4 - 1)
                        elif not first:
                            keep_at(b - 1, 1 - s, KD - 1)
                    if u == UNITS - 1 and not before_last(b):
                        piece(b + 2, s, 0)
                    exps(b, u)
                    if u in ACT_STEP and not last:
                        piece(b + 1, 1 - s, ACT_STEP[u])
                    if u == UNITS - 1 and not before_last(b):
                        piece(b + 2, s, 1)

            over_sequences(act, body)
            keep_pt(NB - 1, UNITS - 3)
            keep_pt(NB - 1, UNITS - 1)
            keep_at(NB - 1, 1, KD - 1)

        @block.vector
        def _(dve):
            def statistics(b, s, t):
                if t == 0:
                    dve.wait_ge(x_in[s], 8 * (b + 2 - s))
                base = 3 * (2 * b + t)
                dve.bn_stats(stats[:], X[s][:, t, :]).then_inc(chain, 1)
                dve.wait_ge(chain, base + 1)
                dve.sem_inc(may_aggr, 1)
                dve.bn_aggr(mv[:], stats[:]).then_inc(chain, 1)
                dve.wait_ge(chain, base + 2)
                dve.tensor_scalar(vare[:], mv[:, 1:2], EPS, None, ALU.add).then_inc(chain, 1)

            def normalise(b, s, t):
                dve.wait_ge(rstd_done, 2 * b + t + 1)
                if not isinstance(b, int) or b >= 1:
                    dve.wait_ge(turned, 2 * b - 1 + t)
                dve.tensor_scalar(XN[:, t, :], X[s][:, t, :], mv[:, 0:1], rstd[:, 0:1], ALU.subtract, ALU.mult).then_inc(xn_done, 1)

            def piece(b, s, k):
                if k < 2:
                    dve.wait_ge(xt_hi, 2 * b + k + 1)
                    dst = (slice(None), slice(None), slice(k * P, (k + 1) * P))
                    dve.tensor_tensor(XT[1][dst], (bT if k == 0 else bA)[:, :].rearrange("p (k n) -> p k n", k=KD), XT[0][dst],
                                      ALU.subtract).then_inc(xt_done, 1)
                    return
                dve.wait_ge(front, 8 * b + k - 1)
                if k == 2:
                    dve.wait_ge(ck_hi, b + 1)
                    dve.scalar_tensor_tensor(CK[1][:], bA[:, 0:SL], sbw["b_dkv"][:, 0:1], CK[0][:], ALU.add, ALU.subtract)
                    dve.scalar_tensor_tensor(RQ[:], bA[:, SL:2 * SL], sbw["b_xq"][:, 0:1], tab[:], ALU.add, ALU.mult).then_inc(ctr_done, 1)
                elif k == 5:
                    dve.scalar_tensor_tensor(RK[:], bB[:, 0:SL], sbw["b_xk"][:, 0:1], tab[:], ALU.add, ALU.mult).then_inc(rk_done, 1)
                else:
                    hi, lo, bias, hi_done, lo_done, into = (QH, QL, "b_q", q_hi, q_lo, qs_in) if k < 5 else (KH, KL, "b_k", k_hi, k_lo, ks_in)
                    m0 = 2 if k in (3, 6) else 0
                    dve.wait_ge(hi_done, 2 * b + (1 if m0 else 2))
                    if m0 and (not isinstance(b, int) or b >= 1):
                        dve.wait_ge(into[1 - s], 96 * (b + s))
                    bank = BANK[k]
                    for j in range(2):
                        ins = dve.scalar_tensor_tensor(lo[:, m0 + j, :], bank[:, j * SL:(j + 1) * SL],
                                                       sbw[bias][:, m0 + j:m0 + j + 1], hi[:, m0 + j, :], ALU.add, ALU.subtract)
                    ins.then_inc(lo_done, 1)

            def maxima(b, u):
                dve.wait_ge(s_done, UNITS * b + u + 1)
                dve.tensor_reduce(nmax[:, u % 4, :], bS[u % 2][:, :].rearrange("p (j n) -> p j n", j=2), AX.X, ALU.max,
                                  negate=True).then_inc(max_done, 1)

            def recip(b, u):
                dve.wait_ge(exp_done, UNITS * b + u + 1)
                dve.reciprocal(rden[:, u % 4, :], den[:, u % 4, :]).then_inc(rd_done, 1)

            def keep_pt(b, u):
                dve.wait_ge(t_done, UNITS * b + u + 1)
                if not isinstance(b, int) or UNITS * b + u >= 2:
                    dve.wait_ge(pv_done, UNITS * b + u - 1)
                dve.tensor_copy(PT[0][:, :, :].rearrange("p k n -> p (k n)"), bP[0][:, :]).then_inc(pte_v, 1)

            def keep_at(b, s, m):
                dve.wait_ge(at_hi, KD * b + m + 1)
                dve.tensor_tensor(ATL[s][:, m, :], bAV[:, 0:SL], ATH[s][:, m, :], ALU.subtract).then_inc(at_done, 1)

            def add_residual(b, s, t):
                dve.wait_ge(out_done, 2 * b + t + 1)
                if t == 0:
                    dve.wait_ge(xb_done, 2 * b + 2)
                    if not isinstance(b, int) or b >= 2:
                        dve.wait_ge(x1_out[s], 16 * (b - s))
                dve.tensor_tensor(X1[s][:, t, :], (bA if t == 0 else bB)[:, :], XB[s][:, t, :], ALU.add).then_inc(x1_done, 1)

            for t in range(NT):
                statistics(0, 0, t)
                normalise(0, 0, t)
            for k in range(8):
                piece(0, 0, k)
            for t in range(NT):
                statistics(1, 1, t)
                normalise(1, 1, t)
            for k in range(2):
                piece(1, 1, k)

            def body(b, s, first, last):
                for u in range(UNITS):
                    if u % 2:
                        if u >= 3:
                            keep_pt(b, u - 3)
                        elif not first:
                            keep_pt(b - 1, UNITS - 2)
                    if u >= 1:
                        recip(b, u - 1)
                    elif not first:
                        recip(b - 1, UNITS - 1)
                    maxima(b, u)
                    if u % 4 == 3:
                        if u >= 4:
                            keep_at(b, s, u // 4 - 1)
                        elif not first:
                            keep_at(b - 1, 1 - s, KD - 1)
                    if u in (13, 15) and not first:
                        add_residual(b - 1, 1 - s, (u - 13) // 2)
                    if not before_last(b):
                        if u in (4, 12):
                            statistics(b + 2, s, u // 8)
                        if u in (6, 14):
                            normalise(b + 2, s, u // 8)
                    if u in DVE_STEP and not last:
                        piece(b + 1, 1 - s, DVE_STEP[u])
                    if u == UNITS - 1 and not before_last(b):
                        piece(b + 2, s, 0)
                        piece(b + 2, s, 1)

            over_sequences(dve, body)
            recip(NB - 1, UNITS - 1)
            keep_pt(NB - 1, UNITS - 2)
            keep_at(NB - 1, 1, KD - 1)
            for t in range(NT):
                add_residual(NB - 1, 1, t)

        @block.tensor
        def _(pe):
            def piece(b, s, k, part=None):
                bank = BANK[k]
                if k < 2:
                    pe.wait_ge(xn_done, 2 * b + k + 1)
                    if k == 1 and (not isinstance(b, int) or b >= 3):
                        pe.wait_ge(x1_done, 2 * b - 5)
                    elif not isinstance(b, int) or b >= 1:
                        pe.wait_ge(v_done, 2 * b - k)
                    for j in range(KD):
                        mm = pe.transpose(bank[:, j * P:(j + 1) * P], XN[:, k, j * P:(j + 1) * P], ident[:])
                    mm.then_inc(turned, 1)
                    return

                def product(dst, name, lo, hi, rot=None):
                    for j in range(KD):
                        for i, (wp, xp) in enumerate(PASSES):
                            mm = pe.matmul(dst, parts[name][wp][:, j, lo:hi], XT[xp][:, j, :], start=(j == 0 and i == 0),
                                           stop=(j == KD - 1 and i == 2 and rot is None))
                    if rot is not None:
                        mm = pe.matmul(dst, sel[:], rot[:], start=False, stop=True)
                    return mm

                def latent(dst, name, lo, hi, rot=None):
                    for i, (wp, xp) in enumerate(PASSES):
                        mm = pe.matmul(dst, parts[name][wp][:, lo:hi], CK[xp][:], start=(i == 0), stop=(i == 2 and rot is None))
                    if rot is not None:
                        mm = pe.matmul(dst, sel[:], rot[:], start=False, stop=True)
                    return mm

                if k == 2:
                    if part != 1:
                        pe.wait_ge(xt_done, 2 * b + 2)
                        mm = product(bank[:, 0:SL], "dkvT", 0, P)
                    if part != 0:
                        mm = product(bank[:, SL:2 * SL], "xqT_f", 0, P)
                elif k in (3, 4):
                    if part != 1:
                        if k == 4:
                            pe.wait_ge(ctr_done, b + 1)
                        elif not isinstance(b, int) or b >= 3:
                            pe.wait_ge(x1_done, 2 * b - 4)
                        elif b >= 1:
                            pe.wait_ge(k_lo, 2 * b)
                    m0 = 2 if k == 3 else 0
                    for m in range(m0, m0 + 2):
                        if part is None or part == m - m0:
                            mm = product(bank[:, (m - m0) * SL:(m - m0 + 1) * SL], "qT_w", m * P, (m + 1) * P,
                                         RQ if m == 0 else None)
                elif k == 5:
                    pe.wait_ge(q_lo, 2 * b + 1)
                    mm = latent(bank[:, 0:SL], "xkT", 0, P)
                elif k == 6:
                    for m in (2, 3):
                        mm = latent(bank[:, (m - 2) * SL:(m - 1) * SL], "kT_w", m * P, (m + 1) * P)
                elif k == 7:
                    pe.wait_ge(rk_done, b + 1)
                    for m in (0, 1):
                        mm = latent(bank[:, m * SL:(m + 1) * SL], "kT_w", m * P, (m + 1) * P, RK if m == 0 else None)
                else:
                    if k == 8:
                        pe.wait_ge(q_lo, 2 * b + 2)
                    else:
                        pe.wait_ge(k_lo, 2 * b + 1)
                    for i, (cp, wp) in enumerate(PASSES):
                        mm = pe.matmul(bank[:, :], CK[cp][:, (k - 8) * P:(k - 7) * P], parts["vT_w"][wp][:], start=(i == 0), stop=(i == 2))
                if part != 0:
                    mm.then_inc(front, 1)

            def scores(b, s, u):
                if u == 0:
                    for sems in (qs_in, ks_in):
                        pe.wait_ge(sems[s], 96 * (b + 2 - s))
                if not isinstance(b, int) or UNITS * b + u >= 2:
                    pe.wait_ge(exp_done, UNITS * b + u - 1)
                t, h, m = unit(u)
                for j in range(2):
                    hq = (h + j) % 4
                    mm = pe.matmul(bS[u % 2][:, j * SL:(j + 1) * SL], QS[s][0:3 * QUAD, hq, m, t * P:(t + 1) * P],
                                   KS[s][0:3 * QUAD, hq, m, :], start=True, stop=True)
                mm.then_inc(s_done, 1)

            def turn(b, u):
                pe.wait_ge(pn_done, UNITS * b + u + 1)
                if not isinstance(b, int) or UNITS * b + u >= 2:
                    pe.wait_ge(pte_a if u % 2 else pte_v, (UNITS // 2) * b + u // 2)
                for j in range(2):
                    for kb in range(NT):
                        mm = pe.transpose(bP[u % 2][:, (2 * j + kb) * P:(2 * j + kb + 1) * P],
                                          PR[u % 4][:, j, kb * P:(kb + 1) * P], ident[:])
                mm.then_inc(t_done, 1)

            def values(b, s, u):
                pe.wait_ge(pte_a if u % 2 else pte_v, (UNITS // 2) * b + u // 2 + 1)
                t, h, m = unit(u)
                if u == 0:
                    pe.wait_ge(v_done, 2 * b + 2)
                if u % 4 == 0 and (not isinstance(b, int) or b >= 1 or m >= 1):
                    pe.wait_ge(at_done, KD * b + m)
                for j in range(2):
                    hq = (h + j) % 4
                    for kb in range(NT):
                        mm = pe.matmul(bAV[QUAD * hq:QUAD * (hq + 1), t * P:(t + 1) * P],
                                       V[s][:, kb, (h + j) * HD:(h + j + 1) * HD], PT[u % 2][:, 2 * j + kb, :],
                                       start=(kb == 0), stop=(kb == NT - 1), tile_position=(0, QUAD * hq))
                mm.then_inc(pv_done, 1)

            def output(b, s, t, part=None):
                if part != 1:
                    pe.wait_ge(at_done, KD * b + KD)
                    if before_last(b):
                        pe.wait_ge(x1_done, 2 * b - 1 + t)
                    elif t == 0:
                        pe.wait_ge(v_done, 2 * b + 5)
                    else:
                        pe.wait_ge(k_lo, 2 * b + 6)
                for j in range(KD):
                    if part is None or part == j // 2:
                        for i, (ap, wp) in enumerate(PASSES):
                            mm = pe.matmul((bA if t == 0 else bB)[:, :], (ATH, ATL)[ap][s][:, j, t * P:(t + 1) * P],
                                           parts["woT"][wp][:, j, :], start=(j == 0 and i == 0), stop=(j == KD - 1 and i == 2))
                if part != 0:
                    mm.then_inc(out_done, 1)

            for k in range(10):
                piece(0, 0, k)
            for k in range(2):
                piece(1, 1, k)

            def body(b, s, first, last):
                for u in range(UNITS):
                    scores(b, s, u)
                    for k, part in PE_STEP.get(u, ()):
                        if not last:
                            piece(b + 1, 1 - s, k, part)
                    if u in (11, 12, 13, 14) and not first:
                        output(b - 1, 1 - s, (u - 11) // 2, (u - 11) % 2)
                    if u >= UNITS - 2 and not before_last(b):
                        piece(b + 2, s, u - UNITS + 2)
                    if u >= 2:
                        turn(b, u - 2)
                    elif not first:
                        turn(b - 1, UNITS + u - 2)
                    if u >= 3:
                        values(b, s, u - 3)
                    elif not first:
                        values(b - 1, 1 - s, UNITS + u - 3)

            over_sequences(pe, body)
            b = NB - 1
            turn(b, UNITS - 2)
            values(b, 1, UNITS - 3)
            turn(b, UNITS - 1)
            values(b, 1, UNITS - 2)
            values(b, 1, UNITS - 1)
            for t in range(NT):
                output(b, 1, t)


XH_SLOTS = 4
CD = SL // CH
LB = D // P
NP = CD // 2
BJ = NB * CD
HJ = BJ // 2
PW = NP * BJ + HJ
WRAP = (NP - 1) * NB
ZS = 4
NE, TOP = 16, 2


def part_ap(full, offset, dims):
    return bass.AP(full.tensor, full.offset + offset, [list(full.ap[0])] + dims)


def tile_ap(t, offset, dims):
    return part_ap(t[:], offset, dims)


def convolution_program(nc, x1, ctx_in, router_w, x2, xn3, kpad, keep, psum, ident, m_half,
                        gate_w, up_w, WGU):
    ctx = ExitStack()
    with ctx:
        def sb(name, shape, dt=F32):
            return ctx.enter_context(nc.sbuf_tensor(name, shape, dt))

        def sem(name):
            return ctx.enter_context(nc.semaphore(name))

        scores, top8, idx8 = keep
        RW = sb("RW", [P, KD, NE])
        WS = [sb(f"WS{s}", [P, 2, 2 * F]) for s in range(2)]
        XH = [sb(f"XH{i}", [P, D]) for i in range(XH_SLOTS)]
        CX = [sb(f"CX{s}", [P, D]) for s in range(2)]
        TH, TL = ([sb(f"T{n}{s}", [P, D], F16) for s in range(2)] for n in "HL")
        XN2 = sb("XN2", [P, D])
        Q2 = [sb(f"Q2_{s}", [P, LB, 2 * BJ]) for s in range(2)]
        CR = sb("CR", [P, D])
        C2 = sb("C2", [P, LB, 2 * BJ])
        KV = sb("KV", [P, LB, PW])
        VH, VL = ([sb(f"V{n}{s}", [P, LB, PW], F16) for s in range(2)] for n in "HL")
        Z1 = [sb(f"Z1_{i}", [P, NP + 1, BJ]) for i in range(ZS)]
        Z2 = [sb(f"Z2_{i}", [P, NP - 1, BJ + WRAP]) for i in range(2)]
        X2 = [sb(f"X2_{s}", [P, D]) for s in range(2)]
        XN3 = [sb(f"XN3_{s}", [P, D]) for s in range(2)]
        X3T = sb("X3T", [P, KD, P])
        st, mv = sb("st2", [P, 2, 6]), sb("mv2", [P, 2, 2])
        vare, rstd = sb("vare2", [P, 2]), sb("rstd2", [P, 2])
        nmean, shift = sb("nmean2", [P, 2]), sb("shift2", [P, 2])

        Y = [psum[:, 2 * i:2 * i + 2, :].rearrange("p k n -> p (k n)") for i in range(2)]
        OT = [psum[:, 4 + s, :] for s in range(2)]
        bQ, bC = psum[:, 6, :], psum[:, 7, :]

        z_set, rw_in, held = sem("z_set"), sem("rw_in"), sem("held")
        w_in, w_hi, w_lo = [sem(f"w_in{s}") for s in range(2)], sem("w_hi"), sem("w_lo")
        xh_in = [sem(f"xh_in{i}") for i in range(XH_SLOTS)]
        cx_in = [sem(f"cx_in{s}") for s in range(2)]
        tt_in = [sem(f"tt_in{s}") for s in range(2)]
        chain, vare_done, rstd_done, may_aggr = sem("chain2"), sem("vare_done"), sem("rstd_done2"), sem("may_aggr2")
        xn2_done, xn3_done, x2_done = sem("xn2_done"), sem("xn3_done"), sem("x2_done")
        c_flipped, c_turned, c_done = sem("c_flipped"), sem("c_turned"), sem("c_done")
        prod_done, sq_done, kv_hi, kv_lo = sem("prod_done"), sem("sq_done"), sem("kv_hi"), sem("kv_lo")
        ps_done, kv_lo3, rooted, wrapped = sem("ps_done"), sem("kv_lo3"), sem("rooted2"), sem("wrapped")
        q_turned, q_done = sem("q_turned"), sem("q_done")
        y_done, z_done, zt_done = sem("y_done"), sem("z_done"), sem("zt_done")
        x3_turned, x3_done, sc_ready, sc_done = sem("x3_turned"), sem("x3_done"), sem("sc_ready"), sem("sc_done")
        x2_out = [sem(f"x2_out{s}") for s in range(2)]

        def rows(t, h):
            return t[:, bass.ds(h * CD, CD), :].rearrange("b j d -> j b d")

        def over_heads(eng, body, lo=4, hi=CH - 4):
            for h in range(lo):
                body(h, h)
            with eng.Fori(0, (hi - lo) // 4) as i:
                for k in range(lo, lo + 4):
                    body(4 * i + k, k)
            for h in range(hi, CH):
                body(h, h)

        def inner(h):
            return not isinstance(h, int)

        block = ctx.enter_context(nc.Block())

        @block.sync
        def _(sp):
            def hold():
                sp.sem_inc(held, 1)

            def load_rows(h, i):
                sp.dma_start(XH[i][:], rows(x1, h)).then_inc(xh_in[i], 16)

            def load_c(h, s):
                sp.dma_start(CX[s][:], rows(ctx_in, h)).then_inc(cx_in[s], 16)

            def load_taps(h, s):
                for part, tile in zip(kpad, (TH[s], TL[s])):
                    sp.dma_start(tile[:], bass.AP(part, h * TAPS + 1, [[1, P], [1, D]])).then_inc(tt_in[s], 16)

            def store_x2(h, s):
                sp.wait_ge(x2_done, h + 1)
                hold()
                sp.dma_start(rows(x2, h), X2[s][:]).then_inc(x2_out[s], 16)

            def store_xn3(h, s):
                sp.wait_ge(xn3_done, h + 1)
                hold()
                sp.dma_start(rows(xn3, h), XN3[s][:]).then_inc(x2_out[s], 16)

            for h in range(2):
                load_rows(h, h)
                load_c(h, h)
            for h in range(2):
                load_taps(h, h)
            load_rows(2, 2)
            sp.dma_start(RW[:], router_w.rearrange("(k p) e -> p k e", p=P)).then_inc(rw_in, 16)
            sp.wait_ge(c_flipped, 1)
            load_c(2, 0)

            def load_weights(h, s):
                if inner(h) or h >= 2:
                    sp.wait_ge(w_lo, h - 1)
                    hold()
                assert NE * KD == 2 * CH
                for w, lo in ((gate_w, 0), (up_w, F)):
                    src = w.rearrange("e (k p) f -> (e k) p f", p=P)[bass.ds(2 * h, 2), :, :].rearrange("n p f -> p n f")
                    sp.dma_start(WS[s][:, :, lo:lo + F], src).then_inc(w_in[s], 16)

            def body(h, k):
                if inner(h) or h + 3 < CH:
                    sp.wait_ge(c_flipped, h + 2)
                    hold()
                    load_c(h + 3, (k + 3) % 2)
                load_weights(h, k % 2)
                if inner(h) or h >= 1:
                    store_x2(h - 1, (k - 1) % 2)
                if inner(h) or h + 3 < CH:
                    if inner(h) or h >= 1:
                        sp.wait_ge(x2_done, h)
                        hold()
                    load_rows(h + 3, (k + 3) % 4)
                if inner(h) or h >= 1:
                    store_xn3(h - 1, (k - 1) % 2)
                if inner(h) or h + 2 < CH:
                    sp.wait_ge(y_done, LB * (h + 1))
                    hold()
                    load_taps(h + 2, k % 2)

            over_heads(sp, body)
            store_x2(CH - 1, (CH - 1) % 2)
            store_xn3(CH - 1, (CH - 1) % 2)
            for s in range(2):
                sp.wait_ge(x2_out[s], 16 * CH)

        @block.gpsimd
        def _(pool):
            def products(h, m):
                pool.wait_ge(c_done, h + 1)
                if m < 3 and (inner(h) or h >= 1):
                    pool.wait_ge(kv_lo, 3 * h - 2 + m)
                pool.tensor_tensor(KV[:, m, BJ:NP * BJ].rearrange("p (d n) -> p d n", d=NP - 1),
                                   tile_ap(C2, m * 2 * BJ, [[0, NP - 1], [1, BJ]]),
                                   tile_ap(C2, m * 2 * BJ + NB, [[NB, NP - 1], [1, BJ]]), ALU.mult)
                pool.tensor_tensor(KV[:, m, NP * BJ:PW], C2[:, m, 0:HJ], C2[:, m, HJ:BJ], ALU.mult).then_inc(prod_done, 1)

            def low(h, k):
                pool.wait_ge(kv_hi, LB * (h + 1))
                pool.tensor_tensor(VL[k % 2][:, 3, :], KV[:, 3, :], VH[k % 2][:, 3, :], ALU.subtract).then_inc(kv_lo3, 1)

            def presum(h, b):
                pool.wait_ge(z_done, LB * h + b + 1)
                z = Z1[b % ZS][:, 1:NP, :]
                pool.tensor_tensor(z, z, Z2[b % 2][:, :, 0:BJ], ALU.add).then_inc(ps_done, 1)

            def roots(h, n):
                pool.wait_ge(vare_done, n)
                if inner(h) or h >= 1:
                    pool.wait_ge(xn2_done, h + 1 if inner(h) else min(h + 1, CH))
                if inner(h) or h >= 2:
                    pool.wait_ge(xn3_done, h - 1)
                pool.tensor_tensor(rstd[:], vare[:], m_half[:].to_broadcast([P, 2]), ALU.pow).then_inc(rooted, 1)
                pool.wait_ge(rooted, n)
                pool.tensor_tensor(shift[:], nmean[:], rstd[:], ALU.mult).then_inc(rstd_done, 1)

            pool.wait_ge(z_set, 1)
            roots(0, 1)
            for m in range(3):
                products(0, m)

            def body(h, k):
                nxt = inner(h) or h + 1 < CH
                if inner(h) or h >= 1:
                    presum(h - 1, 3)
                products(h, 3)
                presum(h, 0)
                low(h, k)
                if nxt:
                    products(h + 1, 0)
                roots(h, h + 2)
                if nxt:
                    products(h + 1, 1)
                presum(h, 1)
                presum(h, 2)
                if nxt:
                    products(h + 1, 2)

            over_heads(pool, body)
            presum(CH - 1, 3)
            roots(CH, CH + 2)

        @block.scalar
        def _(act):
            def keep_c(h, k):
                act.wait_ge(c_turned, h + 1)
                if inner(h) or h >= 1:
                    act.wait_ge(prod_done, LB * h)
                src = bC.rearrange("p (m n) -> p m n", m=LB)
                act.copy(C2[:, :, 0:BJ], src)
                act.copy(C2[:, :, BJ:2 * BJ], src).then_inc(c_done, 1)

            def keep_q(h, k):
                act.wait_ge(q_turned, h + 1)
                if inner(h) or h >= 2:
                    act.wait_ge(z_done, LB * (h - 1))
                src = bQ.rearrange("p (m n) -> p m n", m=LB)
                act.copy(Q2[k % 2][:, :, 0:BJ], src)
                act.copy(Q2[k % 2][:, :, BJ:2 * BJ], src).then_inc(q_done, 1)

            def keep_x3(h, k):
                act.wait_ge(x3_turned, h + 1)
                if inner(h) or h >= 1:
                    act.wait_ge(sc_ready, h)
                act.copy(X3T[:].rearrange("p k n -> p (k n)"), bC).then_inc(x3_done, 1)

            def flip_c(h, k):
                act.wait_ge(cx_in[k % 2], 8 * (h - k % 2) + 16)
                if inner(h) or h >= 1:
                    act.wait_ge(c_turned, h)
                act.copy(CR[:], tile_ap(CX[k % 2], D - 1, [[-1, D]])).then_inc(c_flipped, 1)

            def squares(h):
                act.wait_ge(c_done, h + 1)
                if inner(h) or h >= 1:
                    act.wait_ge(kv_lo, 3 * h)
                    act.wait_ge(kv_lo3, h)
                act.activation(KV[:, :, 0:BJ], C2[:, :, 0:BJ], ACT.Square).then_inc(sq_done, 1)

            def high(h, k, m):
                act.wait_ge(prod_done, LB * h + m + 1)
                if m == 0:
                    act.wait_ge(sq_done, h + 1)
                    if inner(h) or h >= 2:
                        act.wait_ge(y_done, LB * (h - 1))
                act.copy(VH[k % 2][:, m, :], KV[:, m, :]).then_inc(kv_hi, 1)

            def normalise(h, k, n):
                act.wait_ge(rstd_done, n)
                if inner(h) or h + 1 < CH:
                    if inner(h) or h >= 0:
                        act.wait_ge(q_turned, h + 1)
                    act.activation(XN2[:], XH[(k + 1) % XH_SLOTS][:], ACT.Identity, bias=shift[:, 0:1],
                                   scale=rstd[:, 0:1]).then_inc(xn2_done, 1)
                if inner(h) or h >= 1:
                    if inner(h) or h >= 3:
                        act.wait_ge(x2_out[(k - 1) % 2], 16 * (h - 1 - (k - 1) % 2))
                        act.wait_ge(x3_turned, h - 2)
                    act.activation(XN3[(k - 1) % 2][:], X2[(k - 1) % 2][:], ACT.Identity, bias=shift[:, 1:2],
                                   scale=rstd[:, 1:2]).then_inc(xn3_done, 1)

            def split_w(h, k):
                act.wait_ge(w_in[k % 2], 16 * (h - k % 2) + 32)
                act.copy(WGU[0][:, bass.ds(2 * h, 2), :], WS[k % 2][:]).then_inc(w_hi, 1)

            normalise(-1, -1, 1)
            flip_c(0, 0)
            keep_c(0, 0)
            flip_c(1, 1)
            squares(0)
            high(0, 0, 0)
            high(0, 0, 1)
            keep_q(0, 0)

            def body(h, k):
                nxt = inner(h) or h + 1 < CH
                high(h, k, 2)
                high(h, k, 3)
                if nxt:
                    keep_c(h + 1, k + 1)
                if inner(h) or h + 2 < CH:
                    flip_c(h + 2, k + 2)
                if nxt:
                    squares(h + 1)
                    high(h + 1, k + 1, 0)
                normalise(h, k, h + 2)
                if nxt:
                    high(h + 1, k + 1, 1)
                    keep_q(h + 1, k + 1)
                if inner(h) or h >= 1:
                    keep_x3(h - 1, k - 1)
                    split_w(h - 1, k - 1)

            over_heads(act, body)
            split_w(CH - 1, CH - 1)
            normalise(CH, CH, CH + 2)
            keep_x3(CH - 1, CH - 1)

        @block.vector
        def _(dve):
            dve.memset(mv[:], 0.0).then_inc(z_set, 1)
            dve.wait_ge(z_set, 1)

            def statistics(h, k, n):
                base = 2 * n - 2
                nxt = inner(h) or h + 1 < CH
                prev = inner(h) or h >= 1
                if nxt:
                    i = (k + 1) % XH_SLOTS
                    dve.wait_ge(xh_in[i], 4 * (h + 1 - i) + 16)
                    ins = dve.bn_stats(st[:, 0, :], XH[i][:])
                if prev:
                    dve.wait_ge(x2_done, h)
                    ins = dve.bn_stats(st[:, 1, :], X2[(k - 1) % 2][:])
                ins.then_inc(chain, 1)
                dve.wait_ge(chain, base + 1)
                dve.sem_inc(may_aggr, 1)
                if nxt:
                    ins = dve.bn_aggr(mv[:, 0, :], st[:, 0, :])
                if prev:
                    ins = dve.bn_aggr(mv[:, 1, :], st[:, 1, :])
                ins.then_inc(chain, 1)
                dve.wait_ge(chain, base + 2)
                if not isinstance(n, int) or n >= 2:
                    dve.wait_ge(rstd_done, n - 1)
                dve.tensor_scalar(nmean[:], mv[:, :, 0], -1.0, None, ALU.mult)
                dve.tensor_scalar(vare[:], mv[:, :, 1], EPS, None, ALU.add).then_inc(vare_done, 1)

            def low(h, k, m):
                dve.wait_ge(kv_hi, LB * h + m + 1)
                dve.tensor_tensor(VL[k % 2][:, m, :], KV[:, m, :], VH[k % 2][:, m, :], ALU.subtract).then_inc(kv_lo, 1)

            def read_out(h, k, b):
                dve.wait_ge(y_done, LB * h + b + 1)
                if b == 0:
                    dve.wait_ge(q_done, h + 1)
                if inner(h) or LB * h + b >= ZS:
                    dve.wait_ge(zt_done, LB * h + b + 1 - ZS)
                if inner(h) or LB * h + b >= 2:
                    dve.wait_ge(ps_done, LB * h + b - 1)
                y, q, base = Y[b % 2], Q2[k % 2], b * 2 * BJ
                z = Z2[b % 2]
                dve.tensor_tensor(z[:, :, 0:WRAP], part_ap(y, 2 * BJ - NB, [[BJ - NB, NP - 1], [1, WRAP]]),
                                  tile_ap(q, base + BJ - NB, [[-NB, NP - 1], [1, WRAP]]), ALU.mult).then_inc(wrapped, 1)
                dve.tensor_tensor(Z1[b % ZS][:, 0:NP, :], y[:, 0:NP * BJ].rearrange("p (d n) -> p d n", d=NP),
                                  tile_ap(q, base, [[NB, NP], [1, BJ]]), ALU.mult)
                dve.tensor_tensor(Z1[b % ZS][:, NP, :].rearrange("p (r n) -> p r n", r=2),
                                  part_ap(y, NP * BJ, [[0, 2], [1, HJ]]),
                                  tile_ap(q, base + HJ, [[HJ, 2], [1, HJ]]), ALU.mult)
                dve.wait_ge(wrapped, LB * h + b + 1)
                ins = dve.tensor_tensor(tile_ap(z, NB, [[BJ + WRAP + NB, NP - 1], [1, BJ]]),
                                        y[:, BJ:NP * BJ].rearrange("p (d n) -> p d n", d=NP - 1),
                                        tile_ap(q, base, [[0, NP - 1], [1, BJ]]), ALU.mult)
                ins.then_inc(z_done, 1)

            def residual(h, k):
                dve.wait_ge(zt_done, LB * (h + 1))
                if inner(h) or h >= 2:
                    dve.wait_ge(x2_out[k % 2], 16 * (h - k % 2))
                dve.tensor_tensor(X2[k % 2][:], OT[k % 2], XH[k % 4][:], ALU.add).then_inc(x2_done, 1)

            def route(h, k):
                dve.wait_ge(sc_ready, h + 1)
                dve.tensor_copy(scores[:, bass.ds(h, 1), :].rearrange("p o e -> p (o e)"), OT[k % 2][:, 0:NE]).then_inc(sc_done, 1)

            def split_w(h, k):
                dve.wait_ge(w_hi, h + 1)
                dve.tensor_tensor(WGU[1][:, bass.ds(2 * h, 2), :], WS[k % 2][:], WGU[0][:, bass.ds(2 * h, 2), :],
                                  ALU.subtract).then_inc(w_lo, 1)

            statistics(-1, -1, 1)
            low(0, 0, 0)
            low(0, 0, 1)

            def body(h, k):
                nxt = inner(h) or h + 1 < CH
                read_out(h, k, 0)
                if inner(h) or h >= 2:
                    split_w(h - 2, k)
                low(h, k, 2)
                read_out(h, k, 1)
                if inner(h) or h >= 2:
                    route(h - 2, k)
                if inner(h) or h >= 1:
                    residual(h - 1, k - 1)
                statistics(h, k, h + 2)
                read_out(h, k, 2)
                if nxt:
                    low(h + 1, k + 1, 0)
                    low(h + 1, k + 1, 1)
                read_out(h, k, 3)

            over_heads(dve, body)
            residual(CH - 1, CH - 1)
            statistics(CH, CH, CH + 2)
            split_w(CH - 2, CH - 2)
            split_w(CH - 1, CH - 1)
            route(CH - 2, CH - 2)
            route(CH - 1, CH - 1)

        @block.tensor
        def _(pe):
            def turn_c(h, k):
                pe.wait_ge(c_flipped, h + 1)
                if inner(h) or h >= 1:
                    pe.wait_ge(c_done, h)
                if inner(h) or h >= 3:
                    pe.wait_ge(x3_done, h - 2)
                for m in range(LB):
                    mm = pe.transpose(bC[:, m * P:(m + 1) * P], CR[:, (LB - 1 - m) * P:(LB - m) * P], ident[:])
                mm.then_inc(c_turned, 1)

            def turn_q(h, k):
                pe.wait_ge(xn2_done, h + 1)
                if inner(h) or h >= 1:
                    pe.wait_ge(q_done, h)
                for m in range(LB):
                    mm = pe.transpose(bQ[:, m * P:(m + 1) * P], XN2[:, m * P:(m + 1) * P], ident[:])
                mm.then_inc(q_turned, 1)

            def turn_x3(h, k):
                pe.wait_ge(xn3_done, h + 1)
                if inner(h) or h + 2 < CH:
                    pe.wait_ge(c_done, h + 3)
                for m in range(KD):
                    mm = pe.transpose(bC[:, m * P:(m + 1) * P], XN3[k % 2][:, m * P:(m + 1) * P], ident[:])
                mm.then_inc(x3_turned, 1)

            def router(h, k):
                pe.wait_ge(x3_done, h + 1)
                pe.wait_ge(x2_done, h + 1)
                if not inner(h) and h == 0:
                    pe.wait_ge(rw_in, 16)
                for m in range(KD):
                    mm = pe.matmul(OT[k % 2][:, 0:NE], X3T[:, m, :], RW[:, m, :], start=(m == 0), stop=(m == KD - 1))
                mm.then_inc(sc_ready, 1)

            def convolve(h, k, b):
                if b < 3:
                    pe.wait_ge(kv_lo, 3 * h + b + 1)
                else:
                    pe.wait_ge(kv_lo3, h + 1)
                if b == 0:
                    pe.wait_ge(tt_in[k % 2], 16 * (h - k % 2) + 32)
                if inner(h) or LB * h + b >= 2:
                    pe.wait_ge(z_done, LB * h + b - 1)
                for m in range(b + 1):
                    for i, (taps_part, kv_part) in enumerate(((TH, VH), (TH, VL), (TL, VH))):
                        w = taps_part[k % 2][:, (b - m) * P:(b - m + 1) * P]
                        for lo, hi in ((0, NP * BJ), (NP * BJ, PW)):
                            mm = pe.matmul(Y[b % 2][:, lo:hi], w, kv_part[k % 2][:, m, lo:hi],
                                           start=(m == 0 and i == 0), stop=(m == b and i == 2))
                mm.then_inc(y_done, 1)

            def gather(h, k, b):
                pe.wait_ge(ps_done, LB * h + b + 1)
                if b == 0 and (inner(h) or h >= 2):
                    pe.wait_ge(sc_done, h - 1)
                for d in range(NP + 1):
                    mm = pe.matmul(OT[k % 2][:, b * P:(b + 1) * P], Z1[b % ZS][:, d, :], ident[:], start=(d == 0),
                                   stop=(d == NP), is_transpose=True)
                mm.then_inc(zt_done, 1)

            turn_c(0, 0)
            turn_q(0, 0)

            def body(h, k):
                nxt, prev = inner(h) or h + 1 < CH, inner(h) or h >= 1
                convolve(h, k, 0)
                if prev:
                    gather(h - 1, k - 1, 2)
                if nxt:
                    turn_c(h + 1, k + 1)
                convolve(h, k, 1)
                if inner(h) or h >= 2:
                    router(h - 2, k)
                if prev:
                    gather(h - 1, k - 1, 3)
                convolve(h, k, 2)
                gather(h, k, 0)
                convolve(h, k, 3)
                if nxt:
                    turn_q(h + 1, k + 1)
                if prev:
                    turn_x3(h - 1, k - 1)
                gather(h, k, 1)

            over_heads(pe, body)
            router(CH - 2, CH - 2)
            gather(CH - 1, CH - 1, 2)
            gather(CH - 1, CH - 1, 3)
            turn_x3(CH - 1, CH - 1)
            router(CH - 1, CH - 1)


F = 192
FB = 96
FK = F // FB
TOKENS = NB * SL
PAIRS = TOKENS * TOP
TILES = PAIRS // P + NE - 1
HT = CH


PG = 4
WDS = 2


def routing_tables():
    t = {}
    t["count_e"] = np.tile(np.arange(NE, dtype=np.float32), (P, 1))
    t["count_p"] = np.tile(np.arange(P, dtype=np.float32), (P, 1))
    t["count_128"] = np.tile(np.arange(HT, dtype=np.float32) * P, (P, 1))
    p, h = np.arange(P)[:, None], np.arange(HT)[None, :]
    t["row"] = ((p % NB) * SL + h * CD + p // NB + 1).astype(np.float32)
    t["spare"] = (TOKENS + 1 + p).astype(np.float32)
    t["before"] = (np.arange(P)[:, None] < np.arange(P)[None, :]).astype(np.float32)
    t["carry"] = np.tile((np.arange(NE * HT) % HT != 0).astype(np.float32), (P, 1))
    names = list(t)
    at = dict(zip(names, np.cumsum([0] + [t[n].shape[1] for n in names])))
    return np.ascontiguousarray(np.concatenate([t[n] for n in names], 1)), {n: (int(at[n]), int(at[n] + t[n].shape[1])) for n in names}


def routing_program(nc, consts, spans, down_w, keep, WD, route, out, psum):
    ctx = ExitStack()
    with ctx:
        def sb(name, shape, dt=F32):
            return ctx.enter_context(nc.sbuf_tensor(name, shape, dt))

        def sem(name):
            return ctx.enter_context(nc.semaphore(name))

        scores, top8, idx8 = keep
        source, target, share, expert = route
        slots, weight = sb("slots", [P, TOP, HT], I32), sb("weight", [P, TOP, HT])
        none, index_f = sb("none", [P, TILES]), sb("index_f", [P, 2, TILES])
        zeros = sb("zeros", [P, D])
        E = [sb(f"E{i}", [P, PG, TILES]) for i in range(2)]
        K = sb("consts", [P, consts.shape[1]])
        c = {n: K[:, lo:hi] for n, (lo, hi) in spans.items()}
        gap, ex, den = sb("gap", [P, HT]), sb("ex", [P, HT]), sb("den3", [P, HT])
        pick = sb("pick", [P, TOP, HT])
        hot = sb("hot", [P, TOP, NE, HT])
        mask, work = sb("mask", [P, NE, HT]), sb("work", [P, NE, HT])
        incl, ones = sb("incl", [P, NE, HT]), sb("ones", [P, P])
        tiles, end, start = sb("tiles", [P, NE]), sb("end", [P, NE]), sb("start", [P, NE])
        slot_f = sb("slot_f", [P, TOP, HT])
        part_i, part_f = sb("part_i", [P, 2, TOP * HT], I32), sb("part_f", [P, 2, TOP * HT])
        T = [sb(f"T{i}", [P, 2, PG, TILES]) for i in range(2)]
        WS = [sb(f"WDS{i}", [FB, FK, D]) for i in range(WDS)]
        cmp, exp_f = sb("cmp", [P, TILES, NE]), sb("exp_f", [P, TILES])
        R = [cmp[:].rearrange("p t e -> p (t e)")[:, i * PG * P:(i + 1) * PG * P].rearrange("p (g n) -> p g n", g=PG) for i in range(2)]

        wd_in, wd_hi, wd_lo = [sem(f"wd_in{i}") for i in range(WDS)], sem("wd_hi"), [sem(f"wd_lo{i}") for i in range(WDS)]
        consts_in, gap_done, ex_done, step = sem("consts_in"), sem("gap_done"), sem("ex_done"), sem("step")
        cleared, spare_out = sem("cleared"), sem("spare_out")
        rowed, weighed = sem("rowed"), sem("weighed")
        masked, counted, spread, added = sem("masked"), sem("counted"), sem("spread"), sem("added")
        bank_before, bank_all, bank_list = psum[:, 0, :], psum[:, 1, :], psum[:, 2, :]

        def over(ap_tile, dims, off=0):
            return tile_ap(ap_tile, off, dims)

        block = ctx.enter_context(nc.Block())

        @block.sync
        def _(sp):
            sp.dma_start(K[:], consts.ap()).then_inc(consts_in, 16)
            sp.wait_ge(cleared, 1)
            sp.dma_start(out[TOKENS:TOKENS + P, :], zeros[:]).then_inc(spare_out, 16)
            for e in range(NE):
                if e >= WDS:
                    sp.wait_ge(wd_lo[e % WDS], e // WDS)
                sp.dma_start(WS[e % WDS][:], down_w[e].rearrange("(c p) n -> p c n", p=FB)).then_inc(wd_in[e % WDS], 16)
            sp.wait_ge(spare_out, 16)

        @block.scalar
        def _(act):
            def split(e):
                act.wait_ge(wd_in[e % WDS], 16 * (e // WDS + 1))
                act.copy(WD[0][:, e, :, :], WS[e % WDS][:]).then_inc(wd_hi, 1)

            for e in range(2):
                split(e)
            act.wait_ge(gap_done, 1)
            act.activation(ex[:], gap[:], ACT.Exp).then_inc(ex_done, 1)
            for e in range(2, NE // 2):
                split(e)
            for g in range(TOP * HT // PG):
                if g < NE - NE // 2:
                    split(NE // 2 + g)
                act.wait_ge(spread, g + 1)
                if g >= 2:
                    act.wait_ge(added, g - 1)
                for j in range(PG):
                    i = g * PG + j
                    ins = act.activation(T[g % 2][:, 1, j, :], E[g % 2][:, j, :], ACT.Identity,
                                         scale=weight[:, i // HT, i % HT:i % HT + 1])
                ins.then_inc(weighed, 1)

        @block.gpsimd
        def _(pool):
            for e in range(0, NE, WDS):
                pool.wait_ge(wd_hi, e + 1)
                pool.tensor_tensor(WD[1][:, e, :, :], WS[0][:], WD[0][:, e, :, :], ALU.subtract).then_inc(wd_lo[0], 1)

        @block.vector
        def _(dve):
            n = 0

            def then(ins):
                nonlocal n
                n += 1
                ins.then_inc(step, 1)
                dve.wait_ge(step, n)

            def low(e):
                dve.wait_ge(wd_hi, e + 1)
                dve.tensor_tensor(WD[1][:, e, :, :], WS[1][:], WD[0][:, e, :, :], ALU.subtract).then_inc(wd_lo[1], 1)

            dve.memset(zeros[:], 0.0).then_inc(cleared, 1)
            for h in range(HT):
                dve.max(top8[:, h, :], scores[:, h, :]).then_inc(step, 1)
            n = HT
            dve.wait_ge(step, n)
            for h in range(HT):
                ins = dve.max_index(idx8[:, h, :], top8[:, h, :], scores[:, h, :])
            then(ins)
            low(1)
            dve.tensor_tensor(gap[:], top8[:, :, 1], top8[:, :, 0], ALU.subtract).then_inc(gap_done, 1)
            then(dve.tensor_copy(pick[:].rearrange("p c h -> p h c"), idx8[:, :, 0:TOP]))
            then(dve.memset(ones[:], 1.0))
            dve.wait_ge(consts_in, 16)
            for j in range(TOP):
                ins = dve.tensor_tensor(hot[:, j, :, :], over(K, [[1, NE], [0, HT]], spans["count_e"][0]),
                                        over(pick, [[0, NE], [1, HT]], j * HT), ALU.is_equal)
            then(ins)
            then(dve.tensor_tensor(mask[:], hot[:, 0, :, :], hot[:, 1, :, :], ALU.add))
            dve.sem_inc(masked, 1)
            dve.wait_ge(ex_done, 1)
            then(dve.tensor_scalar(den[:], ex[:], 1.0, None, ALU.add))
            then(dve.reciprocal(weight[:, 0, :], den[:]))
            then(dve.tensor_tensor(weight[:, 1, :], ex[:], weight[:, 0, :], ALU.mult))
            low(3)
            dve.wait_ge(counted, 1)
            flat = "p e h -> p (e h)"
            then(dve.tensor_tensor_scan(incl[:].rearrange(flat), c["carry"], bank_all, 0.0, ALU.mult, ALU.add))
            then(dve.tensor_tensor(work[:].rearrange(flat), incl[:].rearrange(flat), bank_all, ALU.subtract))
            then(dve.tensor_tensor(work[:].rearrange(flat), bank_before, work[:].rearrange(flat), ALU.add))
            then(dve.tensor_tensor(mask[:], over(incl, [[HT, NE], [0, HT]], HT - 1),
                                   over(K, [[0, NE], [1, HT]], spans["count_128"][0]), ALU.is_gt))
            then(dve.tensor_reduce(tiles[:], mask[:], AX.X, ALU.add))
            then(dve.tensor_tensor_scan(end[:], ones[:, 0:NE], tiles[:], 0.0, ALU.mult, ALU.add))
            then(dve.tensor_tensor(start[:], end[:], tiles[:], ALU.subtract))
            low(5)
            then(dve.scalar_tensor_tensor(work[:], over(start, [[1, NE], [0, HT]]), float(P), work[:], ALU.mult, ALU.add))
            for j in range(TOP):
                then(dve.tensor_tensor(mask[:], hot[:, j, :, :], work[:], ALU.mult))
                then(dve.tensor_reduce(slot_f[:, j, :], mask[:].rearrange("p e h -> p h e"), AX.X, ALU.add))
            then(dve.tensor_copy(slots[:], slot_f[:]))
            low(7)
            all_slots = slots[:].rearrange("p c h -> p (c h)")
            then(dve.tensor_scalar(part_i[:, 0, :], all_slots, 7, None, ALU.arith_shift_right))
            then(dve.tensor_scalar(part_i[:, 1, :], all_slots, P - 1, None, ALU.bitwise_and))
            then(dve.tensor_copy(part_f[:], part_i[:]))
            then(dve.tensor_tensor(cmp[:], over(end, [[0, TILES], [1, NE]]),
                                   over(K, [[1, TILES], [0, NE]], spans["count_p"][0]), ALU.is_le))
            then(dve.tensor_reduce(exp_f[:], cmp[:], AX.X, ALU.add))
            then(dve.tensor_scalar(exp_f[:], exp_f[:], float(NE - 1), None, ALU.min))
            then(dve.tensor_copy(expert[:], exp_f[:]))
            groups = TOP * HT // PG
            for g in range(groups):
                if g >= 2:
                    dve.wait_ge(added, g - 1)
                i, h = g * PG, g * PG % HT
                dve.tensor_tensor(E[g % 2][:], over(K, [[0, PG], [1, TILES]], spans["count_p"][0]),
                                  over(part_f, [[1, PG], [0, TILES]], i), ALU.is_equal).then_inc(spread, 1)
                dve.tensor_tensor(R[g % 2], over(K, [[0, PG], [1, P]], spans["count_p"][0]),
                                  over(part_f, [[1, PG], [0, P]], TOP * HT + i), ALU.is_equal)
                dve.wait_ge(spread, g + 1)
                dve.tensor_tensor(T[g % 2][:, 0, :, :], E[g % 2][:], over(K, [[1, PG], [0, TILES]], spans["row"][0] + h),
                                  ALU.mult).then_inc(rowed, 1)
                if g % 2 and NE // 2 + g < NE:
                    low(NE // 2 + g)
            dve.wait_ge(added, groups)
            rows = bank_list[:, 0:TILES]
            then(dve.tensor_scalar(index_f[:, 0, :], rows, -1.0, 0.0, ALU.add, ALU.max))
            then(dve.tensor_scalar(none[:], rows, 0.0, None, ALU.is_equal))
            then(dve.scalar_tensor_tensor(index_f[:, 1, :], none[:], c["spare"], rows, ALU.mult, ALU.add))
            then(dve.tensor_scalar(index_f[:, 1, :], index_f[:, 1, :], -1.0, None, ALU.add))
            dve.tensor_copy(source[:], index_f[:, 0, :])
            dve.tensor_copy(target[:], index_f[:, 1, :])
            then(dve.tensor_copy(share[:], bank_list[:, TILES:2 * TILES]))

        @block.tensor
        def _(pe):
            pe.wait_ge(masked, 1)
            m = mask[:].rearrange("p e h -> p (e h)")
            pe.matmul(bank_before, c["before"], m, start=True, stop=True)
            pe.matmul(bank_all, ones[:], m, start=True, stop=True).then_inc(counted, 1)
            groups = TOP * HT // PG
            for g in range(groups):
                pe.wait_ge(rowed, g + 1)
                pe.wait_ge(weighed, g + 1)
                for j in range(PG):
                    mm = pe.matmul(bank_list[:, 0:2 * TILES], R[g % 2][:, j, :], T[g % 2][:, :, j, :],
                                   start=(g == 0 and j == 0), stop=(g == groups - 1 and j == PG - 1))
                mm.then_inc(added, 1)


def experts_program(nc, xn3, out, WGU, WD, route, psum, ident):
    ctx = ExitStack()
    with ctx:
        def sb(name, shape, dt=F32):
            return ctx.enter_context(nc.sbuf_tensor(name, shape, dt))

        def sem(name):
            return ctx.enter_context(nc.semaphore(name))

        source, target, share, expert = route
        col, tcol = ([sb(f"{n}{i}", [P, 1], I32) for i in range(4)] for n in ("col", "tcol"))
        scol = [sb(f"scol{i}", [P, 1]) for i in range(2)]
        G = [sb(f"G{i}", [P, D]) for i in range(4)]
        GH, GL = ([sb(f"G{n}{i}", [P, KD, P], F16) for i in range(2)] for n in "HL")
        SG, HM = [sb(f"SG{i}", [P, F]) for i in range(2)], [sb(f"HM{i}", [P, F]) for i in range(2)]
        HH, HL = ([sb(f"H{n}{i}", [FB, FK, P], F16) for i in range(2)] for n in "HL")
        YO = [sb(f"YO{i}", [P, D]) for i in range(4)]

        bG = [psum[:, i, :] for i in range(2)]
        bGU = [psum[:, 2 + i, :] for i in range(2)]
        bH = [psum[:, 4 + i, :] for i in range(2)]
        bY = [psum[:, 6 + i, :] for i in range(2)]

        col_done = sem("col_done")
        g_in = [sem(f"g_in{i}") for i in range(4)]
        g_turned, gt_done, gu_done, sg_done, hm_done = (sem(n) for n in ("g_turned", "gt_done", "gu_done", "sg_done", "hm_done"))
        g_hi, h_hi = sem("g_hi"), sem("h_hi")
        h_turned, ht_done, dn_done, yo_done, held = (sem(n) for n in ("h_turned", "ht_done", "dn_done", "yo_done", "held3"))
        y_out, tcol_done, scol_done = sem("y_out"), sem("tcol_done"), sem("scol_done")

        LO, HI = 4, TILES - 3
        assert (HI - LO) % 4 == 0

        def over_tiles(eng, body, lo=LO):
            for t in range(lo):
                body(t, t)
            with eng.Fori(0, (HI - lo) // 4) as i:
                for k in range(lo, lo + 4):
                    body(4 * i + k, k)
            for t in range(HI, TILES):
                body(t, t)

        def inner(t):
            return not isinstance(t, int)

        block = ctx.enter_context(nc.Block())

        @block.gpsimd
        def _(pool):
            def fetch(t, k):
                if inner(t) or t >= 4:
                    pool.wait_ge(g_turned, t - 3)
                    pool.sem_inc(held, 1)
                pool.tensor_copy(col[k % 4][:], source[:, bass.ds(t, 1)]).then_inc(col_done, 1)
                pool.wait_ge(col_done, t + 1)
                pool.sem_inc(held, 1)
                pool.indirect_dma_start(G[k % 4][:], None, xn3, bass.IndirectOffsetOnAxis(ap=col[k % 4][:, 0:1], axis=0)).then_inc(g_in[k % 4], 16)

            def add(t, k):
                pool.tensor_copy(tcol[k % 4][:], target[:, bass.ds(t, 1)]).then_inc(tcol_done, 1)
                pool.wait_ge(tcol_done, t + 1)
                pool.sem_inc(held, 1)
                if inner(t) or t >= 1:
                    pool.wait_ge(y_out, 16 * t)
                    pool.sem_inc(held, 1)
                pool.wait_ge(yo_done, t + 1)
                pool.sem_inc(held, 1)
                pool.indirect_dma_start(out, bass.IndirectOffsetOnAxis(ap=tcol[k % 4][:, 0:1], axis=0), YO[k % 4][:], None,
                                        compute_op=ALU.add).then_inc(y_out, 16)

            def body(t, k):
                fetch(t, k)
                if inner(t) or t >= 4:
                    add(t - 4, k - 4)

            over_tiles(pool, body, 2 * LO)
            for t in range(TILES - 4, TILES):
                add(t, t)
            pool.wait_ge(y_out, 16 * TILES)

        @block.scalar
        def _(act):
            def keep_g(t, k):
                act.wait_ge(g_turned, t + 1)
                if inner(t) or t >= 2:
                    act.wait_ge(gu_done, t - 1)
                act.copy(GH[k % 2][:].rearrange("p k n -> p (k n)"), bG[k % 2]).then_inc(g_hi, 1)

            def keep_h(t, k):
                act.wait_ge(h_turned, t + 1)
                if inner(t) or t >= 2:
                    act.wait_ge(dn_done, t - 1)
                act.copy(HH[k % 2][:].rearrange("p c n -> p (c n)"), bH[k % 2][0:FB, 0:FK * P]).then_inc(h_hi, 1)

            def silu(t, k):
                act.wait_ge(gu_done, t + 1)
                if inner(t) or t >= 2:
                    act.wait_ge(hm_done, t - 1)
                act.activation(SG[k % 2][:], bGU[k % 2][:, 0:F], ACT.Silu).then_inc(sg_done, 1)

            def keep_y(t, k):
                act.wait_ge(dn_done, t + 1)
                if inner(t) or t >= 4:
                    act.wait_ge(y_out, 16 * (t - 3))
                act.wait_ge(scol_done, t + 1)
                act.activation(YO[k % 4][:], bY[k % 2], ACT.Identity, scale=scol[k % 2][:, 0:1]).then_inc(yo_done, 1)

            def keep_share(t, k):
                if inner(t) or t >= 2:
                    act.wait_ge(yo_done, t - 1)
                act.copy(scol[k % 2][:], share[:, bass.ds(t, 1)]).then_inc(scol_done, 1)

            keep_g(0, 0)
            keep_g(1, 1)

            def body(t, k):
                silu(t, k)
                keep_share(t, k)
                if inner(t) or t + 2 < TILES:
                    keep_g(t + 2, k + 2)
                keep_h(t, k)
                if inner(t) or t >= 1:
                    keep_y(t - 1, k - 1)

            over_tiles(act, body, 2 * LO)
            keep_y(TILES - 1, TILES - 1)

        @block.vector
        def _(dve):
            def low_g(t, k):
                dve.wait_ge(g_hi, t + 1)
                dve.tensor_tensor(GL[k % 2][:].rearrange("p k n -> p (k n)"), bG[k % 2],
                                  GH[k % 2][:].rearrange("p k n -> p (k n)"), ALU.subtract).then_inc(gt_done, 1)

            def product(t, k):
                dve.wait_ge(sg_done, t + 1)
                if inner(t) or t >= 2:
                    dve.wait_ge(h_turned, t - 1)
                dve.tensor_tensor(HM[k % 2][:], bGU[k % 2][:, F:2 * F], SG[k % 2][:], ALU.mult).then_inc(hm_done, 1)

            def low_h(t, k):
                dve.wait_ge(h_hi, t + 1)
                dve.tensor_tensor(HL[k % 2][:].rearrange("p c n -> p (c n)"), bH[k % 2][0:FB, 0:FK * P],
                                  HH[k % 2][:].rearrange("p c n -> p (c n)"), ALU.subtract).then_inc(ht_done, 1)

            low_g(0, 0)
            low_g(1, 1)

            def body(t, k):
                product(t, k)
                if inner(t) or t + 2 < TILES:
                    low_g(t + 2, k + 2)
                low_h(t, k)

            over_tiles(dve, body)

        @block.tensor
        def _(pe):
            def turn_g(t, k):
                pe.wait_ge(g_in[k % 4], 4 * (t - k % 4) + 16)
                if inner(t) or t >= 2:
                    pe.wait_ge(gt_done, t - 1)
                for m in range(KD):
                    mm = pe.transpose(bG[k % 2][:, m * P:(m + 1) * P], G[k % 4][:, m * P:(m + 1) * P], ident[:])
                mm.then_inc(g_turned, 1)

            def expert_of(t):
                return pe.value_load(expert[0:1, bass.ds(t, 1)], min_val=0, max_val=NE - 1)

            def gate_up(t, k, e):
                pe.wait_ge(gt_done, t + 1)
                if inner(t) or t >= 2:
                    pe.wait_ge(hm_done, t - 1)
                for m in range(KD):
                    for i, (g, w) in enumerate(((GH, WGU[0]), (GH, WGU[1]), (GL, WGU[0]))):
                        mm = pe.matmul(bGU[k % 2][:, 0:2 * F], g[k % 2][:, m, :], w[:, bass.ds(e * KD + m, 1), :].rearrange("p o n -> p (o n)"),
                                       start=(m == 0 and i == 0), stop=(m == KD - 1 and i == 2))
                mm.then_inc(gu_done, 1)

            def turn_h(t, k):
                pe.wait_ge(hm_done, t + 1)
                if inner(t) or t >= 2:
                    pe.wait_ge(ht_done, t - 1)
                for m in range(FK):
                    mm = pe.transpose(bH[k % 2][0:FB, m * P:(m + 1) * P], HM[k % 2][:, m * FB:(m + 1) * FB], ident[:])
                mm.then_inc(h_turned, 1)

            def down(t, k, e):
                pe.wait_ge(ht_done, t + 1)
                if inner(t) or t >= 2:
                    pe.wait_ge(yo_done, t - 1)
                for m in range(FK):
                    for i, (h, w) in enumerate(((HH, WD[0]), (HH, WD[1]), (HL, WD[0]))):
                        mm = pe.matmul(bY[k % 2], h[k % 2][:, m, :], w[:, bass.ds(e, 1), m, :].rearrange("p o n -> p (o n)"),
                                       start=(m == 0 and i == 0), stop=(m == FK - 1 and i == 2))
                mm.then_inc(dn_done, 1)

            turn_g(0, 0)
            turn_g(1, 1)

            def bodies(first, k0, count):
                e, before = expert_of(first), None
                for j in range(count):
                    t, k = first + j, k0 + j
                    gate_up(t, k, e)
                    if j + 1 < count:
                        coming = expert_of(t + 1)
                    if inner(t) or t + 2 < TILES:
                        turn_g(t + 2, k + 2)
                    if inner(t) or t >= 1:
                        down(t - 1, k - 1, before if j else expert_of(t - 1))
                    turn_h(t, k)
                    before = e
                    if j + 1 < count:
                        e = coming
                return e

            bodies(0, 0, LO)
            assert (HI - LO) % 8 == 0
            with pe.Fori(0, (HI - LO) // 8) as i:
                bodies(8 * i + LO, LO, 8)
            last = bodies(HI, HI, TILES - HI)
            down(TILES - 1, TILES - 1, last)


def program(nc, a, out):
    with ExitStack() as ctx:
        def sb(name, shape, dt=F32):
            return ctx.enter_context(nc.sbuf_tensor(name, shape, dt))

        psum = ctx.enter_context(nc.psum_tensor("psum", [P, 8, 512], F32))
        banks = [psum[:, i, :] for i in range(8)]
        ident, tab, sel = sb("ident", [P, P]), sb("rot_tab", [P, SL]), sb("rot_sel", [P, P])
        m_half = sb("m_half", [P, 1])
        keep = (sb("scores", [P, CH, NE]), sb("top8", [P, CH, 8]), sb("idx8", [P, CH, 8], U32))
        x1 = nc.dram_tensor("x1", [NB, SL, D], F32).ap()
        x2 = out[0:TOKENS, :].rearrange("(b t) d -> b t d", b=NB)
        xn3 = nc.dram_tensor("xn3", [NB, SL, D], F32).ap()
        kpad = [nc.dram_tensor(f"kpad_{n}", [CH, TAPS], F16) for n in ("hi", "lo")]
        pick = np.zeros((P, P), np.float32)
        for r in range(ROT):
            pick[r, r] = pick[SWAP + r, r] = 1.0
        w = {n[8:]: v for n, v in a.items() if n.startswith("L0_attn_")}
        w["tab"] = nc.inline_tensor(rotary_table(), name="c_tab").ap()
        w["sel"] = nc.inline_tensor(pick, name="c_sel").ap()
        with ExitStack() as inner:
            def wsb(name, shape, dt=F32):
                return inner.enter_context(nc.sbuf_tensor(name, shape, dt))
            sbw = {"qT_w": wsb("qT_w", [P, KD, D]), "dkvT": wsb("dkvT", [P, KD, P]), "kT_w": wsb("kT_w", [P, D]),
                   "vT_w": wsb("vT_w", [P, D]), "woT": wsb("woT", [P, KD, D]), "xqT_f": wsb("xqT_f", [P, KD, P]),
                   "xkT": wsb("xkT", [P, P]), "b_q": wsb("b_q", [P, KD]), "b_k": wsb("b_k", [P, KD]),
                   "b_xq": wsb("b_xq", [P, 1]), "b_xk": wsb("b_xk", [P, 1]), "b_dkv": wsb("b_dkv", [P, 1]),
                   "b_o": wsb("b_o", [P, D]), "m_half": m_half}
            parts = {}
            for name in ("qT_w", "dkvT", "kT_w", "vT_w", "woT", "xqT_f", "xkT"):
                parts[name] = [wsb(f"{name}_{n}", list(sbw[name][:].shape), F16) for n in "HL"]
            setup_program(nc, w, a["L0_xattn_ssm_kernel"], a["L0_xattn_D"], kpad, sbw, parts, banks, tab, sel, ident)
            attention_program(nc, a["x"], x1, sbw, parts, banks, tab, sel, ident)
        WGU = [sb(f"WGU{n}", [P, NE * KD, 2 * F], F16) for n in "HL"]
        convolution_program(nc, x1, a["ctx_2048"], a["L0_ffn_router_w"],
                            x2, xn3, kpad, keep, psum, ident, m_half, a["L0_ffn_gate_w"], a["L0_ffn_up_w"], WGU)
        WD = [sb(f"WD{n}", [FB, NE, FK, D], F16) for n in "HL"]
        route = (sb("source", [P, TILES], I32), sb("target", [P, TILES], I32), sb("share", [P, TILES]), sb("expert", [P, TILES], I32))
        table, spans = routing_tables()
        routing_program(nc, nc.inline_tensor(table, name="c_route"), spans, a["L0_ffn_down_w"], keep, WD, route, out, psum)
        experts_program(nc, xn3.rearrange("b t d -> (b t) d"), out, WGU, WD, route, psum, ident)




_INS = ['x', 'ctx_2048', 'L0_attn_w_down_q', 'L0_attn_b_down_q', 'L0_attn_w_up_q', 'L0_attn_b_up_q', 'L0_attn_w_down_kv',
        'L0_attn_b_down_kv', 'L0_attn_w_up_k', 'L0_attn_b_up_k', 'L0_attn_w_up_v', 'L0_attn_b_up_v', 'L0_attn_wq_r',
        'L0_attn_bq_r', 'L0_attn_wk_r', 'L0_attn_bk_r', 'L0_attn_wo', 'L0_attn_bo', 'L0_xattn_ssm_kernel', 'L0_xattn_D',
        'L0_ffn_router_w', 'L0_ffn_gate_w', 'L0_ffn_up_w', 'L0_ffn_down_w']


def kernel(**inputs):
    import numpy as _np
    import concourse.bacc as _bacc
    from concourse import mybir as _mybir
    from concourse.bass_utils import run_bass_kernel_spmd as _run

    nc = _bacc.Bacc("TRN2", target_bir_lowering=False, num_devices=1)
    arrays, args = {}, {}
    for name in _INS:
        a = _np.ascontiguousarray(inputs[name])
        arrays[f"in_{name}_dram"] = a
        args[name] = nc.dram_tensor(f"in_{name}_dram", a.shape, _mybir.dt.from_np(a.dtype), kind="ExternalInput").ap()
    out = nc.dram_tensor("out_0_dram", (TOKENS + P, D), _mybir.dt.float32, kind="ExternalOutput").ap()
    program(nc, args, out)
    r = _run(nc, [arrays], core_ids=[0])
    return r.results[0]["out_0_dram"][:TOKENS].reshape(NB, SL, D)
```
